# Optimizing a Trainium2 kernel written in Bass

```python
import numpy as np
import jax
import jax.numpy as jnp

def _softmax(x, axis=-1):
    return jax.nn.softmax(x, axis=axis)

def _gelu(x):
    return jax.nn.gelu(x, approximate=True)

def _silu(x):
    return jax.nn.silu(x)

def _sigmoid(x):
    return jax.nn.sigmoid(x)

def _layernorm(x, axis=-1, eps=1e-05):
    m = jnp.mean(x, axis=axis, keepdims=True)
    v = jnp.var(x, axis=axis, keepdims=True)
    return (x - m) / jnp.sqrt(v + eps)

def _scatter_add(tgt, idx, src, axis=0):
    return tgt.at[idx].add(src)

def _segment_sum(src, seg, n):
    return jax.ops.segment_sum(src, seg, n)
kernel_name = 'mk_adaln_ffn_d2_seqx_r4_0bfec2'

def setup_inputs(seed: int=0):
    np.random.seed(seed)
    _w = jnp.asarray

    def _rec_inputs():
        import jax
        import jax.numpy as jnp
        _rk = jax.random.key(seed)
        x = -0.000125 + 0.9999 * jax.random.normal(jax.random.fold_in(_rk, 1), (64, 64, 1024), jnp.float32)
        _lenS = 64 - jax.random.randint(jax.random.fold_in(_rk, 7), (64,), 0, max(1, 64 // 4) + 1, jnp.int32)
        _lenS2 = 64 - jax.random.randint(jax.random.fold_in(_rk, 8), (64,), 0, max(1, 64 // 4) + 1, jnp.int32)
        cond_128 = 0.0061147 + 1.02565 * jax.random.normal(jax.random.fold_in(_rk, 11), (64, 128), jnp.float32)
        fside_S_0 = -0.022604 + 0.987366 * jax.random.normal(jax.random.fold_in(_rk, 12), (64,), jnp.float32)
        return (x, cond_128, fside_S_0)
    x, cond_128, fside_S_0 = _rec_inputs()

    def _L0_cond_setup():
        import jax, jax.numpy as jnp
        import numpy as np
        from jax import lax
        N, C_IN, L = (32, 64, 1024)
        C_OUT, K, GROUPS = (64, 9, 4)
        C_DIM, PAD, STRIDE = (128, 4, 1)
        key = jax.random.key(seed)
        k1, k2, k3, k4, k5 = jax.random.split(key, 5)
        x = jax.random.normal(k1, (N, C_IN, L), dtype=jnp.float32)
        c = jax.random.normal(k2, (N, C_DIM), dtype=jnp.float32)
        weight = jax.random.normal(k3, (C_OUT, C_IN // GROUPS, K), dtype=jnp.float32)
        c_weight = jax.random.normal(k4, (C_OUT, C_DIM), dtype=jnp.float32)
        bias = jax.random.normal(k5, (C_OUT,), dtype=jnp.float32)
        return {'x': x, 'c': c, 'weight': weight, 'c_weight': c_weight, 'bias': bias}
    _L0_cond_all = _L0_cond_setup()
    _L0_cond_in = {k: v for k, v in _L0_cond_all.items() if k in ('weight', 'c_weight')}
    del _L0_cond_all

    def _L0_ffn_setup():
        import jax, jax.numpy as jnp
        import numpy as np
        TOP_K = 2
        SCALING = 32.0 / 64.0
        key = jax.random.key(seed)
        ks = jax.random.split(key, 6)
        Bsz, S, Din, Dout, R, E = (4, 512, 1024, 1024, 64, 16)
        x = jax.random.normal(ks[0], (Bsz, S, Din), dtype=jnp.float32)
        base_w = jax.random.normal(ks[1], (Dout, Din), dtype=jnp.float32) * 0.02
        base_b = jax.random.normal(ks[2], (Dout,), dtype=jnp.float32) * 0.02
        A = jax.random.normal(ks[3], (R, Din), dtype=jnp.float32) * (1.0 / np.sqrt(Din))
        B = jax.random.normal(ks[4], (E, Dout, R), dtype=jnp.float32) * 0.02
        router_w = jax.random.normal(ks[5], (E, Din), dtype=jnp.float32) * 0.02
        return {'x': x, 'base_w': base_w, 'base_b': base_b, 'A': A, 'B': B, 'router_w': router_w}
    _L0_ffn_all = _L0_ffn_setup()
    _L0_ffn_in = {k: v for k, v in _L0_ffn_all.items() if k in ('base_w', 'base_b', 'A', 'B', 'router_w')}
    del _L0_ffn_all

    def _L1_cond_setup():
        import jax, jax.numpy as jnp
        import numpy as np
        K = 8
        T = 1.0
        D_EMBD = 128
        IN_C = 64
        OUT_C = 64
        BS = 32
        H = 1024
        HID = 128
        key = jax.random.key(seed)
        ks = jax.random.split(key, 10)
        s = lambda fan_in: 1.0 / np.sqrt(fan_in)
        return {'x': jax.random.normal(ks[0], (BS, IN_C, H), dtype=jnp.float32), 'embedding': jax.random.normal(ks[1], (BS, D_EMBD), dtype=jnp.float32), 'W0': jax.random.normal(ks[2], (D_EMBD, HID), dtype=jnp.float32) * s(D_EMBD), 'b0': jnp.zeros((HID,), dtype=jnp.float32), 'W1': jax.random.normal(ks[3], (HID, HID), dtype=jnp.float32) * s(HID), 'b1': jnp.zeros((HID,), dtype=jnp.float32), 'W2': jax.random.normal(ks[4], (HID, K), dtype=jnp.float32) * s(HID), 'b2': jnp.zeros((K,), dtype=jnp.float32), 'weight': jax.random.normal(ks[5], (K, OUT_C, IN_C, 1), dtype=jnp.float32) * s(IN_C), 'bias_k': jax.random.normal(ks[6], (K, OUT_C), dtype=jnp.float32) * 0.1}
    _L1_cond_all = _L1_cond_setup()
    _L1_cond_in = {k: v for k, v in _L1_cond_all.items() if k in ('W0', 'b0', 'W1', 'b1', 'W2', 'b2', 'weight', 'bias_k')}
    del _L1_cond_all

    def _L1_ffn_setup():
        import jax, jax.numpy as jnp
        import numpy as np
        N_EXPERTS = 28
        TOP_K = 2
        RANK = 8
        LORA_ALPHA = 16
        SCALING = LORA_ALPHA / RANK
        TEMP = 1.0
        key = jax.random.key(seed)
        ks = jax.random.split(key, 5)
        B, S, D_IN, D_OUT = (4, 512, 1024, 1024)
        x = jax.random.normal(ks[0], (B, S, D_IN), dtype=jnp.float32)
        base_W = jax.random.normal(ks[1], (D_OUT, D_IN), dtype=jnp.float32) * (1.0 / np.sqrt(D_IN))
        gate_W = jax.random.normal(ks[2], (N_EXPERTS, D_IN), dtype=jnp.float32) * (1.0 / np.sqrt(D_IN))
        lora_A = jax.random.normal(ks[3], (N_EXPERTS, RANK, D_IN), dtype=jnp.float32) * (1.0 / np.sqrt(D_IN))
        lora_B = jax.random.normal(ks[4], (N_EXPERTS, D_OUT, RANK), dtype=jnp.float32) * 0.01
        return {'x': x, 'base_W': base_W, 'gate_W': gate_W, 'lora_A': lora_A, 'lora_B': lora_B}
    _L1_ffn_all = _L1_ffn_setup()
    _L1_ffn_in = {k: v for k, v in _L1_ffn_all.items() if k in ('base_W', 'gate_W', 'lora_A', 'lora_B')}
    del _L1_ffn_all
    return {'x': x, 'cond_128': cond_128, 'fside_S_0': fside_S_0, 'L0_cond_weight': _L0_cond_in['weight'], 'L0_cond_c_weight': _L0_cond_in['c_weight'], 'L0_ffn_base_w': _L0_ffn_in['base_w'], 'L0_ffn_base_b': _L0_ffn_in['base_b'], 'L0_ffn_A': _L0_ffn_in['A'], 'L0_ffn_B': _L0_ffn_in['B'], 'L0_ffn_router_w': _L0_ffn_in['router_w'], 'L1_cond_W0': _L1_cond_in['W0'], 'L1_cond_b0': _L1_cond_in['b0'], 'L1_cond_W1': _L1_cond_in['W1'], 'L1_cond_b1': _L1_cond_in['b1'], 'L1_cond_W2': _L1_cond_in['W2'], 'L1_cond_b2': _L1_cond_in['b2'], 'L1_cond_weight': _L1_cond_in['weight'], 'L1_cond_bias_k': _L1_cond_in['bias_k'], 'L1_ffn_base_W': _L1_ffn_in['base_W'], 'L1_ffn_gate_W': _L1_ffn_in['gate_W'], 'L1_ffn_lora_A': _L1_ffn_in['lora_A'], 'L1_ffn_lora_B': _L1_ffn_in['lora_B']}

def reference(x, cond_128, fside_S_0, L0_cond_weight, L0_cond_c_weight, L0_ffn_base_w, L0_ffn_base_b, L0_ffn_A, L0_ffn_B, L0_ffn_router_w, L1_cond_W0, L1_cond_b0, L1_cond_W1, L1_cond_b1, L1_cond_W2, L1_cond_b2, L1_cond_weight, L1_cond_bias_k, L1_ffn_base_W, L1_ffn_gate_W, L1_ffn_lora_A, L1_ffn_lora_B):
    import jax
    import jax.numpy as jnp

    def _L0_cond_ref(x, c, weight, c_weight, bias):
        import jax, jax.numpy as jnp
        import numpy as np
        from jax import lax
        N, C_IN, L = (32, 64, 1024)
        C_OUT, K, GROUPS = (64, 9, 4)
        C_DIM, PAD, STRIDE = (128, 4, 1)
        out = lax.conv_general_dilated(x, weight, window_strides=(STRIDE,), padding=[(PAD, PAD)], dimension_numbers=('NCH', 'OIH', 'NCH'), feature_group_count=GROUPS)
        ctx = jnp.einsum('nd,od->no', c, c_weight)
        out = out + ctx[:, :, None] + bias[None, :, None]
        return out

    def _L0_ffn_ref(x, base_w, base_b, A, B, router_w):
        import jax, jax.numpy as jnp
        import numpy as np
        TOP_K = 2
        SCALING = 32.0 / 64.0
        base_out = jnp.einsum('bsi,oi->bso', x, base_w) + base_b
        res_hidden = jnp.einsum('bsi,ri->bsr', x, A)
        logits = jnp.einsum('bsi,ei->bse', x, router_w)
        probs = jax.nn.softmax(logits, axis=-1)
        topw, topi = jax.lax.top_k(probs, TOP_K)
        topw = topw / (jnp.sum(topw, axis=-1, keepdims=True) + 1e-06)
        num_experts = B.shape[0]
        combine = jnp.sum(jax.nn.one_hot(topi, num_experts, dtype=x.dtype) * topw[..., None], axis=-2)
        delta = jnp.einsum('bse,bsr,eor->bso', combine, res_hidden, B)
        return base_out + delta * SCALING

    def _L1_cond_ref(x, embedding, W0, b0, W1, b1, W2, b2, weight, bias_k):
        import jax, jax.numpy as jnp
        import numpy as np
        K = 8
        T = 1.0
        D_EMBD = 128
        IN_C = 64
        OUT_C = 64
        BS = 32
        H = 1024
        HID = 128
        h = jax.nn.gelu(embedding @ W0 + b0, approximate=False)
        h = jax.nn.gelu(h @ W1 + b1, approximate=False)
        att = jax.nn.softmax((h @ W2 + b2) / T, axis=-1)
        agg_w = jnp.einsum('bk,koi->boi', att, weight[..., 0])
        agg_b = att @ bias_k
        out = jnp.einsum('boi,bih->boh', agg_w, x) + agg_b[:, :, None]
        return out

    def _L1_ffn_ref(x, base_W, gate_W, lora_A, lora_B):
        import jax, jax.numpy as jnp
        import numpy as np
        N_EXPERTS = 28
        TOP_K = 2
        RANK = 8
        LORA_ALPHA = 16
        SCALING = LORA_ALPHA / RANK
        TEMP = 1.0
        B, S, D_in = x.shape
        xf = x.reshape(B * S, D_in)
        base = xf @ base_W.T
        logits = xf @ gate_W.T
        top_vals, top_idx = jax.lax.top_k(logits, TOP_K)
        top_probs = jax.nn.softmax(top_vals / TEMP, axis=-1)
        N = xf.shape[0]
        gate_full = jnp.zeros((N, N_EXPERTS), dtype=xf.dtype).at[jnp.arange(N)[:, None], top_idx].add(top_probs)
        h = jnp.einsum('nd,erd->ner', xf, lora_A)
        h = h * (gate_full * SCALING)[:, :, None]
        lora_out = jnp.einsum('ner,eor->no', h, lora_B)
        out = base + lora_out
        return out.reshape(B, S, -1)
    x = x + _L0_ffn_ref(_L0_cond_ref(x, cond_128, L0_cond_weight, L0_cond_c_weight, fside_S_0), L0_ffn_base_w, L0_ffn_base_b, L0_ffn_A, L0_ffn_B, L0_ffn_router_w)
    x = x + _L1_ffn_ref(_L1_cond_ref(x, cond_128, L1_cond_W0, L1_cond_b0, L1_cond_W1, L1_cond_b1, L1_cond_W2, L1_cond_b2, L1_cond_weight, L1_cond_bias_k), L1_ffn_base_W, L1_ffn_gate_W, L1_ffn_lora_A, L1_ffn_lora_B)
    return x

_drawn_inputs = setup_inputs


def setup_inputs(seed=0):
    import zlib

    import numpy as np

    out = dict(_drawn_inputs(seed))
    spreads = {'L1_cond_b0': (0.0, 0.61), 'L1_cond_b1': (0.0, 0.422), 'L1_cond_b2': (0.0, 0.332)}
    factors = {'L0_ffn_base_b': 8.0,
     'L1_cond_bias_k': 8.0,
     'L1_ffn_gate_W': 3.425,
     'L1_ffn_lora_A': 3.501,
     'L1_ffn_lora_B': 3.293}
    for name, (base, spread) in spreads.items():
        noise = np.random.default_rng([zlib.crc32(name.encode()), seed]).standard_normal(out[name].shape)
        drawn = base * np.exp(spread * noise) if base else spread * noise
        out[name] = jnp.asarray(drawn.astype(out[name].dtype))
    for name, factor in factors.items():
        out[name] = (out[name] * factor).astype(out[name].dtype)
    return out
```

```python
from contextlib import ExitStack

import concourse.bass as bass
from concourse import mybir

F32 = mybir.dt.float32
F32R = mybir.dt.float32r
U32 = mybir.dt.uint32
ALU = mybir.AluOpType
ACT = mybir.ActivationFunctionType
AX = mybir.AxisListType

P = 128
NS, C, L = 64, 64, 1024
TILES = NS * C // P
HALF = 512
GROUPS, CI, TAPS, PAD = 4, 16, 9, 4
BLK = 8
NB = L // BLK
NG = 2 * GROUPS
KC = L // P
E0, R0 = 16, 64
AR = R0 + E0
E1, R1 = 28, 8
ER1 = E1 * R1
K1 = ER1 // 2
GC = E1 + ER1
MIX = 8
EPS = 1e-6
SCALE0, SCALE1 = 32.0 / 64.0, 16.0 / 8.0
LO = PAD * 2 - 1
SLOTS = 23
PREP_AR, PREP_W0, PREP_B = 2, 16, 16
ROUTE0, ROUTE1 = 10, 10


def build(nc, x, cond, side, conv_w, ctx_w, w0, bias0, loraA0, loraB0, router, cW0, cb0, cW1, cb1,
          cW2, cb2, mix_w, mix_b, w1, gate, loraA1, loraB1, out):
    ctx = ExitStack()
    with ctx:
        def sem(name):
            return ctx.enter_context(nc.semaphore(name))

        def sb(stack, name, shape, dt=F32):
            return stack.enter_context(nc.sbuf_tensor(name, shape, dt))

        bank = [ctx.enter_context(nc.psum_tensor(n, [P, HALF], F32))
                for n in ("z0", "z1", "y0", "y1", "hT0", "hT1", "small", "prep")]
        z, yp, hp, smallp, prepp = bank[0:2], bank[2:4], bank[4:6], bank[6], bank[7]

        def scratch(name, shape):
            return nc.dram_tensor(name, shape, F32, kind="Internal").ap()
        x1_dram = scratch("x1_dram", [TILES * P, L])
        cb_dram = scratch("cb_dram", [NS, C])
        mb_dram = scratch("mb_dram", [NS, C])
        att_dram = scratch("att_dram", [2, TILES, MIX])
        w1_dram = [scratch(f"w1_{s}", [L, L]) for s in ("hi", "lo")]
        g_dram = [scratch(f"g_{s}", [L, GC]) for s in ("hi", "lo")]
        lb_dram = [scratch(f"lb_{s}", [2, K1, L]) for s in ("hi", "lo")]

        ident = sb(ctx, "ident", [P, P])
        iota = sb(ctx, "iota", [P, 32])
        yh = sb(ctx, "yh", [P, KC, P], F32R)
        yl = sb(ctx, "yl", [P, KC, P], F32R)
        xin = [sb(ctx, f"xin{u}", [P, L]) for u in range(2)]
        xb = [sb(ctx, f"xb{u}", [P, L]) for u in range(2)]
        rowb = [sb(ctx, f"rowb{u}", [P, P]) for u in range(2)]
        mixT = sb(ctx, "mixT", [P, MIX, C])
        attb = sb(ctx, "attb", [P, TILES, MIX])
        lg = sb(ctx, "lg", [P, 32])
        top8 = sb(ctx, "top8", [P, 8])
        idx = sb(ctx, "idx", [P, 8], U32)
        idxf = sb(ctx, "idxf", [P, 2])
        negm = sb(ctx, "negm", [P, 1])
        ex = sb(ctx, "ex", [P, 32])
        exsum = sb(ctx, "exsum", [P, 1])
        e12 = sb(ctx, "e12", [P, 2])
        e12sum = sb(ctx, "e12sum", [P, 1])
        den = sb(ctx, "den", [P, 1])
        rden = sb(ctx, "rden", [P, 1])
        w12 = sb(ctx, "w12", [P, 2])
        comb1 = sb(ctx, "comb1", [P, 32])
        comb2 = sb(ctx, "comb2", [P, 32])
        comb = sb(ctx, "comb", [P, 32])

        s0 = ExitStack()
        w0h = sb(s0, "w0h", [P, KC, L], F32R)
        w0l = sb(s0, "w0l", [P, KC, L], F32R)
        pro = ExitStack()
        w0nat = sb(pro, "w0nat", [P, KC, L])
        arnat = sb(pro, "arnat", [AR, L])
        traw = sb(pro, "traw", [P, 2, BLK, C])
        taps = sb(pro, "taps", [CI, SLOTS, C])
        mixnat = sb(pro, "mixnat", [P, 4, 2, C])
        convnat = sb(pro, "convnat", [C, CI * TAPS])
        cnat = sb(pro, "cnat", [NS, P])
        ctxnat = sb(pro, "ctxnat", [C, P])
        condT = sb(pro, "condT", [P, NS])
        ctxT = sb(pro, "ctxT", [P, C])
        sideb = sb(pro, "sideb", [NS, C])
        cbn = sb(pro, "cbn", [NS, C])
        cw = [sb(pro, f"cw{j}", [P, P]) for j in range(2)]
        cbias = [sb(pro, f"cbias{j}", [P, 1]) for j in range(2)]
        w2 = sb(pro, "w2", [P, MIX])
        b2b = sb(pro, "b2b", [NS, MIX])
        mixbias = sb(pro, "mixbias", [MIX, C])
        hid = [sb(pro, f"hid{j}", [P, NS]) for j in range(2)]
        att = sb(pro, "att", [NS, MIX])
        attT = sb(pro, "attT", [MIX, NS])
        astat = sb(pro, "astat", [NS, 4])
        mbn = sb(pro, "mbn", [NS, C])
        pro.close()
        bh = sb(s0, "bh", [P, KC, L], F32R)
        bl = sb(s0, "bl", [P, KC, L], F32R)
        arh = sb(s0, "arh", [P, KC, AR], F32R)
        arl = sb(s0, "arl", [P, KC, AR], F32R)
        th = sb(s0, "th", [P, 2, BLK, C], F32R)
        tl = sb(s0, "tl", [P, 2, BLK, C], F32R)
        bias0b = sb(s0, "bias0b", [P, L])
        xd = sb(s0, "xd", [P, BLK, NB + 1])
        x8h = sb(s0, "x8h", [P, NG, NB + 1], F32R)
        alias = ExitStack()
        x8 = sb(alias, "x8", [P, NG, NB + 1])
        alias.close()
        x8l = sb(s0, "x8l", [P, NG, NB + 1], F32R)
        hx = sb(s0, "hx", [P, L])
        bnat_stack = ExitStack()
        bnat = [sb(bnat_stack, f"bnat{j}", [P, E0, R0]) for j in range(2)]
        bnat_stack.close()
        hTh = sb(s0, "hTh", [P, KC, P], F32R)
        hTl = sb(s0, "hTl", [P, KC, P], F32R)
        w1nat = sb(s0, "w1nat", [64, HALF])
        lbnat = sb(s0, "lbnat", [64, E1, R1])
        gnat = sb(s0, "gnat", [E1, 64])
        lanat = sb(s0, "lanat", [K1, 2, 64])
        stage = [sb(s0, f"stage_{s}", [P, 508], F32R) for s in ("hi", "lo")]
        s0.close()

        s1 = ExitStack()
        gh = sb(s1, "gh", [P, KC, GC], F32R)
        gl = sb(s1, "gl", [P, KC, GC], F32R)
        w1h = sb(s1, "w1h", [P, KC, L], F32R)
        w1l = sb(s1, "w1l", [P, KC, L], F32R)
        lbh = sb(s1, "lbh", [K1, 2, L], F32R)
        lbl = sb(s1, "lbl", [K1, 2, L], F32R)
        x1h = sb(s1, "x1h", [P, L], F32R)
        x1l = sb(s1, "x1l", [P, L], F32R)
        mixh = sb(s1, "mixh", [P, P], F32R)
        mixl = sb(s1, "mixl", [P, P], F32R)
        mprod = sb(s1, "mprod", [P, MIX, C])
        msum = sb(s1, "msum", [P, C])
        hx1 = sb(s1, "hx1", [P, ER1])
        h1h = sb(s1, "h1h", [K1, 2, P], F32R)
        h1l = sb(s1, "h1l", [K1, 2, P], F32R)
        s1.close()

        id_zero, id_ready, iota_ready = sem("id_zero"), sem("id_ready"), sem("iota_ready")
        pads_ready, taps_zero = sem("pads_ready"), sem("taps_zero")
        w0_in = [sem(f"w0_in{j}") for j in range(KC)]
        b_in = [sem(f"b_in{j}") for j in range(2)]
        ar_in, c_in, ctxw_in, side_in = sem("ar_in"), sem("c_in"), sem("ctxw_in"), sem("side_in")
        mlp_in, mixw_in, conv_in, bias0_in = sem("mlp_in"), sem("mixw_in"), sem("conv_in"), sem("bias0_in")
        condT_ps, condT_sb, ctx_ps, ctx_ready = sem("condT_ps"), sem("condT_sb"), sem("ctx_ps"), sem("ctx_ready")
        ctx_stored = sem("ctx_stored")
        hid_ps, hid_ready = sem("hid_ps"), sem("hid_ready")
        att_ps, att_max, att_exp, att_ready, att_stored = (sem(n) for n in ("att_ps", "att_max", "att_exp", "att_ready", "att_stored"))
        attT_ps, attT_sb, mb_ps, mb_ready, mb_stored = (sem(n) for n in ("attT_ps", "attT_sb", "mb_ps", "mb_ready", "mb_stored"))
        attb_in = sem("attb_in")
        taps_ps, taps_sb, traw_in, th_ready, tl_ready = (sem(n) for n in ("taps_ps", "taps_sb", "traw_in", "th_ready", "tl_ready"))
        mixT_ps, mixT_ready = sem("mixT_ps"), sem("mixT_ready")
        prep_ps, prep_hi, prep_lo = sem("prep_ps"), sem("prep_hi"), sem("prep_lo")

        x_in = [sem(f"x_in{u}") for u in range(2)]
        xd_ready, x8_in, x8_hi, x8_lo = (sem(n) for n in ("xd_ready", "x8_in", "x8_hi", "x8_lo"))
        xb_ready = sem("xb_ready")
        w1_in, w1_ps, w1_hi, w1_lo, w1_stored = (sem(n) for n in ("w1_in", "w1_ps", "w1_hi", "w1_lo", "w1_stored"))
        x1_stored = [sem(f"x1_stored{u}") for u in range(2)]

        class Layer:
            pass

        def layer(tag):
            s = Layer()
            s.y_ps = [sem(f"{tag}_y_ps{b}") for b in range(2)]
            s.y_sum = [sem(f"{tag}_y_sum{b}") for b in range(2)]
            s.y_hi = [sem(f"{tag}_y_hi{b}") for b in range(2)]
            s.y_lo = [sem(f"{tag}_y_lo{b}") for b in range(2)]
            s.small_ps = sem(f"{tag}_small_ps")
            s.route = sem(f"{tag}_route")
            s.exp = sem(f"{tag}_exp")
            s.hx = sem(f"{tag}_hx")
            s.hT_ps = sem(f"{tag}_hT_ps")
            s.hT_hi = sem(f"{tag}_hT_hi")
            s.hT_lo = sem(f"{tag}_hT_lo")
            s.base_done = sem(f"{tag}_base_done")
            s.z_ps = [sem(f"{tag}_z_ps{h}") for h in range(2)]
            s.z_out = [sem(f"{tag}_z_out{h}") for h in range(2)]
            return s
        a0, a1 = layer("l0"), layer("l1")
        x1_in = [sem(f"x1_in{u}") for u in range(2)]
        x1_hi, x1_lo = sem("x1_hi"), sem("x1_lo")
        mprod_done, msum_done, mix_hi, mix_lo, mix_zero = (sem(n) for n in ("mprod_done", "msum_done", "mix_hi", "mix_lo", "mix_zero"))
        g_in, w1h_in, w1l_in, lb_in = sem("g_in"), sem("w1h_in"), sem("w1l_in"), sem("lb_in")
        out_stored = [sem(f"out_stored{u}") for u in range(2)]

        x_t = x.rearrange("s c l -> (s c) l").rearrange("(t p) l -> t p l", p=P)
        out_t = out.rearrange("s c l -> (s c) l").rearrange("(t p) l -> t p l", p=P)
        x1_t = x1_dram.rearrange("(t p) l -> t p l", p=P)
        cb_t = cb_dram.rearrange("(t s) c -> t (s c)", s=2)
        mb_t = mb_dram.rearrange("(t s) c -> t (s c)", s=2)
        w1_t = w1.rearrange("(i o) (u l) -> u i o l", o=64, u=2)
        lb_t = loraB1.rearrange("e (i o) r -> i o e r", o=64)
        gate_t = gate.rearrange("e (i l) -> i e l", l=64)
        la_t = loraA1.rearrange("e r l -> (e r) l").rearrange("(k p) (i l) -> i p k l", k=2, l=64)
        w1_st = [d.rearrange("(u k p) (i o) -> u i p k o", u=2, p=P, o=64) for d in w1_dram]
        g_st = [d.rearrange("(i l) c -> i l c", l=64) for d in g_dram]
        lb_st = [d.rearrange("k p (i o) -> i p k o", o=64) for d in lb_dram]

        def row(ap, n):
            return ap.rearrange("(a n) -> a n", a=1).to_broadcast([n, ap.shape[0]])

        def pbank(q):
            return (z[0], z[1], hp[0], hp[1])[q % 4]

        def prep_places(ar, w, b):
            for q in range(PREP_AR):
                yield ar[:, 4 * q:4 * q + 4, :], pbank(q)[:, 0:4 * AR].rearrange("p (k a) -> p k a", a=AR)
            for q in range(PREP_AR, PREP_AR + PREP_W0):
                half, k = divmod(q - PREP_AR, KC)
                yield w[:, k, HALF * half:HALF * (half + 1)], pbank(q)[:, :]
            for q in range(PREP_AR + PREP_W0, PREP_AR + PREP_W0 + PREP_B):
                n, hk = divmod(q - PREP_AR - PREP_W0, 2)
                yield (b[:, 4 * hk:4 * hk + 4, P * n:P * (n + 1)],
                       pbank(q)[:, :].rearrange("p (k o) -> p k o", o=P))

        block = ctx.enter_context(nc.Block())

        @block.sync
        def _(sp):
            def load_x(i, u):
                sp.dma_start(xin[u][:, :], x_t[2 * i + u]).then_inc(x_in[u], 16)
                sp.dma_start(rowb[u][:, :], row(cb_t[2 * i + u], P)).then_inc(x_in[u], 16)

            def spread_x(t, first=False):
                sp.wait_ge(xd_ready, t + 1)
                if not first:
                    sp.wait_ge(a0.y_ps[1], t)
                for n in range(NG):
                    sp.dma_start(x8[:, n, :], xd[CI * n:CI * (n + 1), :, :]).then_inc(x8_in, 16)

            def load_w1(i, u):
                sp.dma_start(w1nat[:, :], w1_t[u, i]).then_inc(w1_in, 16)
                if u == 0:
                    with nc.allow_non_contiguous_dma(reason="rank-8 rows"):
                        sp.dma_start(lbnat[:, :, :], lb_t[i]).then_inc(w1_in, 32)
                else:
                    sp.dma_start(gnat[:, :], gate_t[i]).then_inc(w1_in, 16)
                    sp.dma_start(lanat[:, :, :], la_t[i]).then_inc(w1_in, 16)

            def store_w1(i, u, t):
                for s, done in ((0, w1_hi), (1, w1_lo)):
                    sp.wait_ge(done, t + 1)
                    src = stage[s][:, :].bitcast(F32)
                    sp.dma_start(w1_st[s][u, i], src[:, 0:256].rearrange("p (k o) -> p k o", o=64))\
                      .then_inc(w1_stored, 16)
                    if u == 0:
                        sp.dma_start(lb_st[s][i], src[0:K1, 256:384].rearrange("p (k o) -> p k o", o=64))\
                          .then_inc(w1_stored, 16)
                    else:
                        sp.dma_start(g_st[s][i], src[0:64, 256:256 + GC]).then_inc(w1_stored, 16)

            def store_x1(i, u):
                sp.wait_ge(a0.z_out[0], 2 * i + u + 1)
                sp.wait_ge(a0.z_out[1], 2 * i + u + 1)
                sp.dma_start(x1_t[2 * i + u], xb[u][:, :]).then_inc(x1_stored[u], 16)

            sp.dma_start(xin[0][:, :], x_t[0]).then_inc(x_in[0], 16)
            sp.dma_start(arnat[0:R0, :], loraA0).then_inc(ar_in, 16)
            sp.dma_start(arnat[R0:AR, :], router).then_inc(ar_in, 16)
            for j in range(KC):
                sp.dma_start(w0nat[:, j, :], w0[P * j:P * (j + 1), :]).then_inc(w0_in[j], 16)
            sp.wait_ge(taps_sb, 2)
            for w in range(2):
                for j in range(BLK):
                    s = 15 - BLK * w - j
                    sp.dma_start(traw[j:P:BLK, w, :, :], taps[:, s:s + BLK, :])\
                      .then_inc(traw_in, 16)
            sp.wait_ge(ctx_ready, 1)
            sp.dma_start(cb_dram, cbn[:, :]).then_inc(ctx_stored, 16)
            sp.wait_ge(ctx_stored, 16)
            sp.dma_start(rowb[0][:, :], row(cb_t[0], P)).then_inc(x_in[0], 16)
            sp.dma_start(bias0b[:, :], row(bias0, P)).then_inc(bias0_in, 16)
            spread_x(0, first=True)
            load_x(0, 1)
            sp.wait_ge(att_ready, 1)
            sp.dma_start(att_dram.rearrange("s t k -> t s k"), att[:, :]).then_inc(att_stored, 16)
            sp.wait_ge(att_stored, 16)
            for s in range(2):
                sp.dma_start(attb[64 * s:64 * (s + 1), :, :].rearrange("p t k -> p (t k)"),
                             row(att_dram[s].rearrange("t k -> (t k)"), 64)).then_inc(attb_in, 16)
            sp.wait_ge(mb_ready, 1)
            sp.dma_start(mb_dram, mbn[:, :]).then_inc(mb_stored, 16)
            sp.wait_ge(mb_stored, 16)
            for j in range(KC):
                if j >= 2:
                    sp.wait_ge(prep_ps, PREP_AR + PREP_W0 + 2 * (j - 1))
                sp.dma_start(bnat[j % 2][:, :, :], loraB0[:, P * j:P * (j + 1), :].rearrange("e o r -> o e r"))\
                  .then_inc(b_in[j % 2], 16)
            load_w1(0, 0)

            def step0(i, u, prefetch=True, last=False):
                t = 2 * i + u
                if prefetch:
                    sp.wait_ge(xd_ready, t + 1)
                    sp.wait_ge(xb_ready, t + 1)
                    sp.wait_ge(a0.y_sum[1], t + 1)
                    load_x(i + 1, u)
                if not last:
                    spread_x(t + 1)
                sp.wait_ge(w1_ps, t + 1)
                if not last:
                    load_w1(i + u, 1 - u)
                store_w1(i, u, t)
                store_x1(i, u)

            with sp.Fori(0, TILES // 2 - 1) as i:
                step0(i, 0)
                step0(i, 1)
            step0(TILES // 2 - 1, 0, prefetch=False)
            n = TILES // 2 - 1
            sp.wait_ge(w1_ps, TILES)
            store_w1(n, 1, TILES - 1)
            sp.wait_ge(w1_stored, 64 * TILES)
            sp.wait_ge(a0.base_done, TILES)
            for dst, d in ((gh, g_dram[0]), (gl, g_dram[1])):
                sp.dma_start(dst[:, :, :].bitcast(F32), d.rearrange("(k p) c -> p k c", p=P)).then_inc(g_in, 16)
            hc = KC // 2
            w1v = [d.rearrange("(k p) o -> p k o", p=P) for d in w1_dram]
            sp.wait_ge(x1_stored[0], 16 * (TILES // 2))

            def load_x1(i, u):
                sp.dma_start(xin[u][:, :], x1_t[2 * i + u]).then_inc(x1_in[u], 16)
                sp.dma_start(rowb[u][:, :], row(mb_t[2 * i + u], P)).then_inc(x1_in[u], 16)

            sp.wait_ge(xb_ready, TILES)
            sp.wait_ge(xd_ready, TILES)
            sp.wait_ge(a0.y_sum[1], TILES)
            load_x1(0, 0)
            sp.dma_start(w1h[:, 0:hc, :].bitcast(F32), w1v[0][:, 0:hc, :]).then_inc(w1h_in, 16)
            sp.wait_ge(a0.z_ps[1], TILES)
            sp.dma_start(w1h[:, hc:KC, :].bitcast(F32), w1v[0][:, hc:KC, :]).then_inc(w1h_in, 16)
            sp.dma_start(w1l[:, :, :].bitcast(F32), w1v[1]).then_inc(w1l_in, 16)
            store_x1(n, 1)
            load_x1(0, 1)
            for dst, d in ((lbh, lb_dram[0]), (lbl, lb_dram[1])):
                sp.dma_start(dst[:, :, :].bitcast(F32), d.rearrange("k p o -> p k o")).then_inc(lb_in, 16)

            def step1(i, u, prefetch=True):
                t = 2 * i + u
                sp.wait_ge(a1.z_out[0], t + 1)
                sp.wait_ge(a1.z_out[1], t + 1)
                sp.dma_start(out_t[t], xb[u][:, :]).then_inc(out_stored[u], 16)
                if prefetch:
                    load_x1(i + 1, u)

            with sp.Fori(0, TILES // 2 - 1) as i:
                step1(i, 0)
                step1(i, 1)
            step1(n, 0, prefetch=False)
            step1(n, 1, prefetch=False)
            for u in range(2):
                sp.wait_ge(out_stored[u], 16 * (TILES // 2))
                sp.wait_ge(x1_stored[u], 16 * (TILES // 2))

        @block.gpsimd
        def _(pool):
            nc.gpsimd.memset(ident[:, :], 0.0).then_inc(id_zero, 1)
            pool.wait_ge(id_zero, 1)
            nc.gpsimd.affine_select(out=ident[:, :], in_=ident[:, :], compare_op=ALU.not_equal, fill=1.0,
                                    base=0, pattern=[[-1, P]], channel_multiplier=1).then_inc(id_ready, 1)
            nc.gpsimd.memset(taps[:, :, :], 0.0).then_inc(taps_zero, 1)
            nc.gpsimd.iota(iota[:, :], pattern=[[1, 32]], base=0, channel_multiplier=0,
                           allow_small_or_imprecise_dtypes=True).then_inc(iota_ready, 1)
            nc.gpsimd.memset(xd[:, 0:PAD, 0:1], 0.0).then_inc(pads_ready, 1)
            nc.gpsimd.memset(xd[:, PAD:BLK, NB:NB + 1], 0.0).then_inc(pads_ready, 1)
            pool.wait_ge(bias0_in, 16)

            def residual(i, u, first=False):
                pool.wait_ge(x_in[u], 32 * (i + 1))
                if not first:
                    pool.wait_ge(x1_stored[u], 16 * i)
                nc.gpsimd.tensor_tensor(xb[u][:, :], xin[u][:, :], bias0b[:, :], ALU.add).then_inc(xb_ready, 1)

            residual(0, 0, first=True)
            residual(0, 1, first=True)
            with pool.Fori(1, TILES // 2) as i:
                residual(i, 0)
                residual(i, 1)

        @block.scalar
        def _(act):
            def copy(o, i_):
                return nc.scalar.activation(o, i_, ACT.Copy)

            act.dma_start(convnat[:, :], conv_w.rearrange("o c k -> o (c k)")).then_inc(conv_in, 16)
            act.dma_start(cnat[:, :], cond).then_inc(c_in, 16)
            act.dma_start(ctxnat[:, :], ctx_w).then_inc(ctxw_in, 16)
            act.dma_start(sideb[:, :], row(side, NS)).then_inc(side_in, 16)
            for j, (w, b) in enumerate(((cW0, cb0), (cW1, cb1))):
                act.dma_start(cw[j][:, :], w).then_inc(mlp_in, 16)
                act.dma_start(cbias[j][:, :], b.rearrange("(n a) -> n a", a=1)).then_inc(mlp_in, 16)
            act.dma_start(w2[:, :], cW2).then_inc(mlp_in, 16)
            act.dma_start(b2b[:, :], row(cb2, NS)).then_inc(mlp_in, 16)
            act.dma_start(mixbias[:, :], mix_b).then_inc(mlp_in, 16)
            mixw_v = mix_w.rearrange("k o i a -> (k o) (i a)").rearrange("(j p) i -> p j i", p=P)
            for s in range(2):
                act.dma_start(mixnat[:, :, s, :], mixw_v).then_inc(mixw_in, 16)

            def blocks(i, u):
                act.wait_ge(x_in[u], 16 if isinstance(i, int) and i == 0 and u == 0 else 32 * i + 32)
                v = xin[u][:, :].rearrange("p (m j) -> p j m", j=BLK)
                copy(xd[:, PAD:BLK, 0:NB], v[:, 0:PAD, :])
                copy(xd[:, 0:PAD, 1:NB + 1], v[:, PAD:BLK, :]).then_inc(xd_ready, 1)

            def x8_high(t):
                act.wait_ge(x8_in, 128 * t + 128)
                copy(x8h[:, :, :], x8[:, :, :]).then_inc(x8_hi, 1)

            def y_high(s, t, b):
                act.wait_ge(s.y_sum[b], t + 1)
                if s is a0:
                    o = yh[:, :, C * b:C * (b + 1)]
                    v = yp[b][:, :].rearrange("p (j c) -> p j c", c=C)
                else:
                    o = yh[:, 4 * b:4 * b + 4, :]
                    v = yp[b][:, :].rearrange("p (j c) -> p j c", c=P)
                copy(o, v).then_inc(s.y_hi[b], 1)

            def exps(s, t):
                act.wait_ge(s.route, ROUTE0 * t + 3)
                if s is a0:
                    nc.scalar.activation(ex[:, 0:E0], lg[:, 0:E0], ACT.Exp, bias=negm[:, :],
                                         accum_out=exsum[:, :]).then_inc(s.exp, 1)
                else:
                    copy(ex[:, 0:1], negm[:, :]).then_inc(s.exp, 1)
                nc.scalar.activation(e12[:, :], top8[:, 0:2], ACT.Exp, bias=negm[:, :],
                                     accum_out=e12sum[:, :]).then_inc(s.exp, 1)

            act.wait_ge(pads_ready, 2)
            blocks(0, 0)
            act.wait_ge(taps_zero, 1)
            act.wait_ge(taps_ps, 1)
            copy(taps[:, LO:LO + 8, :], yp[0][0:CI, :].rearrange("p (k o) -> p k o", o=C)).then_inc(taps_sb, 1)
            copy(taps[:, LO + 8, :], yp[1][0:CI, 0:C]).then_inc(taps_sb, 1)
            act.wait_ge(condT_ps, 2)
            copy(condT[:, :], prepp[:, 0:NS]).then_inc(condT_sb, 1)
            copy(ctxT[:, :], prepp[:, NS:NS + C]).then_inc(condT_sb, 1)

            high = list(prep_places(arh, w0h, bh))

            def prep_high(first, end):
                for q in range(first, end):
                    act.wait_ge(prep_ps, q + 1)
                    copy(*high[q]).then_inc(prep_hi, 1)

            prep_high(0, PREP_AR)
            act.wait_ge(mlp_in, 16 * 7)
            for j in range(2):
                act.wait_ge(hid_ps, j + 1)
                nc.scalar.activation(hid[j][:, :], yp[0][:, NS * j:NS * (j + 1)], ACT.Gelu,
                                     bias=cbias[j][:, :]).then_inc(hid_ready, 1)
            act.wait_ge(traw_in, 16 * 2 * BLK)
            copy(th[:, :, :, :], traw[:, :, :, :]).then_inc(th_ready, 1)
            x8_high(0)
            act.wait_ge(mixT_ps, 1)
            copy(mixT[:, :, :], yp[1][:, :].rearrange("p (k o) -> p k o", o=C)).then_inc(mixT_ready, 1)
            act.wait_ge(att_max, 3)
            nc.scalar.activation(att[:, :], lg[0:NS, 0:MIX], ACT.Exp, bias=astat[:, 1:2],
                                 accum_out=astat[:, 2:3]).then_inc(att_exp, 1)
            prep_high(PREP_AR, PREP_AR + PREP_W0 + PREP_B)
            y_high(a0, 0, 0)
            y_high(a0, 0, 1)

            def step0(i, u, first=False, last=False):
                t = 2 * i + u
                if not last:
                    act.wait_ge(x8_in, 128 * t + 128)
                    blocks(i + u, 1 - u)
                exps(a0, t)
                if not last:
                    act.wait_ge(a0.y_ps[1], t + 1)
                    x8_high(t + 1)
                if not first:
                    act.wait_ge(w1_stored, 64 * t)
                act.wait_ge(w1_ps, t + 1)
                copy(stage[0][:, 0:256], prepp[:, 0:256])
                if u == 0:
                    copy(stage[0][0:K1, 256:384], prepp[0:K1, 256:384]).then_inc(w1_hi, 1)
                else:
                    copy(stage[0][0:64, 256:256 + GC], prepp[0:64, 256:256 + GC]).then_inc(w1_hi, 1)
                for b in range(2):
                    act.wait_ge(a0.hT_ps, 2 * t + b + 1)
                    copy(hTh[:, 4 * b:4 * b + 4, :], hp[b][:, :].rearrange("p (k r) -> p k r", r=P))\
                        .then_inc(a0.hT_hi, 1)
                if not last:
                    y_high(a0, t + 1, 0)
                    y_high(a0, t + 1, 1)

            step0(0, 0, first=True)
            step0(0, 1)
            with act.Fori(1, TILES // 2 - 1) as i:
                step0(i, 0)
                step0(i, 1)
            step0(TILES // 2 - 1, 0)
            step0(TILES // 2 - 1, 1, last=True)

            def x1_high(i, u, t):
                act.wait_ge(x1_in[u], 32 * i + 32)
                copy(x1h[:, :], xin[u][:, :]).then_inc(x1_hi, 1)
                act.wait_ge(msum_done, t + 1)
                for s in range(2):
                    q = slice(64 * s, 64 * (s + 1))
                    copy(mixh[q, q], msum[q, :]).then_inc(mix_hi, 1)

            act.wait_ge(a0.z_ps[1], TILES)
            act.wait_ge(mix_zero, 2)
            x1_high(0, 0, 0)
            y_high(a1, 0, 0)
            y_high(a1, 0, 1)

            def step1(i, u, last=False):
                t = 2 * i + u
                exps(a1, t)
                if not last:
                    act.wait_ge(a1.y_ps[1], t + 1)
                    x1_high(i + u, 1 - u, t + 1)
                act.wait_ge(a1.hT_ps, t + 1)
                copy(h1h[:, :, :], hp[0][0:K1, 0:2 * P].rearrange("p (k r) -> p k r", r=P)).then_inc(a1.hT_hi, 1)
                if not last:
                    y_high(a1, t + 1, 0)
                    y_high(a1, t + 1, 1)

            with act.Fori(0, TILES // 2 - 1) as i:
                step1(i, 0)
                step1(i, 1)
            step1(TILES // 2 - 1, 0)
            step1(TILES // 2 - 1, 1, last=True)

        @block.vector
        def _(dve):
            V = nc.vector

            def x8_low(t):
                dve.wait_ge(x8_hi, t + 1)
                V.tensor_tensor(x8l[:, :, :], x8[:, :, :], x8h[:, :, :], ALU.subtract).then_inc(x8_lo, 1)

            def y_low(s, t, b, bias):
                dve.wait_ge(s.y_ps[b], t + 1)
                if s is a0:
                    v = yp[b][:, :].rearrange("p (j c) -> p j c", c=C)
                    rb = bias[:, C * b:C * (b + 1)].unsqueeze(1).to_broadcast([P, KC, C])
                    oh, ol = (y[:, :, C * b:C * (b + 1)] for y in (yh, yl))
                else:
                    v = yp[b][:, :].rearrange("p (j c) -> p j c", c=P)
                    rb = bias[:, :].unsqueeze(1).to_broadcast([P, 4, P])
                    oh, ol = (y[:, 4 * b:4 * b + 4, :] for y in (yh, yl))
                V.tensor_tensor(v, v, rb, ALU.add).then_inc(s.y_sum[b], 1)
                return v, oh, ol

            def y_parts(s, i, u, t):
                dve.wait_ge((x_in if s is a0 else x1_in)[u], 32 * i + 32)
                parts = [y_low(s, t, b, rowb[u]) for b in range(2)]
                for b, (v, oh, ol) in enumerate(parts):
                    dve.wait_ge(s.y_hi[b], t + 1)
                    V.tensor_tensor(ol, v, oh, ALU.subtract).then_inc(s.y_lo[b], 1)

            def routing(s, t, first, experts, scale):
                r = s.route

                def after(k):
                    dve.wait_ge(r, ROUTE0 * t + k)
                dve.wait_ge(s.small_ps, t + 1)
                V.tensor_copy(lg[:, 0:experts], smallp[:, first:first + experts]).then_inc(r, 1)
                V.max(top8[:, :], smallp[:, first:first + experts]).then_inc(r, 1)
                after(2)
                V.tensor_scalar(negm[:, :], top8[:, 0:1], -1.0, None, ALU.mult).then_inc(r, 1)
                V.max_index(idx[:, :], top8[:, :], lg[:, 0:experts]).then_inc(r, 1)
                after(4)
                V.tensor_copy(idxf[:, :], idx[:, 0:2]).then_inc(r, 1)
                dve.wait_ge(s.exp, 2 * t + 2)
                if s is a0:
                    V.tensor_scalar(den[:, :], exsum[:, :], EPS, e12sum[:, :], ALU.mult, ALU.add).then_inc(r, 1)
                else:
                    V.tensor_copy(den[:, :], e12sum[:, :]).then_inc(r, 1)
                after(6)
                V.reciprocal(rden[:, :], den[:, :]).then_inc(r, 1)
                after(7)
                V.tensor_scalar(w12[:, :], e12[:, :], rden[:, :], scale, ALU.mult, ALU.mult).then_inc(r, 1)
                after(8)
                V.tensor_scalar(comb1[:, 0:experts], iota[:, 0:experts], idxf[:, 0:1], w12[:, 0:1],
                                ALU.is_equal, ALU.mult).then_inc(r, 1)
                V.tensor_scalar(comb2[:, 0:experts], iota[:, 0:experts], idxf[:, 1:2], w12[:, 1:2],
                                ALU.is_equal, ALU.mult).then_inc(r, 1)
                after(10)

            def spread0(t):
                routing(a0, t, R0, E0, SCALE0)
                V.tensor_tensor(comb[:, 0:E0], comb1[:, 0:E0], comb2[:, 0:E0], ALU.add).then_inc(a0.hx, 1)
                dve.wait_ge(a0.hx, 2 * t + 1)
                V.tensor_tensor(hx[:, :].rearrange("p (e r) -> p e r", r=R0),
                                smallp[:, 0:R0].unsqueeze(1).to_broadcast([P, E0, R0]),
                                comb[:, 0:E0].unsqueeze(2).to_broadcast([P, E0, R0]), ALU.mult).then_inc(a0.hx, 1)

            def spread1(t):
                routing(a1, t, 0, E1, SCALE1)
                V.tensor_tensor(comb[:, 0:E1], comb1[:, 0:E1], comb2[:, 0:E1], ALU.add).then_inc(a1.hx, 1)
                dve.wait_ge(a1.hx, 2 * t + 1)
                V.tensor_tensor(hx1[:, :].rearrange("p (e r) -> p e r", r=R1),
                                smallp[:, E1:GC].rearrange("p (e r) -> p e r", r=R1),
                                comb[:, 0:E1].unsqueeze(2).to_broadcast([P, E1, R1]), ALU.mult).then_inc(a1.hx, 1)

            high, low = list(prep_places(arh, w0h, bh)), list(prep_places(arl, w0l, bl))

            def prep_low(first, end):
                for q in range(first, end):
                    dve.wait_ge(prep_hi, q + 1)
                    V.tensor_tensor(low[q][0], low[q][1], high[q][0], ALU.subtract).then_inc(prep_lo, 1)

            prep_low(0, PREP_AR)
            dve.wait_ge(side_in, 16)
            dve.wait_ge(ctx_ps, 1)
            V.tensor_tensor(cbn[:, :], smallp[0:NS, 0:C], sideb[:, :], ALU.add).then_inc(ctx_ready, 1)
            dve.wait_ge(mlp_in, 16 * 7)
            dve.wait_ge(th_ready, 1)
            V.tensor_tensor(tl[:, :, :, :], traw[:, :, :, :], th[:, :, :, :], ALU.subtract).then_inc(tl_ready, 1)
            x8_low(0)
            dve.wait_ge(att_ps, 1)
            V.tensor_tensor(lg[0:NS, 0:MIX], smallp[0:NS, 256:256 + MIX], b2b[:, :], ALU.add).then_inc(att_max, 1)
            dve.wait_ge(att_max, 1)
            V.tensor_reduce(astat[:, 0:1], lg[0:NS, 0:MIX], AX.X, ALU.max).then_inc(att_max, 1)
            dve.wait_ge(att_max, 2)
            V.tensor_scalar(astat[:, 1:2], astat[:, 0:1], -1.0, None, ALU.mult).then_inc(att_max, 1)
            dve.wait_ge(att_exp, 1)
            V.reciprocal(astat[:, 3:4], astat[:, 2:3]).then_inc(att_max, 1)
            dve.wait_ge(att_max, 4)
            V.tensor_scalar(att[:, :], att[:, :], astat[:, 3:4], None, ALU.mult).then_inc(att_ready, 1)
            dve.wait_ge(attT_ps, 1)
            V.tensor_copy(attT[:, :], smallp[0:MIX, 320:320 + NS]).then_inc(attT_sb, 1)
            dve.wait_ge(mb_ps, 1)
            V.tensor_copy(mbn[:, :], smallp[0:NS, 384:384 + C]).then_inc(mb_ready, 1)
            prep_low(PREP_AR, PREP_AR + PREP_W0)
            dve.wait_ge(attb_in, 32)
            dve.wait_ge(mb_stored, 16)
            prep_low(PREP_AR + PREP_W0, PREP_AR + PREP_W0 + PREP_B)
            y_parts(a0, 0, 0, 0)
            dve.wait_ge(iota_ready, 1)

            def step0(i, u, last=False):
                t = 2 * i + u
                spread0(t)
                if not last:
                    x8_low(t + 1)
                dve.wait_ge(w1_hi, t + 1)
                V.tensor_tensor(stage[1][:, 0:256], prepp[:, 0:256], stage[0][:, 0:256], ALU.subtract)
                if u == 0:
                    q, w = slice(0, K1), slice(256, 384)
                else:
                    q, w = slice(0, 64), slice(256, 256 + GC)
                V.tensor_tensor(stage[1][q, w], prepp[q, w], stage[0][q, w], ALU.subtract).then_inc(w1_lo, 1)
                for b in range(2):
                    dve.wait_ge(a0.hT_hi, 2 * t + b + 1)
                    V.tensor_tensor(hTl[:, 4 * b:4 * b + 4, :], hp[b][:, :].rearrange("p (k r) -> p k r", r=P),
                                    hTh[:, 4 * b:4 * b + 4, :], ALU.subtract).then_inc(a0.hT_lo, 1)
                if not last:
                    y_parts(a0, i + u, 1 - u, t + 1)
                dve.wait_ge(xb_ready, t + 1)
                for h in range(2):
                    dve.wait_ge(a0.z_ps[h], t + 1)
                    o = xb[u][:, HALF * h:HALF * (h + 1)]
                    V.tensor_tensor(o, z[h][:, :], o, ALU.add).then_inc(a0.z_out[h], 1)

            with dve.Fori(0, TILES // 2 - 1) as i:
                step0(i, 0)
                step0(i, 1)
            step0(TILES // 2 - 1, 0)
            step0(TILES // 2 - 1, 1, last=True)

            def mix(i, u, t):
                V.tensor_tensor(mprod[:, :, :], mixT[:, :, :],
                                attb[:, t, :].unsqueeze(2).to_broadcast([P, MIX, C]), ALU.mult).then_inc(mprod_done, 1)
                dve.wait_ge(mprod_done, t + 1)
                V.tensor_reduce(msum[:, :], mprod[:, :, :].rearrange("p k o -> p o k"), AX.X, ALU.add)\
                    .then_inc(msum_done, 1)
                dve.wait_ge(x1_hi, t + 1)
                V.tensor_tensor(x1l[:, :], xin[u][:, :], x1h[:, :], ALU.subtract).then_inc(x1_lo, 1)
                dve.wait_ge(mix_hi, 2 * t + 2)
                for s in range(2):
                    q = slice(64 * s, 64 * (s + 1))
                    V.tensor_tensor(mixl[q, q], msum[q, :], mixh[q, q], ALU.subtract).then_inc(mix_lo, 1)

            dve.wait_ge(a0.z_ps[1], TILES)
            dve.wait_ge(mixT_ready, 1)
            for m in (mixh, mixl):
                V.memset(m[:, :].bitcast(U32), 0).then_inc(mix_zero, 1)
            dve.wait_ge(mix_zero, 2)
            mix(0, 0, 0)
            y_parts(a1, 0, 0, 0)

            def step1(i, u, first=False, last=False):
                t = 2 * i + u
                spread1(t)
                if not last:
                    mix(i + u, 1 - u, t + 1)
                dve.wait_ge(a1.hT_hi, t + 1)
                V.tensor_tensor(h1l[:, :, :], hp[0][0:K1, 0:2 * P].rearrange("p (k r) -> p k r", r=P),
                                h1h[:, :, :], ALU.subtract).then_inc(a1.hT_lo, 1)
                if not last:
                    y_parts(a1, i + u, 1 - u, t + 1)
                dve.wait_ge(x1_stored[u], 16 * (TILES // 2))
                if not first:
                    dve.wait_ge(out_stored[u], 16 * i)
                for h in range(2):
                    dve.wait_ge(a1.z_ps[h], t + 1)
                    w = slice(HALF * h, HALF * (h + 1))
                    V.tensor_tensor(xb[u][:, w], z[h][:, :], xin[u][:, w], ALU.add).then_inc(a1.z_out[h], 1)

            step1(0, 0, first=True)
            step1(0, 1, first=True)
            with dve.Fori(1, TILES // 2 - 1) as i:
                step1(i, 0)
                step1(i, 1)
            step1(TILES // 2 - 1, 0)
            step1(TILES // 2 - 1, 1, last=True)

        @block.tensor
        def _(pe):
            T = nc.tensor

            def three(o, ah, al, wh, wl, start, stop, **kw):
                T.matmul(o, ah, wh, start=start, stop=False, **kw)
                T.matmul(o, al, wh, start=False, stop=False, **kw)
                return T.matmul(o, ah, wl, start=False, stop=stop, **kw)

            def over_y(o, wh, wl, w, stop):
                for k in range(KC):
                    mm = three(o, yh[:, k, :], yl[:, k, :], wh[:, k, w], wl[:, k, w], k == 0, stop and k == KC - 1,
                               skip_group_check=not stop)
                return mm

            def conv(t):
                pe.wait_ge(x8_hi, t + 1)
                pe.wait_ge(x8_lo, t + 1)
                for n in range(2):
                    o = yp[n][:, :].rearrange("p (j g c) -> p g j c", g=GROUPS, c=CI)
                    for g in range(GROUPS):
                        for w in range(2):
                            wv = slice(w, w + NB)
                            gv = slice(CI * g, CI * (g + 1))
                            mm = three(o[:, g, :, :], x8h[:, GROUPS * n + g, wv], x8l[:, GROUPS * n + g, wv],
                                       th[:, w, :, gv], tl[:, w, :, gv], g == 0 and w == 0, w == 1,
                                       skip_group_check=True)
                    mm.then_inc(a0.y_ps[n], 1)

            pe.wait_ge(id_ready, 1)
            pe.wait_ge(conv_in, 16)
            cv = convnat[:, :].rearrange("o (c k) -> o k c", k=TAPS)
            for k in range(TAPS):
                s = 8 - k
                o = yp[s // 8][0:CI, C * (s % 8):C * (s % 8) + C]
                mm = T.transpose(o, cv[:, k, :], ident[0:C, 0:C])
            mm.then_inc(taps_ps, 1)
            pe.wait_ge(c_in, 16)
            T.transpose(prepp[:, 0:NS], cnat[:, :], ident[0:NS, 0:NS]).then_inc(condT_ps, 1)
            pe.wait_ge(ctxw_in, 16)
            T.transpose(prepp[:, NS:NS + C], ctxnat[:, :], ident[0:C, 0:C]).then_inc(condT_ps, 1)
            pe.wait_ge(condT_sb, 2)
            T.matmul(smallp[0:NS, 0:C], condT[:, :], ctxT[:, :], start=True, stop=True).then_inc(ctx_ps, 1)
            pe.wait_ge(taps_sb, 2)
            pe.wait_ge(mlp_in, 16 * 7)
            T.matmul(yp[0][:, 0:NS], cw[0][:, :], condT[:, :], start=True, stop=True).then_inc(hid_ps, 1)
            pe.wait_ge(ar_in, 32)
            av = arnat[:, :].rearrange("a (b j) -> a j b", j=BLK)
            for q in range(PREP_AR):
                for k in range(4):
                    mm = T.transpose(pbank(q)[:, AR * k:AR * (k + 1)], av[:, 4 * q + k, :], ident[0:AR, 0:AR])
                mm.then_inc(prep_ps, 1)
            pe.wait_ge(hid_ready, 1)
            T.matmul(yp[0][:, NS:2 * NS], cw[1][:, :], hid[0][:, :], start=True, stop=True).then_inc(hid_ps, 1)
            pe.wait_ge(mixw_in, 32)
            pe.wait_ge(taps_sb, 2)
            for j in range(4):
                mm = T.transpose(yp[1][:, P * j:P * (j + 1)], mixnat[:, j, :, :].rearrange("p s i -> p (s i)"),
                                 ident[:, :])
            mm.then_inc(mixT_ps, 1)
            pe.wait_ge(hid_ready, 2)
            pe.wait_ge(ctx_ready, 1)
            T.matmul(smallp[0:NS, 256:256 + MIX], hid[1][:, :], w2[:, :], start=True, stop=True).then_inc(att_ps, 1)
            pe.wait_ge(att_ready, 1)
            T.transpose(smallp[0:MIX, 320:320 + NS], att[:, :], ident[0:NS, 0:NS]).then_inc(attT_ps, 1)
            pe.wait_ge(attT_sb, 1)
            T.matmul(smallp[0:NS, 384:384 + C], attT[:, :], mixbias[:, :], start=True, stop=True).then_inc(mb_ps, 1)
            wv = w0nat[:, :, :].rearrange("p n (b j) -> p n j b", j=BLK)
            for q in range(PREP_AR, PREP_AR + PREP_W0):
                half, k = divmod(q - PREP_AR, KC)
                if q >= 4:
                    pe.wait_ge(prep_lo, q - 3)
                for n in range(4 * half, 4 * half + 4):
                    if k == 0:
                        pe.wait_ge(w0_in[n], 16)
                    mm = T.transpose(pbank(q)[:, P * (n % 4):P * (n % 4) + P], wv[:, n, k, :], ident[:, :])
                mm.then_inc(prep_ps, 1)
            for q in range(PREP_AR + PREP_W0, PREP_AR + PREP_W0 + PREP_B):
                n, hk = divmod(q - PREP_AR - PREP_W0, 2)
                pe.wait_ge(prep_lo, q - 3)
                if hk == 0:
                    pe.wait_ge(b_in[n % 2], 16 * (n // 2 + 1))
                for k in range(4):
                    e = 2 * (4 * hk + k)
                    mm = T.transpose(pbank(q)[:, P * k:P * (k + 1)],
                                     bnat[n % 2][:, e:e + 2, :].rearrange("p e r -> p (e r)"), ident[:, :])
                mm.then_inc(prep_ps, 1)
            pe.wait_ge(prep_lo, PREP_AR + PREP_W0 + PREP_B)
            pe.wait_ge(tl_ready, 1)
            pe.wait_ge(mixT_ready, 1)
            conv(0)

            def w1_pieces(t, u):
                for k in range(4):
                    T.transpose(prepp[:, 64 * k:64 * (k + 1)], w1nat[:, P * k:P * (k + 1)], ident[0:64, 0:64])
                if u == 0:
                    for k in range(2):
                        e = E1 // 2
                        mm = T.transpose(prepp[0:K1, 256 + 64 * k:320 + 64 * k],
                                         lbnat[:, e * k:e * (k + 1), :].rearrange("p e r -> p (e r)"),
                                         ident[0:64, 0:64])
                else:
                    T.transpose(prepp[0:64, 256:256 + E1], gnat[:, :], ident[0:E1, 0:E1])
                    for k in range(2):
                        c0 = 256 + E1 + K1 * k
                        mm = T.transpose(prepp[0:64, c0:c0 + K1], lanat[:, k, :], ident[0:K1, 0:K1])
                mm.then_inc(w1_ps, 1)

            def step0(t, u, first=False, last=False):
                for b in range(2):
                    pe.wait_ge(a0.y_hi[b], t + 1)
                    pe.wait_ge(a0.y_lo[b], t + 1)
                over_y(smallp[:, 0:AR], arh, arl, slice(0, AR), True).then_inc(a0.small_ps, 1)
                pe.wait_ge(w1_in, 48 * t + 48)
                if not first:
                    pe.wait_ge(w1_lo, t)
                    pe.wait_ge(a0.z_out[0], t)
                over_y(z[0][:, :], w0h, w0l, slice(0, HALF), False)
                w1_pieces(t, u)
                if not first:
                    pe.wait_ge(a0.z_out[1], t)
                over_y(z[1][:, :], w0h, w0l, slice(HALF, L), False).then_inc(a0.base_done, 1)
                pe.wait_ge(a0.hx, 2 * t + 2)
                for b in range(2):
                    for k in range(4):
                        mm = T.transpose(hp[b][:, P * k:P * (k + 1)], hx[:, P * (4 * b + k):P * (4 * b + k + 1)],
                                         ident[:, :])
                    mm.then_inc(a0.hT_ps, 1)
                if not last:
                    conv(t + 1)
                for h in range(2):
                    w = slice(HALF * h, HALF * (h + 1))
                    for k in range(KC):
                        if h == 0 and k % 4 == 0:
                            pe.wait_ge(a0.hT_lo, 2 * t + k // 4 + 1)
                        mm = three(z[h][:, :], hTh[:, k, :], hTl[:, k, :], bh[:, k, w], bl[:, k, w], False,
                                   k == KC - 1, skip_group_check=True)
                    mm.then_inc(a0.z_ps[h], 1)

            step0(0, 0, first=True)
            step0(1, 1)
            with pe.Fori(1, TILES // 2 - 1) as i:
                step0(2 * i, 0)
                step0(2 * i + 1, 1)
            step0(TILES - 2, 0)
            step0(TILES - 1, 1, last=True)

            def mixing(t):
                pe.wait_ge(x1_hi, t + 1)
                pe.wait_ge(x1_lo, t + 1)
                pe.wait_ge(mix_lo, 2 * t + 2)
                for b in range(2):
                    for k in range(4):
                        w = slice(P * (4 * b + k), P * (4 * b + k + 1))
                        mm = three(yp[b][:, P * k:P * (k + 1)], x1h[:, w], x1l[:, w], mixh[:, :], mixl[:, :],
                                   True, True)
                    mm.then_inc(a1.y_ps[b], 1)

            mixing(0)
            pe.wait_ge(g_in, 32)

            def step1(t, last=False, first=False):
                for b in range(2):
                    pe.wait_ge(a1.y_hi[b], t + 1)
                    pe.wait_ge(a1.y_lo[b], t + 1)
                over_y(smallp[:, 0:GC], gh, gl, slice(0, GC), True).then_inc(a1.small_ps, 1)
                if first:
                    pe.wait_ge(w1h_in, 32)
                    pe.wait_ge(w1l_in, 16)
                    for h in range(2):
                        pe.wait_ge(a0.z_out[h], TILES)
                for h in range(2):
                    if not first:
                        pe.wait_ge(a1.z_out[h], t)
                    over_y(z[h][:, :], w1h, w1l, slice(HALF * h, HALF * (h + 1)), False)
                pe.wait_ge(a1.hx, 2 * t + 2)
                for k in range(2):
                    mm = T.transpose(hp[0][0:K1, P * k:P * (k + 1)], hx1[:, K1 * k:K1 * (k + 1)], ident[:, :])
                mm.then_inc(a1.hT_ps, 1)
                if not last:
                    mixing(t + 1)
                if first:
                    pe.wait_ge(lb_in, 32)
                pe.wait_ge(a1.hT_lo, t + 1)
                for h in range(2):
                    w = slice(HALF * h, HALF * (h + 1))
                    for k in range(2):
                        mm = three(z[h][:, :], h1h[:, k, :], h1l[:, k, :], lbh[:, k, w], lbl[:, k, w], False,
                                   k == 1, skip_group_check=True)
                    mm.then_inc(a1.z_ps[h], 1)

            step1(0, first=True)
            with pe.Fori(1, TILES - 1) as t:
                step1(t)
            step1(TILES - 1, last=True)


_INS = ['x', 'cond_128', 'fside_S_0', 'L0_cond_weight', 'L0_cond_c_weight', 'L0_ffn_base_w', 'L0_ffn_base_b',
        'L0_ffn_A', 'L0_ffn_B', 'L0_ffn_router_w', 'L1_cond_W0', 'L1_cond_b0', 'L1_cond_W1', 'L1_cond_b1',
        'L1_cond_W2', 'L1_cond_b2', 'L1_cond_weight', 'L1_cond_bias_k', 'L1_ffn_base_W', 'L1_ffn_gate_W',
        'L1_ffn_lora_A', 'L1_ffn_lora_B']


def kernel(**inputs):
    import numpy as _np
    import concourse.bacc as _bacc
    from concourse import mybir as _mybir
    from concourse.bass_utils import run_bass_kernel_spmd as _run

    nc = _bacc.Bacc("TRN2", target_bir_lowering=False, num_devices=1)
    arrays, args = {}, []
    for name in _INS:
        a = _np.ascontiguousarray(inputs[name])
        arrays[f"in_{name}_dram"] = a
        args.append(nc.dram_tensor(f"in_{name}_dram", a.shape, _mybir.dt.from_np(a.dtype), kind="ExternalInput").ap())
    args.append(nc.dram_tensor("out_0_dram", (NS, C, L), F32, kind="ExternalOutput").ap())
    build(nc, *args)
    r = _run(nc, [arrays], core_ids=[0])
    return r.results[0]["out_0_dram"]
```

```python
from contextlib import ExitStack

import concourse.bass as bass
from concourse import mybir

F32 = mybir.dt.float32
F32R = mybir.dt.float32r
U32 = mybir.dt.uint32
ALU = mybir.AluOpType
ACT = mybir.ActivationFunctionType
AX = mybir.AxisListType

P = 128
NS, C, L = 64, 64, 1024
TILES = NS * C // P
HALF = 512
GROUPS, CI, TAPS, PAD = 4, 16, 9, 4
BLK = 8
NB = L // BLK
NG = 2 * GROUPS
KC = L // P
E0, R0 = 16, 64
AR = R0 + E0
E1, R1 = 28, 8
ER1 = E1 * R1
K1 = ER1 // 2
GC = E1 + ER1
MIX = 8
EPS = 1e-6
SCALE0, SCALE1 = 32.0 / 64.0, 16.0 / 8.0
LO = BLK - 1
SLOTS = 3 * BLK - 1
ROUTE = 10
B0, B1 = 3 * P, HALF


def base_columns(b, width):
    return slice(min(b * width, L), min((b + 1) * width, L))


SM0, SM1 = L - 2 * B0, 0
W0B = (B0, B0, SM0 + AR)
W1B = (B1, B1, GC)
PREP_A = 3 * KC
PREP = PREP_A + 2 * KC


def build(nc, x, cond, side, conv_w, ctx_w, w0, bias0, loraA0, loraB0, router, cW0, cb0, cW1, cb1,
          cW2, cb2, mix_w, mix_b, w1, gate, loraA1, loraB1, out):
    ctx = ExitStack()
    with ctx:
        def sem(name):
            return ctx.enter_context(nc.semaphore(name))

        def sb(stack, name, shape, dt=F32):
            return stack.enter_context(nc.sbuf_tensor(name, shape, dt))

        bank = [ctx.enter_context(nc.psum_tensor(n, [P, HALF], F32))
                for n in ("z0", "z1", "z2", "c0", "c1", "t0", "t1", "prep")]
        z = bank[0:3]
        cp = bank[3:5]
        tp = bank[5:7]
        prepp = bank[7]

        def scratch(name, shape):
            return nc.dram_tensor(name, shape, F32, kind="Internal").ap()
        x1_dram = scratch("x1_dram", [TILES * P, L])
        att_dram = scratch("att_dram", [2, TILES, MIX])
        w1_dram = [scratch(f"w1_{s}", [L, L]) for s in ("hi", "lo")]
        g_dram = [scratch(f"g_{s}", [L, GC]) for s in ("hi", "lo")]
        lb_dram = [scratch(f"lb_{s}", [2, K1, L]) for s in ("hi", "lo")]

        ident = sb(ctx, "ident", [P, P])
        iota = sb(ctx, "iota", [P, 32])
        yh = sb(ctx, "yh", [P, KC, P], F32R)
        yl = sb(ctx, "yl", [P, KC, P], F32R)
        xin = [sb(ctx, f"xin{u}", [P, L]) for u in range(2)]
        xb = [sb(ctx, f"xb{u}", [P, L]) for u in range(2)]
        att = sb(ctx, "att", [NS, MIX])
        cbT = sb(ctx, "cbT", [P, TILES, GROUPS, 2])
        mbT = sb(ctx, "mbT", [P, TILES, 1])
        mixT = sb(ctx, "mixT", [P, MIX, C])
        attb = sb(ctx, "attb", [P, TILES, MIX])
        lg = sb(ctx, "lg", [P, 32])
        top8 = sb(ctx, "top8", [P, 8])
        idx = sb(ctx, "idx", [P, 8], U32)
        idxf = sb(ctx, "idxf", [P, 2])
        negm = sb(ctx, "negm", [P, 1])
        ex = sb(ctx, "ex", [P, 32])
        exsum = sb(ctx, "exsum", [P, 1])
        e12 = sb(ctx, "e12", [P, 2])
        e12sum = sb(ctx, "e12sum", [P, 1])
        den = sb(ctx, "den", [P, 1])
        rden = sb(ctx, "rden", [P, 1])
        w12 = sb(ctx, "w12", [P, 2])
        comb1 = sb(ctx, "comb1", [P, 32])
        comb2 = sb(ctx, "comb2", [P, 32])
        comb = sb(ctx, "comb", [P, 32])

        s0 = ExitStack()
        w0h, w0l = {}, {}
        for b in (2, 0, 1):
            w0h[b] = sb(s0, f"w0h{b}", [P, KC, W0B[b]], F32R)
            w0l[b] = sb(s0, f"w0l{b}", [P, KC, W0B[b]], F32R)
        pro = ExitStack()
        w0nat = sb(pro, "w0nat", [P, KC, L])
        arnat = sb(pro, "arnat", [AR, L])
        traw = sb(pro, "traw", [P, 2, BLK, C])
        taps = sb(pro, "taps", [CI, SLOTS, C])
        mixnat = sb(pro, "mixnat", [P, 4, 2, C])
        convnat = sb(pro, "convnat", [C, CI * TAPS])
        cnat = sb(pro, "cnat", [NS, P])
        ctxnat = sb(pro, "ctxnat", [C, P])
        condT = sb(pro, "condT", [P, NS])
        ctxT = sb(pro, "ctxT", [P, C])
        siderow = sb(pro, "siderow", [1, C])
        ones = sb(pro, "ones", [1, NS])
        ctxrep = sb(pro, "ctxrep", [P, GROUPS, BLK, CI])
        siderep = sb(pro, "siderep", [1, GROUPS, BLK, CI])
        cw = [sb(pro, f"cw{j}", [P, P]) for j in range(2)]
        cbias = [sb(pro, f"cbias{j}", [P, 1]) for j in range(2)]
        w2 = sb(pro, "w2", [P, MIX])
        b2b = sb(pro, "b2b", [NS, MIX])
        mixbias = sb(pro, "mixbias", [MIX, 2, C])
        hid = [sb(pro, f"hid{j}", [P, NS]) for j in range(2)]
        attT = sb(pro, "attT", [MIX, NS])
        astat = sb(pro, "astat", [NS, 4])
        pro.close()
        bh = sb(s0, "bh", [P, KC, L], F32R)
        bl = sb(s0, "bl", [P, KC, L], F32R)
        s0b = ExitStack()
        th = sb(s0b, "th", [P, 2, GROUPS, BLK, CI], F32R)
        tl = sb(s0b, "tl", [P, 2, GROUPS, BLK, CI], F32R)
        bias0b = sb(s0b, "bias0b", [P, L])
        xd = sb(s0b, "xd", [P, BLK, NB + 1])
        x8h = sb(s0b, "x8h", [P, NG, NB + 1], F32R)
        alias = ExitStack()
        x8 = sb(alias, "x8", [P, NG, NB + 1])
        alias.close()
        x8l = sb(s0b, "x8l", [P, NG, NB + 1], F32R)
        mid = sb(s0b, "mid", [P, L])
        bnat_stack = ExitStack()
        bnat = [sb(bnat_stack, f"bnat{j}", [P, 2, BLK, R0]) for j in range(2)]
        bnat_stack.close()
        hTh = sb(s0b, "hTh", [P, KC, P], F32R)
        hTl = sb(s0b, "hTl", [P, KC, P], F32R)
        w1nat = sb(s0b, "w1nat", [64, HALF])
        lbnat = sb(s0b, "lbnat", [64, E1, R1])
        gnat = sb(s0b, "gnat", [E1, 64])
        lanat = sb(s0b, "lanat", [K1, 2, 64])
        stage = [sb(s0b, f"stage_{s}", [P, 508], F32R) for s in ("hi", "lo")]
        s0b.close()

        s1b = ExitStack()
        x1h = sb(s1b, "x1h", [P, L], F32R)
        x1l = sb(s1b, "x1l", [P, L], F32R)
        mixh = sb(s1b, "mixh", [P, P], F32R)
        mixl = sb(s1b, "mixl", [P, P], F32R)
        mprod = sb(s1b, "mprod", [P, MIX, C])
        msum = sb(s1b, "msum", [P, C])
        mbrow = sb(s1b, "mbrow", [P, 1])
        hx1 = sb(s1b, "hx1", [P, ER1])
        mid1 = sb(s1b, "mid1", [P, L])
        h1h = sb(s1b, "h1h", [K1, 2, P], F32R)
        h1l = sb(s1b, "h1l", [K1, 2, P], F32R)
        s1b.close()
        s0.close()
        s1 = ExitStack()
        w1h, w1l = {}, {}
        for b in (2, 0, 1):
            w1h[b] = sb(s1, f"w1h{b}", [P, KC, W1B[b]], F32R)
            w1l[b] = sb(s1, f"w1l{b}", [P, KC, W1B[b]], F32R)
        lbh = sb(s1, "lbh", [K1, 2, L], F32R)
        lbl = sb(s1, "lbl", [K1, 2, L], F32R)
        s1.close()

        id_zero, id_ready, iota_ready = sem("id_zero"), sem("id_ready"), sem("iota_ready")
        pads_ready, taps_zero, ones_ready = sem("pads_ready"), sem("taps_zero"), sem("ones_ready")
        w0_in = [sem(f"w0_in{j}") for j in range(KC)]
        b_in = [sem(f"b_in{j}") for j in range(2)]
        b_ready = [sem(f"b_ready{j}") for j in range(2)]
        ar_in, c_in, ctxw_in, side_in = sem("ar_in"), sem("c_in"), sem("ctxw_in"), sem("side_in")
        mlp_in, mixw_in, conv_in, bias0_in = sem("mlp_in"), sem("mixw_in"), sem("conv_in"), sem("bias0_in")
        condT_ps, condT_sb, rep_ready, ctx_ps, cbT_ready = (sem(n) for n in ("condT_ps", "condT_sb", "rep_ready", "ctx_ps", "cbT_ready"))
        hid_ps, hid_ready = sem("hid_ps"), sem("hid_ready")
        att_ps, att_max, att_exp, att_ready, att_stored = (sem(n) for n in ("att_ps", "att_max", "att_exp", "att_ready", "att_stored"))
        attT_ps, attT_sb, mb_ps, mbT_ready = (sem(n) for n in ("attT_ps", "attT_sb", "mb_ps", "mbT_ready"))
        attb_in = sem("attb_in")
        taps_ps, taps_sb, traw_in, th_ready, tl_ready = (sem(n) for n in ("taps_ps", "taps_sb", "traw_in", "th_ready", "tl_ready"))
        mixT_ps, mixT_ready = sem("mixT_ps"), sem("mixT_ready")
        prep_ps, prep_hi, prep_lo = sem("prep_ps"), sem("prep_hi"), sem("prep_lo")

        x_in = [sem(f"x_in{u}") for u in range(2)]
        xd_ready, x8_in, x8_hi, x8_lo = (sem(n) for n in ("xd_ready", "x8_in", "x8_hi", "x8_lo"))
        xb_ready = sem("xb_ready")
        w1_in, w1_ps, w1_hi, w1_lo, w1_stored = (sem(n) for n in ("w1_in", "w1_ps", "w1_hi", "w1_lo", "w1_stored"))
        x1_stored = [sem(f"x1_stored{u}") for u in range(2)]

        class Layer:
            pass

        def layer(tag, banks):
            s = Layer()
            s.c_ps = [sem(f"{tag}_c_ps{b}") for b in range(2)]
            s.c_out = [sem(f"{tag}_c_out{b}") for b in range(2)]
            s.y_ps = [sem(f"{tag}_y_ps{b}") for b in range(2)]
            s.y_hi = [sem(f"{tag}_y_hi{b}") for b in range(2)]
            s.y_lo = [sem(f"{tag}_y_lo{b}") for b in range(2)]
            s.route = sem(f"{tag}_route")
            s.exp = sem(f"{tag}_exp")
            s.hx = sem(f"{tag}_hx")
            s.hT_ps = sem(f"{tag}_hT_ps")
            s.hT_hi = sem(f"{tag}_hT_hi")
            s.hT_lo = sem(f"{tag}_hT_lo")
            s.z_ps = [sem(f"{tag}_z_ps{h}") for h in range(banks)]
            s.z_out = [sem(f"{tag}_z_out{h}") for h in range(banks)]
            return s
        a0, a1 = layer("l0", 3), layer("l1", 2)
        small_done = sem("small_done")
        base_done = [sem(f"base_done{b}") for b in range(3)]
        x1_in = [sem(f"x1_in{u}") for u in range(2)]
        x1_hi, x1_lo = sem("x1_hi"), sem("x1_lo")
        mbrow_ready = sem("mbrow_ready")
        mprod_done, msum_done, mix_hi, mix_lo, mix_zero = (sem(n) for n in ("mprod_done", "msum_done", "mix_hi", "mix_lo", "mix_zero"))
        w1_back = [sem(f"w1_back{b}") for b in range(3)]
        lb_in = sem("lb_in")
        out_stored = [sem(f"out_stored{u}") for u in range(2)]

        x_t = x.rearrange("s c l -> (s c) l").rearrange("(t p) l -> t p l", p=P)
        out_t = out.rearrange("s c l -> (s c) l").rearrange("(t p) l -> t p l", p=P)
        x1_t = x1_dram.rearrange("(t p) l -> t p l", p=P)
        w1_t = w1.rearrange("(i o) (u l) -> u i o l", o=64, u=2)
        lb_t = loraB1.rearrange("e (i o) r -> i o e r", o=64)
        gate_t = gate.rearrange("e (i l) -> i e l", l=64)
        la_t = loraA1.rearrange("e r l -> (e r) l").rearrange("(k p) (i l) -> i p k l", k=2, l=64)
        w1_st = [d.rearrange("(u k p) (i o) -> u i p k o", u=2, p=P, o=64) for d in w1_dram]
        g_st = [d.rearrange("(i l) c -> i l c", l=64) for d in g_dram]
        lb_st = [d.rearrange("k p (i o) -> i p k o", o=64) for d in lb_dram]

        def row(ap, n):
            return ap.rearrange("(a n) -> a n", a=1).to_broadcast([n, ap.shape[0]])

        def pbank(q):
            return (tp[0], tp[1], cp[0], cp[1])[q % 4]

        def prep_places(w, b):
            for q in range(PREP_A):
                n, k = divmod(q, KC)
                yield w[n][:, k, :], pbank(q)[:, 0:W0B[n]]
            for q in range(PREP_A, PREP):
                k, hj = divmod(q - PREP_A, 2)
                yield (b[:, k, :].rearrange("q (p j) -> q j p", j=BLK)[:, 4 * hj:4 * hj + 4, :],
                       pbank(q)[:, :].rearrange("q (j p) -> q j p", p=P))

        def b_turn(k):
            return xb[k % 2][:, :].rearrange("p (j e r) -> p j e r", j=BLK, e=2)

        def y_places(s, y, b):
            if s is a0:
                return (y[:, :, C * b:C * (b + 1)].rearrange("p j (g c) -> p g j c", c=CI),
                        tp[b][:, :].rearrange("p (g j c) -> p g j c", g=GROUPS, c=CI))
            return y[:, 4 * b:4 * b + 4, :], tp[b][:, :].rearrange("p (k r) -> p k r", r=P)

        block = ctx.enter_context(nc.Block())

        @block.sync
        def _(sp):
            def load_x(i, u):
                sp.dma_start(xin[u][:, :], x_t[2 * i + u]).then_inc(x_in[u], 16)

            def spread_x(t, first=False):
                sp.wait_ge(xd_ready, t + 1)
                if not first:
                    sp.wait_ge(a0.c_ps[1], t)
                for n in range(NG):
                    sp.dma_start(x8[:, n, :], xd[CI * n:CI * (n + 1), :, :]).then_inc(x8_in, 16)

            def load_w1(i, u):
                sp.dma_start(w1nat[:, :], w1_t[u, i]).then_inc(w1_in, 16)
                if u == 0:
                    with nc.allow_non_contiguous_dma(reason="rank-8 rows"):
                        sp.dma_start(lbnat[:, :, :], lb_t[i]).then_inc(w1_in, 32)
                else:
                    sp.dma_start(gnat[:, :], gate_t[i]).then_inc(w1_in, 16)
                    sp.dma_start(lanat[:, :, :], la_t[i]).then_inc(w1_in, 16)

            def store_w1(i, u, t):
                for s, done in ((0, w1_hi), (1, w1_lo)):
                    sp.wait_ge(done, t + 1)
                    src = stage[s][:, :].bitcast(F32)
                    sp.dma_start(w1_st[s][u, i], src[:, 0:256].rearrange("p (k o) -> p k o", o=64))\
                      .then_inc(w1_stored, 16)
                    if u == 0:
                        sp.dma_start(lb_st[s][i], src[0:K1, 256:384].rearrange("p (k o) -> p k o", o=64))\
                          .then_inc(w1_stored, 16)
                    else:
                        sp.dma_start(g_st[s][i], src[0:64, 256:256 + GC]).then_inc(w1_stored, 16)

            def store_x1(i, u):
                for b in range(3):
                    sp.wait_ge(a0.z_out[b], 2 * i + u + 1)
                sp.dma_start(x1_t[2 * i + u], xb[u][:, :]).then_inc(x1_stored[u], 16)

            load_x(0, 0)
            for j in range(KC):
                sp.dma_start(w0nat[:, j, :], w0[P * j:P * (j + 1), :]).then_inc(w0_in[j], 16)
            sp.wait_ge(taps_sb, 2)
            tv = taps[:, :, :]
            for w in range(2):
                sp.dma_start(traw[:, w, :, :].rearrange("p j c -> p (j c)"),
                             bass.AP(tv.tensor, tv.offset + BLK * w * C, [list(tv.ap[0]), [C, BLK], [1, BLK * C]]))\
                  .then_inc(traw_in, 16)
            spread_x(0, first=True)
            for j, (w, b) in enumerate(((cW0, cb0), (cW1, cb1))):
                sp.dma_start(cw[j][:, :], w).then_inc(mlp_in, 16)
                sp.dma_start(cbias[j][:, :], b.rearrange("(n a) -> n a", a=1)).then_inc(mlp_in, 16)
            sp.dma_start(w2[:, :], cW2).then_inc(mlp_in, 16)
            sp.dma_start(b2b[:, :], row(cb2, NS)).then_inc(mlp_in, 16)
            for s in range(2):
                sp.dma_start(mixbias[:, s, :], mix_b).then_inc(mlp_in, 16)
            mixw_v = mix_w.rearrange("k o i a -> (k o) (i a)").rearrange("(j p) i -> p j i", p=P)
            for s in range(2):
                sp.dma_start(mixnat[:, :, s, :], mixw_v).then_inc(mixw_in, 16)
            for j in range(KC):
                if j >= 2:
                    sp.wait_ge(b_ready[j % 2], j // 2)
                sp.dma_start(bnat[j % 2][:, :, :, :],
                             loraB0[2 * j:2 * j + 2].rearrange("e (p j) r -> p e j r", j=BLK)).then_inc(b_in[j % 2], 16)
                if j == 1:
                    sp.dma_start(bias0b[:, :], row(bias0, P)).then_inc(bias0_in, 16)
                    load_x(0, 1)
                    load_w1(0, 0)
            sp.wait_ge(att_ready, 1)
            sp.dma_start(att_dram.rearrange("s t k -> t s k"), att[:, :]).then_inc(att_stored, 16)
            sp.wait_ge(att_stored, 16)
            for s in range(2):
                sp.dma_start(attb[64 * s:64 * (s + 1), :, :].rearrange("p t k -> p (t k)"),
                             row(att_dram[s].rearrange("t k -> (t k)"), 64)).then_inc(attb_in, 16)

            def step0(i, u, first=False, prefetch=True):
                t = 2 * i + u
                if first:
                    spread_x(1)
                if prefetch:
                    sp.wait_ge(xd_ready, t + 1)
                    sp.wait_ge(xb_ready, t + 1)
                    load_x(i + 1, u)
                if not first:
                    spread_x(t + 1)
                sp.wait_ge(w1_ps, t + 1)
                load_w1(i + u, 1 - u)
                store_w1(i, u, t)
                store_x1(i, u)

            step0(0, 0, first=True)
            step0(0, 1)
            with sp.Fori(1, TILES // 2 - 1) as i:
                step0(i, 0)
                step0(i, 1)
            step0(TILES // 2 - 1, 0, prefetch=False)
            n = TILES // 2 - 1

            def load_x1(i, u):
                sp.dma_start(xin[u][:, :], x1_t[2 * i + u]).then_inc(x1_in[u], 16)

            sp.wait_ge(xb_ready, TILES)
            sp.wait_ge(xd_ready, TILES)
            for u in range(2):
                sp.wait_ge(x1_stored[u], 16)
                load_x1(0, u)
            sp.wait_ge(w1_ps, TILES)
            store_w1(n, 1, TILES - 1)
            sp.wait_ge(w1_stored, 64 * TILES)

            def load_back(b, s):
                src = g_dram[s] if b == 2 else w1_dram[s][:, base_columns(b, B1)]
                sp.dma_start((w1h, w1l)[s][b][:, :, :].bitcast(F32), src.rearrange("(k p) c -> p k c", p=P))\
                  .then_inc(w1_back[b], 16)

            sp.wait_ge(base_done[2], TILES)
            load_back(2, 0)
            load_back(2, 1)
            sp.wait_ge(base_done[0], TILES)
            load_back(0, 0)
            sp.wait_ge(base_done[1], TILES)
            load_back(0, 1)
            load_back(1, 0)
            sp.wait_ge(a0.z_ps[1], TILES)
            load_back(1, 1)
            for dst, d in ((lbh, lb_dram[0]), (lbl, lb_dram[1])):
                sp.dma_start(dst[:, :, :].bitcast(F32), d.rearrange("k p o -> p k o")).then_inc(lb_in, 16)
            store_x1(n, 1)
            for u in range(2):
                sp.wait_ge(x1_stored[u], 16 * (TILES // 2))

            def step1(i, u, prefetch=True):
                t = 2 * i + u
                for b in range(2):
                    sp.wait_ge(a1.z_out[b], t + 1)
                if prefetch:
                    load_x1(i + 1, u)
                sp.dma_start(out_t[t], xb[u][:, :]).then_inc(out_stored[u], 16)

            with sp.Fori(0, TILES // 2 - 1) as i:
                step1(i, 0)
                step1(i, 1)
            step1(n, 0, prefetch=False)
            step1(n, 1, prefetch=False)
            for u in range(2):
                sp.wait_ge(out_stored[u], 16 * (TILES // 2))
                sp.wait_ge(x1_stored[u], 16 * (TILES // 2))

        @block.gpsimd
        def _(pool):
            nc.gpsimd.memset(ones[:, :], 1.0).then_inc(ones_ready, 1)
            nc.gpsimd.memset(ident[:, :], 0.0).then_inc(id_zero, 1)
            pool.wait_ge(id_zero, 1)
            nc.gpsimd.affine_select(out=ident[:, :], in_=ident[:, :], compare_op=ALU.not_equal, fill=1.0,
                                    base=0, pattern=[[-1, P]], channel_multiplier=1).then_inc(id_ready, 1)
            nc.gpsimd.memset(taps[:, :, :], 0.0).then_inc(taps_zero, 1)
            nc.gpsimd.iota(iota[:, :], pattern=[[1, 32]], base=0, channel_multiplier=0,
                           allow_small_or_imprecise_dtypes=True).then_inc(iota_ready, 1)
            nc.gpsimd.memset(xd[:, 0:PAD, 0:1], 0.0).then_inc(pads_ready, 1)
            nc.gpsimd.memset(xd[:, PAD:BLK, NB:NB + 1], 0.0).then_inc(pads_ready, 1)
            for w in range(2):
                pool.wait_ge(th_ready, w + 1)
                nc.gpsimd.tensor_tensor(tl[:, w, :, :, :], traw[:, w, :, :].rearrange("p j (g c) -> p g j c", c=CI),
                                        th[:, w, :, :, :], ALU.subtract).then_inc(tl_ready, 1)
            for k in range(0, KC, 2):
                pool.wait_ge(b_in[0], 16 * (k // 2 + 1))
                if k >= 2:
                    pool.wait_ge(prep_ps, PREP_A + 2 * (k - 1))
                nc.gpsimd.tensor_copy(b_turn(k).rearrange("p j e r -> p e j r"), bnat[0][:, :, :, :])\
                  .then_inc(b_ready[0], 1)
            pool.wait_ge(bias0_in, 16)
            pool.wait_ge(prep_ps, PREP)

            def residual(i, u, first=False):
                pool.wait_ge(x_in[u], 16 * (i + 1))
                if not first:
                    pool.wait_ge(x1_stored[u], 16 * i)
                nc.gpsimd.tensor_tensor(xb[u][:, :], xin[u][:, :], bias0b[:, :], ALU.add).then_inc(xb_ready, 1)

            residual(0, 0, first=True)
            residual(0, 1, first=True)
            with pool.Fori(1, TILES // 2) as i:
                residual(i, 0)
                residual(i, 1)

        @block.scalar
        def _(act):
            def copy(o, i_):
                return nc.scalar.activation(o, i_, ACT.Copy)

            act.dma_start(convnat[:, :], conv_w.rearrange("o c k -> o (c k)")).then_inc(conv_in, 16)
            act.dma_start(cnat[:, :], cond).then_inc(c_in, 16)
            act.dma_start(ctxnat[:, :], ctx_w).then_inc(ctxw_in, 16)
            act.dma_start(siderow[:, :], row(side, 1)).then_inc(side_in, 16)
            act.dma_start(arnat[0:R0, :], loraA0).then_inc(ar_in, 16)
            act.dma_start(arnat[R0:AR, :], router).then_inc(ar_in, 16)

            def blocks(i, u):
                act.wait_ge(x_in[u], 16 * i + 16)
                v = xin[u][:, :].rearrange("p (m j) -> p j m", j=BLK)
                copy(xd[:, PAD:BLK, 0:NB], v[:, 0:PAD, :])
                copy(xd[:, 0:PAD, 1:NB + 1], v[:, PAD:BLK, :]).then_inc(xd_ready, 1)

            def x8_high(t):
                act.wait_ge(x8_in, 128 * t + 128)
                copy(x8h[:, :, :], x8[:, :, :]).then_inc(x8_hi, 1)

            def y_high(s, t, b):
                act.wait_ge(s.y_ps[b], t + 1)
                copy(*y_places(s, yh, b)).then_inc(s.y_hi[b], 1)

            def exps(s, t):
                act.wait_ge(s.route, ROUTE * t + 3)
                if s is a0:
                    nc.scalar.activation(ex[:, 0:E0], lg[:, 0:E0], ACT.Exp, bias=negm[:, :],
                                         accum_out=exsum[:, :]).then_inc(s.exp, 1)
                else:
                    copy(ex[:, 0:1], negm[:, :]).then_inc(s.exp, 1)
                nc.scalar.activation(e12[:, :], top8[:, 0:2], ACT.Exp, bias=negm[:, :],
                                     accum_out=e12sum[:, :]).then_inc(s.exp, 1)

            high = list(prep_places(w0h, bh))

            def prep_high(first, end):
                for q in range(first, end):
                    act.wait_ge(prep_ps, q + 1)
                    copy(*high[q]).then_inc(prep_hi, 1)

            def hidden(j):
                act.wait_ge(hid_ps, j + 1)
                nc.scalar.activation(hid[j][:, :], z[0][:, NS * j:NS * (j + 1)], ACT.Gelu,
                                     bias=cbias[j][:, :]).then_inc(hid_ready, 1)

            act.wait_ge(taps_zero, 1)
            act.wait_ge(taps_ps, 1)
            copy(taps[:, LO:LO + 8, :], z[0][0:CI, :].rearrange("p (k o) -> p k o", o=C)).then_inc(taps_sb, 1)
            copy(taps[:, LO + 8, :], z[1][0:CI, 0:C]).then_inc(taps_sb, 1)
            act.wait_ge(pads_ready, 2)
            blocks(0, 0)
            prep_high(0, 2)
            act.wait_ge(traw_in, 16 * 2)
            for w in range(2):
                copy(th[:, w, :, :, :], traw[:, w, :, :].rearrange("p j (g c) -> p g j c", c=CI)).then_inc(th_ready, 1)
            prep_high(2, 8)
            act.wait_ge(condT_ps, 2)
            copy(condT[:, :], prepp[:, 0:NS]).then_inc(condT_sb, 1)
            copy(ctxrep[:, :, :, :], prepp[:, NS:NS + C].rearrange("p (g c) -> p g c", c=CI).unsqueeze(2)
                 .to_broadcast([P, GROUPS, BLK, CI])).then_inc(rep_ready, 1)
            act.wait_ge(side_in, 16)
            copy(siderep[:, :, :, :], siderow[:, :].rearrange("p (g c) -> p g c", c=CI).unsqueeze(2)
                 .to_broadcast([1, GROUPS, BLK, CI])).then_inc(rep_ready, 1)
            prep_high(8, 12)
            x8_high(0)
            prep_high(12, 16)
            act.wait_ge(mlp_in, 16 * 8)
            hidden(0)
            prep_high(16, 18)
            hidden(1)
            act.wait_ge(mixT_ps, 1)
            copy(mixT[:, :, :], z[1][:, :].rearrange("p (k o) -> p k o", o=C)).then_inc(mixT_ready, 1)
            prep_high(18, PREP_A)
            act.wait_ge(att_max, 3)
            nc.scalar.activation(att[:, :], lg[0:NS, 0:MIX], ACT.Exp, bias=astat[:, 1:2],
                                 accum_out=astat[:, 2:3]).then_inc(att_exp, 1)

            def regroup(k):
                act.wait_ge(b_in[1], 16 * (k // 2 + 1))
                if k >= 2:
                    act.wait_ge(prep_ps, PREP_A + 2 * (k - 1))
                copy(b_turn(k).rearrange("p j e r -> p e j r"), bnat[1][:, :, :, :]).then_inc(b_ready[1], 1)

            regroup(1)
            y_high(a0, 0, 0)
            y_high(a0, 0, 1)

            def x1_high(i, u):
                act.wait_ge(x1_in[u], 16 * i + 16)
                copy(x1h[:, :], xin[u][:, :]).then_inc(x1_hi, 1)

            def mix_high(t):
                act.wait_ge(msum_done, t + 1)
                for s in range(2):
                    q = slice(64 * s, 64 * (s + 1))
                    copy(mixh[q, q], msum[q, :]).then_inc(mix_hi, 1)

            def mixed_out(t):
                for b in range(2):
                    act.wait_ge(a1.c_ps[b], t + 1)
                    act.wait_ge(mbrow_ready, t + 1)
                    nc.scalar.activation(mid1[:, HALF * b:HALF * (b + 1)], cp[b][:, :], ACT.Identity,
                                         bias=mbrow[:, :]).then_inc(a1.c_out[b], 1)

            def step0(i, u, first=False, last=False):
                t = 2 * i + u
                if not last:
                    act.wait_ge(x8_in, 128 * t + 128)
                    blocks(i + u, 1 - u)
                else:
                    act.wait_ge(a0.c_ps[1], TILES)
                    act.wait_ge(mix_zero, 2)
                    mix_high(0)
                    x1_high(0, 0)
                if first:
                    for k in range(KC):
                        prep_high(PREP_A + 2 * k, PREP_A + 2 * k + 2)
                        if k % 2 and k + 2 < KC:
                            regroup(k + 2)
                exps(a0, t)
                if not last:
                    act.wait_ge(a0.c_ps[1], t + 1)
                    x8_high(t + 1)
                if not first:
                    act.wait_ge(w1_stored, 64 * t)
                act.wait_ge(w1_ps, t + 1)
                copy(stage[0][:, 0:256], prepp[:, 0:256])
                if u == 0:
                    copy(stage[0][0:K1, 256:384], prepp[0:K1, 256:384]).then_inc(w1_hi, 1)
                else:
                    copy(stage[0][0:64, 256:256 + GC], prepp[0:64, 256:256 + GC]).then_inc(w1_hi, 1)
                for b in range(2):
                    act.wait_ge(a0.hT_ps, 2 * t + b + 1)
                    copy(hTh[:, 4 * b:4 * b + 4, :], tp[b][:, :].rearrange("p (k r) -> p k r", r=P))\
                        .then_inc(a0.hT_hi, 1)
                if not last:
                    y_high(a0, t + 1, 0)
                    y_high(a0, t + 1, 1)
                else:
                    mixed_out(0)
                    y_high(a1, 0, 0)
                    y_high(a1, 0, 1)

            step0(0, 0, first=True)
            step0(0, 1)
            with act.Fori(1, TILES // 2 - 1) as i:
                step0(i, 0)
                step0(i, 1)
            step0(TILES // 2 - 1, 0)
            step0(TILES // 2 - 1, 1, last=True)

            def step1(i, u, last=False):
                t = 2 * i + u
                if not last:
                    act.wait_ge(a1.c_ps[1], t + 1)
                    mix_high(t + 1)
                exps(a1, t)
                if not last:
                    x1_high(i + u, 1 - u)
                    mixed_out(t + 1)
                act.wait_ge(a1.hT_ps, t + 1)
                copy(h1h[:, :, :], prepp[0:K1, 0:2 * P].rearrange("p (k r) -> p k r", r=P)).then_inc(a1.hT_hi, 1)
                if not last:
                    y_high(a1, t + 1, 0)
                    y_high(a1, t + 1, 1)

            with act.Fori(0, TILES // 2 - 1) as i:
                step1(i, 0)
                step1(i, 1)
            step1(TILES // 2 - 1, 0)
            step1(TILES // 2 - 1, 1, last=True)

        @block.vector
        def _(dve):
            V = nc.vector

            def x8_low(t):
                dve.wait_ge(x8_hi, t + 1)
                V.tensor_tensor(x8l[:, :, :], x8[:, :, :], x8h[:, :, :], ALU.subtract).then_inc(x8_lo, 1)

            def conv_out(t):
                for b in range(2):
                    dve.wait_ge(a0.c_ps[b], t + 1)
                    v = [a[:, :].rearrange("p (g s m) -> p g s m", g=2, s=2)
                         for a in (mid[:, HALF * b:HALF * (b + 1)], cp[b])]
                    V.tensor_tensor(v[0], v[1], cbT[:, t, 2 * b:2 * b + 2, :].unsqueeze(3)
                                    .to_broadcast([P, 2, 2, NB]), ALU.add).then_inc(a0.c_out[b], 1)

            def y_low(s, t):
                for b in range(2):
                    dve.wait_ge(s.y_hi[b], t + 1)
                    o, v = y_places(s, yl, b)
                    V.tensor_tensor(o, v, y_places(s, yh, b)[0], ALU.subtract).then_inc(s.y_lo[b], 1)

            def routing(s, t, projected, first, experts, scale):
                r = s.route

                def after(k):
                    dve.wait_ge(r, ROUTE * t + k)
                dve.wait_ge(projected, t + 1)
                V.tensor_copy(lg[:, 0:experts], z[2][:, first:first + experts]).then_inc(r, 1)
                V.max(top8[:, :], z[2][:, first:first + experts]).then_inc(r, 1)
                after(2)
                V.tensor_scalar(negm[:, :], top8[:, 0:1], -1.0, None, ALU.mult).then_inc(r, 1)
                V.max_index(idx[:, :], top8[:, :], lg[:, 0:experts]).then_inc(r, 1)
                after(4)
                V.tensor_copy(idxf[:, :], idx[:, 0:2]).then_inc(r, 1)
                dve.wait_ge(s.exp, 2 * t + 2)
                if s is a0:
                    V.tensor_scalar(den[:, :], exsum[:, :], EPS, e12sum[:, :], ALU.mult, ALU.add).then_inc(r, 1)
                else:
                    V.tensor_copy(den[:, :], e12sum[:, :]).then_inc(r, 1)
                after(6)
                V.reciprocal(rden[:, :], den[:, :]).then_inc(r, 1)
                after(7)
                V.tensor_scalar(w12[:, :], e12[:, :], rden[:, :], scale, ALU.mult, ALU.mult).then_inc(r, 1)
                after(8)
                V.tensor_scalar(comb1[:, 0:experts], iota[:, 0:experts], idxf[:, 0:1], w12[:, 0:1],
                                ALU.is_equal, ALU.mult).then_inc(r, 1)
                V.tensor_scalar(comb2[:, 0:experts], iota[:, 0:experts], idxf[:, 1:2], w12[:, 1:2],
                                ALU.is_equal, ALU.mult).then_inc(r, 1)
                after(10)

            def spread0(t):
                routing(a0, t, base_done[2], SM0 + R0, E0, SCALE0)
                V.tensor_tensor(comb[:, 0:E0], comb1[:, 0:E0], comb2[:, 0:E0], ALU.add).then_inc(a0.hx, 1)
                dve.wait_ge(a0.hx, 2 * t + 1)
                V.tensor_tensor(mid[:, :].rearrange("p (e r) -> p e r", r=R0),
                                z[2][:, SM0:SM0 + R0].unsqueeze(1).to_broadcast([P, E0, R0]),
                                comb[:, 0:E0].unsqueeze(2).to_broadcast([P, E0, R0]), ALU.mult).then_inc(a0.hx, 1)

            def spread1(t):
                routing(a1, t, small_done, SM1, E1, SCALE1)
                V.tensor_tensor(comb[:, 0:E1], comb1[:, 0:E1], comb2[:, 0:E1], ALU.add).then_inc(a1.hx, 1)
                dve.wait_ge(a1.hx, 2 * t + 1)
                V.tensor_tensor(hx1[:, :].rearrange("p (e r) -> p e r", r=R1),
                                z[2][:, SM1 + E1:SM1 + GC].rearrange("p (e r) -> p e r", r=R1),
                                comb[:, 0:E1].unsqueeze(2).to_broadcast([P, E1, R1]), ALU.mult).then_inc(a1.hx, 1)

            high, low = list(prep_places(w0h, bh)), list(prep_places(w0l, bl))

            def prep_low(first, end):
                for q in range(first, end):
                    dve.wait_ge(prep_hi, q + 1)
                    V.tensor_tensor(low[q][0], low[q][1], high[q][0], ALU.subtract).then_inc(prep_lo, 1)

            prep_low(0, 12)
            x8_low(0)
            prep_low(12, 16)
            dve.wait_ge(ctx_ps, 1)
            V.tensor_copy(cbT[:, :, :, :].rearrange("p t g s -> p g t s"),
                          z[2][:, 0:GROUPS * NS].rearrange("p (g t s) -> p g t s", g=GROUPS, s=2)).then_inc(cbT_ready, 1)
            prep_low(16, 20)
            dve.wait_ge(mlp_in, 16 * 8)
            dve.wait_ge(att_ps, 1)
            V.tensor_tensor(lg[0:NS, 0:MIX], prepp[0:NS, 256:256 + MIX], b2b[:, :], ALU.add).then_inc(att_max, 1)
            dve.wait_ge(att_max, 1)
            V.tensor_reduce(astat[:, 0:1], lg[0:NS, 0:MIX], AX.X, ALU.max).then_inc(att_max, 1)
            dve.wait_ge(att_max, 2)
            V.tensor_scalar(astat[:, 1:2], astat[:, 0:1], -1.0, None, ALU.mult).then_inc(att_max, 1)
            prep_low(20, PREP_A)
            conv_out(0)
            dve.wait_ge(att_exp, 1)
            V.reciprocal(astat[:, 3:4], astat[:, 2:3]).then_inc(att_max, 1)
            dve.wait_ge(att_max, 4)
            V.tensor_scalar(att[:, :], att[:, :], astat[:, 3:4], None, ALU.mult).then_inc(att_ready, 1)
            y_low(a0, 0)
            dve.wait_ge(attT_ps, 1)
            V.tensor_copy(attT[:, :], prepp[0:MIX, 320:320 + NS]).then_inc(attT_sb, 1)
            dve.wait_ge(mb_ps, 1)
            mv = prepp[:, 384:384 + NS].rearrange("p (t s) -> p t s", s=2)
            for s in range(2):
                q = slice(64 * s, 64 * (s + 1))
                V.tensor_copy(mbT[q, :, 0], mv[q, :, s]).then_inc(mbT_ready, 1)
            dve.wait_ge(iota_ready, 1)

            def x1_low(u, t):
                dve.wait_ge(x1_hi, t + 1)
                V.tensor_tensor(x1l[:, :], xin[u][:, :], x1h[:, :], ALU.subtract).then_inc(x1_lo, 1)

            def mix(t):
                V.tensor_copy(mbrow[:, :], mbT[:, t, :]).then_inc(mbrow_ready, 1)
                V.tensor_tensor(mprod[:, :, :], mixT[:, :, :],
                                attb[:, t, :].unsqueeze(2).to_broadcast([P, MIX, C]), ALU.mult).then_inc(mprod_done, 1)
                dve.wait_ge(mprod_done, t + 1)
                V.tensor_reduce(msum[:, :], mprod[:, :, :].rearrange("p k o -> p o k"), AX.X, ALU.add)\
                    .then_inc(msum_done, 1)
                dve.wait_ge(mix_hi, 2 * t + 2)
                for s in range(2):
                    q = slice(64 * s, 64 * (s + 1))
                    V.tensor_tensor(mixl[q, q], msum[q, :], mixh[q, q], ALU.subtract).then_inc(mix_lo, 1)

            def step0(i, u, first=False, last=False):
                t = 2 * i + u
                if first:
                    prep_low(PREP_A, PREP)
                if last:
                    dve.wait_ge(a0.c_ps[1], TILES)
                    dve.wait_ge(xb_ready, TILES)
                    dve.wait_ge(mixT_ready, 1)
                    dve.wait_ge(attb_in, 32)
                    dve.wait_ge(mbT_ready, 2)
                    for m in (mixh, mixl):
                        V.memset(m[:, :].bitcast(U32), 0).then_inc(mix_zero, 1)
                    dve.wait_ge(mix_zero, 2)
                    mix(0)
                    x1_low(0, 0)
                spread0(t)
                if not last:
                    x8_low(t + 1)
                dve.wait_ge(w1_hi, t + 1)
                V.tensor_tensor(stage[1][:, 0:256], prepp[:, 0:256], stage[0][:, 0:256], ALU.subtract)
                if u == 0:
                    q, w = slice(0, K1), slice(256, 384)
                else:
                    q, w = slice(0, 64), slice(256, 256 + GC)
                V.tensor_tensor(stage[1][q, w], prepp[q, w], stage[0][q, w], ALU.subtract).then_inc(w1_lo, 1)
                for b in range(2):
                    dve.wait_ge(a0.hT_hi, 2 * t + b + 1)
                    V.tensor_tensor(hTl[:, 4 * b:4 * b + 4, :], tp[b][:, :].rearrange("p (k r) -> p k r", r=P),
                                    hTh[:, 4 * b:4 * b + 4, :], ALU.subtract).then_inc(a0.hT_lo, 1)
                if not last:
                    conv_out(t + 1)
                dve.wait_ge(xb_ready, t + 1)

                def residual(b):
                    dve.wait_ge(a0.z_ps[b], t + 1)
                    w = base_columns(b, B0)
                    o = xb[u][:, w]
                    V.tensor_tensor(o, z[b][:, 0:w.stop - w.start], o, ALU.add).then_inc(a0.z_out[b], 1)

                residual(2)
                if last:
                    y_low(a1, 0)
                else:
                    y_low(a0, t + 1)
                residual(0)
                residual(1)

            step0(0, 0, first=True)
            step0(0, 1)
            with dve.Fori(1, TILES // 2 - 1) as i:
                step0(i, 0)
                step0(i, 1)
            step0(TILES // 2 - 1, 0)
            step0(TILES // 2 - 1, 1, last=True)

            def step1(i, u, first=False, last=False):
                t = 2 * i + u
                if not last:
                    dve.wait_ge(a1.c_out[1], t + 1)
                    mix(t + 1)
                spread1(t)
                if not last:
                    x1_low(1 - u, t + 1)
                dve.wait_ge(a1.hT_hi, t + 1)
                V.tensor_tensor(h1l[:, :, :], prepp[0:K1, 0:2 * P].rearrange("p (k r) -> p k r", r=P),
                                h1h[:, :, :], ALU.subtract).then_inc(a1.hT_lo, 1)
                if not last:
                    y_low(a1, t + 1)
                dve.wait_ge(x1_stored[u], 16 * (TILES // 2))
                if not first:
                    dve.wait_ge(out_stored[u], 16 * i)
                for b in range(2):
                    dve.wait_ge(a1.z_ps[b], t + 1)
                    w = base_columns(b, B1)
                    V.tensor_tensor(xb[u][:, w], z[b][:, 0:w.stop - w.start], xin[u][:, w], ALU.add)\
                        .then_inc(a1.z_out[b], 1)

            step1(0, 0, first=True)
            step1(0, 1, first=True)
            with dve.Fori(1, TILES // 2 - 1) as i:
                step1(i, 0)
                step1(i, 1)
            step1(TILES // 2 - 1, 0)
            step1(TILES // 2 - 1, 1, last=True)

        @block.tensor
        def _(pe):
            T = nc.tensor

            def three(o, ah, al, wh, wl, start, stop, **kw):
                T.matmul(o, ah, wh, start=start, stop=False, **kw)
                T.matmul(o, al, wh, start=False, stop=False, **kw)
                return T.matmul(o, ah, wl, start=False, stop=stop, **kw)

            def over_y(b, wh, wl):
                for k in range(KC):
                    mm = three(z[b][:, 0:wh[b].shape[2]], yh[:, k, :], yl[:, k, :], wh[b][:, k, :], wl[b][:, k, :],
                               k == 0, False, skip_group_check=True)
                return mm

            def over_h(s, b, width, hh, hl, wh, wl):
                w = base_columns(b, width)
                for k in range(hh.shape[1]):
                    mm = three(z[b][:, 0:w.stop - w.start], hh[:, k, :], hl[:, k, :], wh[:, k, w], wl[:, k, w],
                               False, k == hh.shape[1] - 1, skip_group_check=True)
                mm.then_inc(s.z_ps[b], 1)

            def conv(t):
                pe.wait_ge(x8_hi, t + 1)
                pe.wait_ge(x8_lo, t + 1)
                for b in range(2):
                    for g in (2 * b, 2 * b + 1):
                        o = cp[b][:, 2 * NB * (g % 2):2 * NB * (g % 2 + 1)].rearrange("p (s m) -> p s m", s=2)
                        for w in range(2):
                            ah, al = (a[:, w, g, :, :].rearrange("p j c -> p (j c)") for a in (th, tl))
                            vh, vl = (a[:, g:g + GROUPS + 1:GROUPS, w:w + NB] for a in (x8h, x8l))
                            mm = three(o, ah, al, vh, vl, w == 0, w == 1)
                    mm.then_inc(a0.c_ps[b], 1)

            def turn_conv(t):
                for b in range(2):
                    pe.wait_ge(a0.c_out[b], t + 1)
                for n in range(2):
                    for g in range(GROUPS):
                        mm = T.transpose(tp[n][:, P * g:P * (g + 1)], mid[:, NB * (2 * g + n):NB * (2 * g + n + 1)],
                                         ident[:, :])
                    mm.then_inc(a0.y_ps[n], 1)

            pe.wait_ge(id_ready, 1)
            pe.wait_ge(conv_in, 16)
            cv = convnat[:, :].rearrange("o (c k) -> o k c", k=TAPS)
            for k in range(TAPS):
                o = z[k // 8][0:CI, C * (k % 8):C * (k % 8) + C]
                mm = T.transpose(o, cv[:, k, :], ident[0:C, 0:C])
            mm.then_inc(taps_ps, 1)
            wv = w0nat[:, :, :].rearrange("p n (b j) -> p n j b", j=BLK)
            av = arnat[:, :].rearrange("a (b j) -> a j b", j=BLK)

            def turn_w0(first, end):
                for q in range(first, end):
                    b, k = divmod(q, KC)
                    if q >= 4:
                        pe.wait_ge(prep_lo, q - 3)
                    w = base_columns(b, B0)
                    for n in range(w.start // P, w.stop // P):
                        if k == 0:
                            pe.wait_ge(w0_in[n], 16)
                        c0 = P * n - w.start
                        mm = T.transpose(pbank(q)[:, c0:c0 + P], wv[:, n, BLK - 1 - k, :], ident[:, :])
                    if b == 2:
                        if k == 0:
                            pe.wait_ge(ar_in, 32)
                        mm = T.transpose(pbank(q)[:, SM0:SM0 + AR], av[:, BLK - 1 - k, :], ident[0:AR, 0:AR])
                    mm.then_inc(prep_ps, 1)

            turn_w0(0, 8)
            pe.wait_ge(c_in, 16)
            T.transpose(prepp[:, 0:NS], cnat[:, :], ident[0:NS, 0:NS]).then_inc(condT_ps, 1)
            pe.wait_ge(ctxw_in, 16)
            T.transpose(prepp[:, NS:NS + C], ctxnat[:, :], ident[0:C, 0:C]).then_inc(condT_ps, 1)
            turn_w0(8, 12)
            pe.wait_ge(condT_sb, 1)
            pe.wait_ge(rep_ready, 2)
            pe.wait_ge(ones_ready, 1)
            for g in range(GROUPS):
                o = z[2][:, NS * g:NS * (g + 1)]
                T.matmul(o, ctxrep[:, g, :, :].rearrange("p j c -> p (j c)"), condT[:, :], start=True, stop=False)
                mm = T.matmul(o, siderep[:, g, :, :].rearrange("p j c -> p (j c)"), ones[:, :], start=False, stop=True)
            mm.then_inc(ctx_ps, 1)
            turn_w0(12, 16)
            pe.wait_ge(taps_sb, 2)
            pe.wait_ge(mlp_in, 16 * 8)
            T.matmul(z[0][:, 0:NS], cw[0][:, :], condT[:, :], start=True, stop=True).then_inc(hid_ps, 1)
            turn_w0(16, 18)
            pe.wait_ge(hid_ready, 1)
            T.matmul(z[0][:, NS:2 * NS], cw[1][:, :], hid[0][:, :], start=True, stop=True).then_inc(hid_ps, 1)
            pe.wait_ge(mixw_in, 32)
            for j in range(4):
                mm = T.transpose(z[1][:, P * j:P * (j + 1)], mixnat[:, j, :, :].rearrange("p s i -> p (s i)"),
                                 ident[:, :])
            mm.then_inc(mixT_ps, 1)
            turn_w0(18, 20)
            pe.wait_ge(hid_ready, 2)
            T.matmul(prepp[0:NS, 256:256 + MIX], hid[1][:, :], w2[:, :], start=True, stop=True).then_inc(att_ps, 1)
            turn_w0(20, PREP_A)
            pe.wait_ge(tl_ready, 2)
            pe.wait_ge(prep_lo, PREP_A)
            conv(0)
            turn_conv(0)

            def turn_b(first, end):
                for q in range(PREP_A + 2 * first, PREP_A + 2 * end):
                    k, hj = divmod(q - PREP_A, 2)
                    if q >= PREP_A + 2:
                        pe.wait_ge(prep_lo, q - 3)
                    if hj == 0:
                        pe.wait_ge(b_ready[k % 2], k // 2 + 1)
                    for j in range(4 * hj, 4 * hj + 4):
                        mm = T.transpose(pbank(q)[:, P * (j % 4):P * (j % 4) + P], b_turn(k)[:, j, :, :].rearrange("p e r -> p (e r)"),
                                         ident[:, :])
                    mm.then_inc(prep_ps, 1)

            pe.wait_ge(att_ready, 1)
            T.transpose(prepp[0:MIX, 320:320 + NS], att[:, :], ident[0:NS, 0:NS]).then_inc(attT_ps, 1)
            pe.wait_ge(attT_sb, 1)
            T.matmul(prepp[:, 384:384 + NS], mixbias[:, :, :].rearrange("p s c -> p (s c)"), attT[:, :],
                     start=True, stop=True).then_inc(mb_ps, 1)
            turn_b(0, 1)

            def w1_pieces(t, u):
                for k in range(4):
                    T.transpose(prepp[:, 64 * k:64 * (k + 1)], w1nat[:, P * k:P * (k + 1)], ident[0:64, 0:64])
                if u == 0:
                    for k in range(2):
                        e = E1 // 2
                        mm = T.transpose(prepp[0:K1, 256 + 64 * k:320 + 64 * k],
                                         lbnat[:, e * k:e * (k + 1), :].rearrange("p e r -> p (e r)"),
                                         ident[0:64, 0:64])
                else:
                    T.transpose(prepp[0:64, 256:256 + E1], gnat[:, :], ident[0:E1, 0:E1])
                    for k in range(2):
                        c0 = 256 + E1 + K1 * k
                        mm = T.transpose(prepp[0:64, c0:c0 + K1], lanat[:, k, :], ident[0:K1, 0:K1])
                mm.then_inc(w1_ps, 1)

            def mixing(t):
                pe.wait_ge(x1_hi, t + 1)
                pe.wait_ge(x1_lo, t + 1)
                pe.wait_ge(mix_lo, 2 * t + 2)
                for b in range(2):
                    w = slice(HALF * b, HALF * (b + 1))
                    three(cp[b][:, :], mixh[:, :], mixl[:, :], x1h[:, w], x1l[:, w], True, True)\
                        .then_inc(a1.c_ps[b], 1)

            def turn_mixed(t):
                for b in range(2):
                    pe.wait_ge(a1.c_out[b], t + 1)
                    for k in range(4):
                        mm = T.transpose(tp[b][:, P * k:P * (k + 1)], mid1[:, P * (4 * b + k):P * (4 * b + k + 1)],
                                         ident[:, :])
                    mm.then_inc(a1.y_ps[b], 1)

            def step0(t, u, first=False, last=False):
                for b in range(2):
                    pe.wait_ge(a0.y_hi[b], t + 1)
                    pe.wait_ge(a0.y_lo[b], t + 1)
                if first:
                    pe.wait_ge(cbT_ready, 1)
                    pe.wait_ge(mixT_ready, 1)
                else:
                    pe.wait_ge(a0.z_out[2], t)
                over_y(2, w0h, w0l).then_inc(base_done[2], 1)
                if first:
                    turn_b(1, 4)
                    pe.wait_ge(mbT_ready, 2)
                pe.wait_ge(w1_in, 48 * t + 48)
                if not first:
                    pe.wait_ge(w1_lo, t)
                    pe.wait_ge(a0.z_out[0], t)
                over_y(0, w0h, w0l).then_inc(base_done[0], 1)
                if first:
                    turn_b(4, 6)
                w1_pieces(t, u)
                if not first:
                    pe.wait_ge(a0.z_out[1], t)
                over_y(1, w0h, w0l).then_inc(base_done[1], 1)
                if first:
                    turn_b(6, 8)
                    pe.wait_ge(prep_lo, PREP)
                pe.wait_ge(a0.hx, 2 * t + 2)
                for b in range(2):
                    for k in range(4):
                        mm = T.transpose(tp[b][:, P * k:P * (k + 1)], mid[:, P * (4 * b + k):P * (4 * b + k + 1)],
                                         ident[:, :])
                    mm.then_inc(a0.hT_ps, 1)
                if last:
                    mixing(0)
                else:
                    conv(t + 1)
                pe.wait_ge(a0.hT_lo, 2 * t + 2)
                over_h(a0, 2, B0, hTh, hTl, bh, bl)
                if last:
                    turn_mixed(0)
                else:
                    turn_conv(t + 1)
                over_h(a0, 0, B0, hTh, hTl, bh, bl)
                over_h(a0, 1, B0, hTh, hTl, bh, bl)

            step0(0, 0, first=True)
            step0(1, 1)
            with pe.Fori(1, TILES // 2 - 1) as i:
                step0(2 * i, 0)
                step0(2 * i + 1, 1)
            step0(TILES - 2, 0)
            step0(TILES - 1, 1, last=True)

            def step1(t, first=False, last=False):
                for b in range(2):
                    pe.wait_ge(a1.y_hi[b], t + 1)
                    pe.wait_ge(a1.y_lo[b], t + 1)
                if first:
                    pe.wait_ge(a0.z_out[2], TILES)
                    pe.wait_ge(w1_back[2], 32)
                over_y(2, w1h, w1l).then_inc(small_done, 1)
                if first:
                    pe.wait_ge(a0.z_out[0], TILES)
                    pe.wait_ge(w1_back[0], 32)
                else:
                    pe.wait_ge(a1.z_out[0], t)
                over_y(0, w1h, w1l)
                if not last:
                    mixing(t + 1)
                pe.wait_ge(a1.hx, 2 * t + 2)
                for k in range(2):
                    mm = T.transpose(prepp[0:K1, P * k:P * (k + 1)], hx1[:, K1 * k:K1 * (k + 1)], ident[:, :])
                mm.then_inc(a1.hT_ps, 1)
                if first:
                    pe.wait_ge(a0.z_out[1], TILES)
                    pe.wait_ge(w1_back[1], 32)
                else:
                    pe.wait_ge(a1.z_out[1], t)
                over_y(1, w1h, w1l)
                if not last:
                    turn_mixed(t + 1)
                if first:
                    pe.wait_ge(lb_in, 32)
                pe.wait_ge(a1.hT_lo, t + 1)
                for b in range(2):
                    over_h(a1, b, B1, h1h, h1l, lbh, lbl)

            step1(0, first=True)
            with pe.Fori(1, TILES - 1) as t:
                step1(t)
            step1(TILES - 1, last=True)


_INS = ['x', 'cond_128', 'fside_S_0', 'L0_cond_weight', 'L0_cond_c_weight', 'L0_ffn_base_w', 'L0_ffn_base_b',
        'L0_ffn_A', 'L0_ffn_B', 'L0_ffn_router_w', 'L1_cond_W0', 'L1_cond_b0', 'L1_cond_W1', 'L1_cond_b1',
        'L1_cond_W2', 'L1_cond_b2', 'L1_cond_weight', 'L1_cond_bias_k', 'L1_ffn_base_W', 'L1_ffn_gate_W',
        'L1_ffn_lora_A', 'L1_ffn_lora_B']


def kernel(**inputs):
    import numpy as _np
    import concourse.bacc as _bacc
    from concourse import mybir as _mybir
    from concourse.bass_utils import run_bass_kernel_spmd as _run

    nc = _bacc.Bacc("TRN2", target_bir_lowering=False, num_devices=1)
    arrays, args = {}, []
    for name in _INS:
        a = _np.ascontiguousarray(inputs[name])
        arrays[f"in_{name}_dram"] = a
        args.append(nc.dram_tensor(f"in_{name}_dram", a.shape, _mybir.dt.from_np(a.dtype), kind="ExternalInput").ap())
    args.append(nc.dram_tensor("out_0_dram", (NS, C, L), F32, kind="ExternalOutput").ap())
    build(nc, *args)
    r = _run(nc, [arrays], core_ids=[0])
    return r.results[0]["out_0_dram"]
```

```python
from contextlib import ExitStack

import concourse.bass as bass
from concourse import mybir

F32 = mybir.dt.float32
F32R = mybir.dt.float32r
U32 = mybir.dt.uint32
I32 = mybir.dt.int32
ALU = mybir.AluOpType
ACT = mybir.ActivationFunctionType
AX = mybir.AxisListType

P = 128
NS, C, L = 64, 64, 1024
TILES = NS * C // P
HALF = 512
GROUPS, CI, TAPS, PAD = 4, 16, 9, 4
BLK = 8
NB = L // BLK
NG = 2 * GROUPS
KC = L // P
E0, R0 = 16, 64
AR = R0 + E0
E1, R1 = 28, 8
ER1 = E1 * R1
K1 = ER1 // 2
GC = E1 + ER1
MIX = 8
EPS = 1e-6
CAP = 2 * TILES * P + P
LISTED = 2 * TILES + E0
SCALE0, SCALE1 = 32.0 / 64.0, 16.0 / 8.0
LO = BLK - 1
SLOTS = 3 * BLK - 1
ROUTE0, ROUTE1 = 16, 10
B0, B1 = 3 * P, HALF


def base_columns(b, width):
    return slice(min(b * width, L), min((b + 1) * width, L))


SM0, SM1 = L - 2 * B0, 0
RK = 448
W0B = (B0, B0, SM0 + AR)
W1B = (B1, B1, GC)
PREP_A = 3 * KC
PREP = PREP_A + 2 * KC


def build(nc, x, cond, side, conv_w, ctx_w, w0, bias0, loraA0, loraB0, router, cW0, cb0, cW1, cb1,
          cW2, cb2, mix_w, mix_b, w1, gate, loraA1, loraB1, out):
    ctx = ExitStack()
    with ctx:
        def sem(name):
            return ctx.enter_context(nc.semaphore(name))

        def sb(stack, name, shape, dt=F32):
            return stack.enter_context(nc.sbuf_tensor(name, shape, dt))

        bank = [ctx.enter_context(nc.psum_tensor(n, [P, HALF], F32))
                for n in ("z0", "z1", "z2", "c0", "c1", "t0", "t1", "prep")]
        z = bank[0:3]
        cp = bank[3:5]
        tp = bank[5:7]
        prepp = bank[7]

        def scratch(name, shape):
            return nc.dram_tensor(name, shape, F32, kind="Internal").ap()
        x1_dram = scratch("x1_dram", [TILES * P, L])
        hs_dram = scratch("hs_dram", [E0 * CAP, 2 * R0])
        zs_dram = scratch("zs_dram", [LISTED * P, L])
        att_dram = scratch("att_dram", [2, TILES, MIX])
        w1_dram = [scratch(f"w1_{s}", [L, L]) for s in ("hi", "lo")]
        g_dram = [scratch(f"g_{s}", [L, GC]) for s in ("hi", "lo")]
        lb_dram = [scratch(f"lb_{s}", [2, K1, L]) for s in ("hi", "lo")]

        ident = sb(ctx, "ident", [P, P])
        iota = sb(ctx, "iota", [P, 32])
        yh = [sb(ctx, "yh0", [P, KC, P], F32R)]
        yl = [sb(ctx, "yl0", [P, KC, P], F32R)]
        xin = [sb(ctx, f"xin{u}", [P, L]) for u in range(2)]
        xb = [sb(ctx, f"xb{u}", [P, L]) for u in range(2)]
        att = sb(ctx, "att", [NS, MIX])
        cbT = sb(ctx, "cbT", [P, TILES, GROUPS, 2])
        mbT = sb(ctx, "mbT", [P, TILES, 1])
        carrier = sb(ctx, "carrier", [P, 1])
        ones_col = sb(ctx, "ones_col", [P, 1])
        mixbias = sb(ctx, "mixbias", [MIX, 2, C])
        attT = sb(ctx, "attT", [MIX, NS])
        mixT = sb(ctx, "mixT", [P, MIX, C])
        upper = sb(ctx, "upper", [P, P])
        onehot = sb(ctx, "onehot", [P, 2, E0])
        before = sb(ctx, "before", [P, 2, E0])
        listed = sb(ctx, "listed", [P, 2, 2, R0])
        place = sb(ctx, "place", [P, 2], I32)
        placef = sb(ctx, "placef", [P, 2])
        rank = sb(ctx, "rank", [P, TILES, 2])
        chosen = sb(ctx, "chosen", [P, TILES, 2])
        odd = sb(ctx, "odd", [P, 2], U32)
        oddf = sb(ctx, "oddf", [P, 2])
        w22 = sb(ctx, "w22", [P, 2, 2])
        lg = sb(ctx, "lg", [P, 32])
        top8 = sb(ctx, "top8", [P, 8])
        idx = sb(ctx, "idx", [P, 8], U32)
        idxf = sb(ctx, "idxf", [P, 2])
        negm = sb(ctx, "negm", [P, 1])
        exsum = sb(ctx, "exsum", [P, 1])
        e12 = sb(ctx, "e12", [P, 2])
        e12sum = sb(ctx, "e12sum", [P, 1])
        den = sb(ctx, "den", [P, 1])
        rden = sb(ctx, "rden", [P, 1])
        w12 = sb(ctx, "w12", [P, 2])
        comb1 = sb(ctx, "comb1", [P, 32])
        ex = comb1
        comb2 = sb(ctx, "comb2", [P, 32])
        comb = sb(ctx, "comb", [P, 32])

        s0 = ExitStack()
        w0h, w0l = {}, {}
        for b in (2, 0, 1):
            w0h[b] = sb(s0, f"w0h{b}", [P, KC, W0B[b]], F32R)
            w0l[b] = sb(s0, f"w0l{b}", [P, KC, W0B[b]], F32R)
        pro = ExitStack()
        w0nat = sb(pro, "w0nat", [P, KC, L])
        arnat = sb(pro, "arnat", [AR, L])
        traw = sb(pro, "traw", [P, 2, BLK, C])
        taps = sb(pro, "taps", [CI, SLOTS, C])
        mixnat = sb(pro, "mixnat", [P, 4, 2, C])
        convnat = sb(pro, "convnat", [C, CI * TAPS])
        cnat = sb(pro, "cnat", [NS, P])
        ctxnat = sb(pro, "ctxnat", [C, P])
        condT = sb(pro, "condT", [P, NS])
        siderow = sb(pro, "siderow", [1, C])
        ones = sb(pro, "ones", [1, NS])
        ctxrep = sb(pro, "ctxrep", [P, GROUPS, BLK, CI])
        siderep = sb(pro, "siderep", [1, GROUPS, BLK, CI])
        cw = [sb(pro, f"cw{j}", [P, P]) for j in range(2)]
        cbias = [sb(pro, f"cbias{j}", [P, 1]) for j in range(2)]
        w2 = sb(pro, "w2", [P, MIX])
        b2b = sb(pro, "b2b", [NS, MIX])
        hid = [sb(pro, f"hid{j}", [P, NS]) for j in range(2)]
        astat = sb(pro, "astat", [NS, 4])
        pro.close()
        bh = sb(s0, "bh", [P, KC, L], F32R)
        bl = sb(s0, "bl", [P, KC, L], F32R)
        s0b = ExitStack()
        th = sb(s0b, "th", [P, 2, GROUPS, BLK, CI], F32R)
        tl = sb(s0b, "tl", [P, 2, GROUPS, BLK, CI], F32R)
        bias0b = sb(s0b, "bias0b", [P, L])
        xd = sb(s0b, "xd", [P, BLK, NB + 1])
        x8h = sb(s0b, "x8h", [P, NG, NB + 1], F32R)
        alias = ExitStack()
        x8 = sb(alias, "x8", [P, NG, NB + 1])
        alias.close()
        x8l = sb(s0b, "x8l", [P, NG, NB + 1], F32R)
        mid = sb(s0b, "mid", [P, L])
        bnat_stack = ExitStack()
        bnat = [sb(bnat_stack, f"bnat{j}", [P, BLK, 2, R0]) for j in range(2)]
        bnat_stack.close()
        bnat += [xb[j].ap().rearrange("p (j e r) -> p j e r", j=BLK, e=2) for j in range(2)]
        yh.append(sb(s0b, "yh1", [P, KC, P], F32R))
        yl.append(sb(s0b, "yl1", [P, KC, P], F32R))
        w1nat = sb(s0b, "w1nat", [64, HALF])
        odd_piece = ExitStack()
        lbnat = sb(odd_piece, "lbnat", [64, E1, R1])
        odd_piece.close()
        gnat = sb(s0b, "gnat", [E1, 96])
        lanat = sb(s0b, "lanat", [K1, 2, 64])
        stage = [sb(s0b, f"stage_{s}", [P, 508], F32R) for s in ("hi", "lo")]
        s0b.close()

        s1b = ExitStack()
        x1h = sb(s1b, "x1h", [P, L], F32R)
        x1l = sb(s1b, "x1l", [P, L], F32R)
        mixh = sb(s1b, "mixh", [P, P], F32R)
        mixl = sb(s1b, "mixl", [P, P], F32R)
        mprod = sb(s1b, "mprod", [P, MIX, C])
        msum = sb(s1b, "msum", [P, C])
        mbrow = sb(s1b, "mbrow", [P, 1])
        hx1 = sb(s1b, "hx1", [P, ER1])
        mid1 = sb(s1b, "mid1", [P, L])
        h1h = sb(s1b, "h1h", [K1, 2, P], F32R)
        h1l = sb(s1b, "h1l", [K1, 2, P], F32R)
        attb = sb(s1b, "attb", [P, TILES, MIX])
        gpos = [sb(s1b, f"gpos{u}", [P, 2], I32) for u in range(2)]
        place1 = sb(s1b, "place1", [P, TILES, 2], I32)
        tab_row = sb(s1b, "tab_row", [1, LISTED, 1], I32)
        tab_pair = sb(s1b, "tab_pair", [1, LISTED, 1], I32)
        s_listed = ExitStack()
        zt = [sb(s_listed, f"zt{v}", [P, L]) for v in range(4)]
        ht = [sb(s_listed, f"ht{v}", [P, 2 * R0]) for v in range(4)]
        hh = [sb(s_listed, f"hh{v}", [P, P], F32R) for v in range(2)]
        hl = [sb(s_listed, f"hl{v}", [P, P], F32R) for v in range(2)]
        s_listed.close()
        s_tables = ExitStack()
        match = sb(s_tables, "match", [P, 2 * TILES, E0])
        first_row = sb(s_tables, "first_row", [P, E0])
        place1f = sb(s_tables, "place1f", [P, TILES * 2])
        zeros = sb(s_tables, "zeros", [P, 2 * R0])
        tile_no = sb(s_tables, "tile_no", [E0, LISTED])
        tile_row = sb(s_tables, "tile_row", [E0, 2 * TILES])
        ind, ind2, indj = (sb(s_tables, n, [E0, LISTED]) for n in ("ind", "ind2", "indj"))
        counts, tiles_of, first_tile, end_tile, jump, pairf, place0 = (
            sb(s_tables, n, [E0, 1]) for n in ("counts", "tiles_of", "first_tile", "end_tile", "jump", "pairf", "place0"))
        expert = sb(s_tables, "expert", [E0, 1], I32)
        pair = sb(s_tables, "pair", [E0, 1], I32)
        spread_tiles = sb(s_tables, "spread_tiles", [E0, E0])
        pad_no = sb(s_tables, "pad_no", [1, E0])
        padf = sb(s_tables, "padf", [1, E0])
        pad_row = sb(s_tables, "pad_row", [1, E0, 1], I32)
        s_tables.close()
        s1b.close()
        s0.close()
        s1 = ExitStack()
        w1h, w1l = {}, {}
        for b in (2, 0, 1):
            w1h[b] = sb(s1, f"w1h{b}", [P, KC, W1B[b]], F32R)
            w1l[b] = sb(s1, f"w1l{b}", [P, KC, W1B[b]], F32R)
        lbh = sb(s1, "lbh", [K1, 2, L], F32R)
        lbl = sb(s1, "lbl", [K1, 2, L], F32R)
        xr = [sb(s1, f"xr{u}", [P, L]) for u in range(2)]
        ga = [sb(s1, f"ga{u}", [P, 2, L]) for u in range(2)]
        s1.close()

        id_zero, id_ready, iota_ready = sem("id_zero"), sem("id_ready"), sem("iota_ready")
        pads_ready, taps_zero, ones_ready = sem("pads_ready"), sem("taps_zero"), sem("ones_ready")
        w0_in = [sem(f"w0_in{j}") for j in range(KC)]
        b_in = [sem(f"b_in{j}") for j in range(4)]
        ar_in, c_in, ctxw_in, side_in = sem("ar_in"), sem("c_in"), sem("ctxw_in"), sem("side_in")
        mlp_in, mixw_in, conv_in, bias0_in = sem("mlp_in"), sem("mixw_in"), sem("conv_in"), sem("bias0_in")
        condT_ps, condT_sb, rep_ready, ctx_ps, cbT_ready = (sem(n) for n in ("condT_ps", "condT_sb", "rep_ready", "ctx_ps", "cbT_ready"))
        hid_ps, hid_ready = sem("hid_ps"), sem("hid_ready")
        att_ps, att_max, att_exp, att_ready, att_stored = (sem(n) for n in ("att_ps", "att_max", "att_exp", "att_ready", "att_stored"))
        attT_ps, attT_sb, mb_ps, mbT_ready = (sem(n) for n in ("attT_ps", "attT_sb", "mb_ps", "mbT_ready"))
        attb_in = sem("attb_in")
        taps_ps, taps_sb, traw_in, th_ready, tl_ready = (sem(n) for n in ("taps_ps", "taps_sb", "traw_in", "th_ready", "tl_ready"))
        mixT_ps, mixT_ready = sem("mixT_ps"), sem("mixT_ready")
        prep_ps, prep_hi, prep_lo = sem("prep_ps"), sem("prep_hi"), sem("prep_lo")

        x_in = [sem(f"x_in{u}") for u in range(2)]
        xd_ready, x8_in, x8_hi, x8_lo = (sem(n) for n in ("xd_ready", "x8_in", "x8_hi", "x8_lo"))
        xb_ready = sem("xb_ready")
        w1_in, w1_ps, w1_hi, w1_lo, w1_stored = (sem(n) for n in ("w1_in", "w1_ps", "w1_hi", "w1_lo", "w1_stored"))
        x1_stored = [sem(f"x1_stored{u}") for u in range(2)]

        class Layer:
            pass

        def layer(tag, banks):
            s = Layer()
            s.c_ps = [sem(f"{tag}_c_ps{b}") for b in range(2)]
            s.c_out = [sem(f"{tag}_c_out{b}") for b in range(2)]
            s.y_ps = [sem(f"{tag}_y_ps{b}") for b in range(2)]
            s.y_hi = [sem(f"{tag}_y_hi{b}") for b in range(2)]
            s.y_lo = [sem(f"{tag}_y_lo{b}") for b in range(2)]
            s.route = sem(f"{tag}_route")
            s.exp = sem(f"{tag}_exp")
            if tag == "l1":
                s.hx = sem("l1_hx")
                s.hT_ps, s.hT_hi, s.hT_lo = sem("l1_hT_ps"), sem("l1_hT_hi"), sem("l1_hT_lo")
                s.z_ps = [sem(f"l1_z_ps{h}") for h in range(banks)]
            s.z_out = [sem(f"{tag}_z_out{h}") for h in range(banks)]
            return s
        a0, a1 = layer("l0", 3), layer("l1", 2)
        small_done = sem("small_done")
        base_done = [sem(f"base_done{b}") for b in range(3)]
        xr_in = [sem(f"xr_in{u}") for u in range(2)]
        ga_in = [sem(f"ga_in{u}") for u in range(2)]
        gpos_ready, ga_sum, x1_ready = sem("gpos_ready"), sem("ga_sum"), sem("x1_ready")
        carried = sem("carried")
        listed_ready, before_ready, rank_ps, place_ready, listed_out = (
            sem(n) for n in ("listed_ready", "before_ready", "rank_ps", "place_ready", "listed_out"))
        upper_ready, zeros_ready, lists_ps, tab, pad_ready, pad_out, tab_ready, place1_ready = (
            sem(n) for n in ("upper_ready", "zeros_ready", "lists_ps", "tab", "pad_ready",
                             "pad_out", "tab_ready", "place1_ready"))
        lists_ready = sem("lists_ready")
        ht_in = [sem(f"ht_in{v}") for v in range(4)]
        zs_out = [sem(f"zs_out{v}") for v in range(4)]
        ht_ps, hh_ready, hl_ready, zt_ps, zt_act, zt_dve = (
            sem(n) for n in ("ht_ps", "hh_ready", "hl_ready", "zt_ps", "zt_act", "zt_dve"))
        x1_hi, x1_lo = sem("x1_hi"), sem("x1_lo")
        mbrow_ready = sem("mbrow_ready")
        mprod_done, msum_done, mix_hi, mix_lo, mix_zero = (sem(n) for n in ("mprod_done", "msum_done", "mix_hi", "mix_lo", "mix_zero"))
        w1_back = [sem(f"w1_back{b}") for b in range(3)]
        lb_in = sem("lb_in")
        out_stored = [sem(f"out_stored{u}") for u in range(2)]

        x_t = x.rearrange("s c l -> (s c) l").rearrange("(t p) l -> t p l", p=P)
        out_t = out.rearrange("s c l -> (s c) l").rearrange("(t p) l -> t p l", p=P)
        hs_t = hs_dram.rearrange("(t p) c -> t p c", p=P)
        zs_t = zs_dram.rearrange("(t p) c -> t p c", p=P)
        x1_t = x1_dram.rearrange("(t p) l -> t p l", p=P)
        w1_t = w1.rearrange("(i o) (u l) -> u i o l", o=64, u=2)
        lb_t = loraB1.rearrange("e (i o) r -> i o e r", o=64)
        gate_t = gate.rearrange("e (i l) -> i e l", l=64)
        la_t = loraA1.rearrange("e r l -> (e r) l").rearrange("(k p) (i l) -> i p k l", k=2, l=64)
        w1_st = [d.rearrange("(u k p) (i o) -> u i p k o", u=2, p=P, o=64) for d in w1_dram]
        g_st = [d.rearrange("(i l) c -> i l c", l=64) for d in g_dram]
        lb_st = [d.rearrange("k p (i o) -> i p k o", o=64) for d in lb_dram]

        def row(ap, n):
            return ap.rearrange("(a n) -> a n", a=1).to_broadcast([n, ap.shape[0]])

        def pbank(q):
            return (tp[0], tp[1], cp[0], cp[1])[(q if q < PREP_A else q - PREP_A + 2) % 4]

        def prep_places(w, b):
            for q in range(PREP_A):
                n, k = divmod(q, KC)
                yield w[n][:, k, :], pbank(q)[:, 0:W0B[n]]
            for q in range(PREP_A, PREP):
                k, hj = divmod(q - PREP_A, 2)
                yield (b[:, k, :].rearrange("q (p j) -> q j p", j=BLK)[:, 4 * hj:4 * hj + 4, :],
                       pbank(q)[:, :].rearrange("q (j p) -> q j p", p=P))

        def exists(t):
            return not isinstance(t, int) or t < TILES

        def y_places(s, y, b):
            if s is a0:
                return (y[:, :, C * b:C * (b + 1)].rearrange("p j (g c) -> p g j c", c=CI),
                        tp[b][:, :].rearrange("p (g j c) -> p g j c", g=GROUPS, c=CI))
            return y[:, 4 * b:4 * b + 4, :], tp[b][:, :].rearrange("p (k r) -> p k r", r=P)

        def pad_lists(engine, half):
            engine.wait_ge(zeros_ready, 5)
            engine.wait_ge(pad_ready, 1)
            for e in range(E0 // 2 * half, E0 // 2 * (half + 1)):
                at = engine.value_load(pad_row[0:1, e, :], min_val=0, max_val=E0 * CAP - P)
                engine.dma_start(hs_dram[bass.ds(at, P), :], zeros[:, :]).then_inc(pad_out, 16)

        block = ctx.enter_context(nc.Block())

        @block.sync
        def _(sp):
            def load_x(i, u):
                sp.dma_start(xin[u][:, :], x_t[2 * i + u]).then_inc(x_in[u], 16)

            def spread_x(t):
                sp.wait_ge(xd_ready, t + 1)
                for n in range(NG):
                    sp.dma_start(x8[:, n, :], xd[CI * n:CI * (n + 1), :, :]).then_inc(x8_in, 16)

            def load_w1(i, u):
                sp.dma_start(w1nat[:, :], w1_t[u, i]).then_inc(w1_in, 16)
                if u == 0:
                    with nc.allow_non_contiguous_dma(reason="rank-8 rows"):
                        sp.dma_start(lbnat[:, :, :], lb_t[i]).then_inc(w1_in, 32)
                else:
                    sp.dma_start(gnat[:, 0:64], gate_t[i]).then_inc(w1_in, 16)
                    sp.dma_start(lanat[:, :, :], la_t[i]).then_inc(w1_in, 16)

            def store_w1(i, u, t):
                for s, done in ((0, w1_hi), (1, w1_lo)):
                    sp.wait_ge(done, t + 1)
                    src = stage[s][:, :].bitcast(F32)
                    sp.dma_start(w1_st[s][u, i], src[:, 0:256].rearrange("p (k o) -> p k o", o=64))\
                      .then_inc(w1_stored, 16)
                    if u == 0:
                        sp.dma_start(lb_st[s][i], src[0:K1, 256:384].rearrange("p (k o) -> p k o", o=64))\
                          .then_inc(w1_stored, 16)
                    else:
                        sp.dma_start(g_st[s][i], src[0:64, 256:256 + GC]).then_inc(w1_stored, 16)

            def store_x1(i, u):
                for b in range(3):
                    sp.wait_ge(a0.z_out[b], 2 * i + u + 1)
                sp.dma_start(x1_t[2 * i + u], xb[u][:, :]).then_inc(x1_stored[u], 16)

            load_x(0, 0)
            for j in range(KC):
                sp.dma_start(w0nat[:, j, :], w0[P * j:P * (j + 1), :]).then_inc(w0_in[j], 16)
            sp.wait_ge(taps_sb, 2)
            tv = taps[:, :, :]
            for w in range(2):
                sp.dma_start(traw[:, w, :, :].rearrange("p j c -> p (j c)"),
                             bass.AP(tv.tensor, tv.offset + BLK * w * C, [list(tv.ap[0]), [C, BLK], [1, BLK * C]]))\
                  .then_inc(traw_in, 16)
            spread_x(0)
            for j, (w, b) in enumerate(((cW0, cb0), (cW1, cb1))):
                sp.dma_start(cw[j][:, :], w).then_inc(mlp_in, 16)
                sp.dma_start(cbias[j][:, :], b.rearrange("(n a) -> n a", a=1)).then_inc(mlp_in, 16)
            sp.dma_start(w2[:, :], cW2).then_inc(mlp_in, 16)
            sp.dma_start(b2b[:, :], row(cb2, NS)).then_inc(mlp_in, 16)
            for s in range(2):
                sp.dma_start(mixbias[:, s, :], mix_b).then_inc(mlp_in, 16)
            mixw_v = mix_w.rearrange("k o i a -> (k o) (i a)").rearrange("(j p) i -> p j i", p=P)
            for s in range(2):
                sp.dma_start(mixnat[:, :, s, :], mixw_v).then_inc(mixw_in, 16)
            for j in range(KC):
                if j >= 4:
                    sp.wait_ge(prep_ps, PREP_A + 2 * (j - 3))
                sp.dma_start(bnat[j % 4][:, :, :, :], loraB0[2 * j:2 * j + 2].rearrange("e (p j) r -> p j e r", j=BLK))\
                  .then_inc(b_in[j % 4], 16)
                if j == 1:
                    sp.dma_start(bias0b[:, :], row(bias0, P)).then_inc(bias0_in, 16)
                    load_x(0, 1)
                    load_w1(0, 0)

            def step0(i, u, first=False):
                t = 2 * i + u
                if not first:
                    store_x1(i + u - 1, 1 - u)
                if exists(t + 2):
                    spread_x(t + 2)
                sp.wait_ge(w1_ps, t + 1)
                if exists(t + 1):
                    load_w1(i + u, 1 - u)
                store_w1(i, u, t)
                if exists(t + 3):
                    sp.wait_ge(xd_ready, t + 2)
                    sp.wait_ge(xb_ready, t + 2)
                    load_x(i + u + 1, 1 - u)

            spread_x(1)
            sp.wait_ge(xb_ready, 1)
            load_x(1, 0)

            step0(0, 0, first=True)
            step0(0, 1)
            with sp.Fori(1, TILES // 2 - 2) as i:
                step0(i, 0)
                step0(i, 1)
            n = TILES // 2 - 1
            for i, u in ((n - 1, 0), (n - 1, 1), (n, 0), (n, 1)):
                step0(i, u)
            sp.wait_ge(w1_stored, 64 * TILES)

            def load_back(b, s):
                src = g_dram[s] if b == 2 else w1_dram[s][:, base_columns(b, B1)]
                sp.dma_start((w1h, w1l)[s][b][:, :, :].bitcast(F32), src.rearrange("(k p) c -> p k c", p=P))\
                  .then_inc(w1_back[b], 16)

            sp.wait_ge(base_done[2], TILES)
            load_back(2, 0)
            load_back(2, 1)
            pad_lists(sp, 0)
            store_x1(n, 1)
            sp.wait_ge(att_ready, 1)
            sp.dma_start(att_dram.rearrange("s t k -> t s k"), att[:, :]).then_inc(att_stored, 16)
            sp.wait_ge(att_stored, 16)
            for s in range(2):
                sp.dma_start(attb[64 * s:64 * (s + 1), :, :].rearrange("p t k -> p (t k)"),
                             row(att_dram[s].rearrange("t k -> (t k)"), 64)).then_inc(attb_in, 16)

            def load_ht(j, v):
                at = sp.value_load(tab_row[0:1, j, :], min_val=0, max_val=E0 * CAP // P - 1)
                sp.dma_start(ht[v][:, :], hs_t[at]).then_inc(ht_in[v], 16)

            def listed_out_and_in(i, v, more=True):
                j = 4 * i + v
                if more:
                    sp.wait_ge(ht_ps, j + 1)
                    load_ht(j + 4, v)
                sp.wait_ge(zt_act, j + 1)
                sp.wait_ge(zt_dve, j + 1)
                sp.dma_start(zs_t[j], zt[v][:, :]).then_inc(zs_out[v], 16)

            sp.wait_ge(listed_out, 32 * TILES)
            sp.wait_ge(pad_out, 16 * E0)
            sp.wait_ge(tab_ready, 2)
            for v in range(4):
                load_ht(v, v)
            load_back(0, 0)
            for v in range(4):
                listed_out_and_in(0, v)
            with sp.Fori(1, LISTED // 4 - 1) as i:
                for v in range(4):
                    listed_out_and_in(i, v)
            for v in range(4):
                listed_out_and_in(LISTED // 4 - 1, v, more=False)

            def load_xr(i, u):
                sp.dma_start(xr[u][:, :], x1_t[2 * i + u]).then_inc(xr_in[u], 16)

            sp.wait_ge(zt_ps, LISTED)
            for u in range(2):
                sp.wait_ge(x1_stored[u], 16 * (TILES // 2))
            load_xr(0, 0)
            load_xr(0, 1)
            for u in range(2):
                sp.wait_ge(ga_in[u], 32)
            load_back(0, 1)
            load_back(1, 0)
            load_back(1, 1)
            for dst, d in ((lbh, lb_dram[0]), (lbl, lb_dram[1])):
                sp.dma_start(dst[:, :, :].bitcast(F32), d.rearrange("k p o -> p k o")).then_inc(lb_in, 16)

            def step1(i, u, prefetch=True):
                t = 2 * i + u
                if prefetch:
                    sp.wait_ge(x1_ready, t + 1)
                    load_xr(i + 1, u)
                for b in range(2):
                    sp.wait_ge(a1.z_out[b], t + 1)
                sp.dma_start(out_t[t], xb[u][:, :]).then_inc(out_stored[u], 16)

            with sp.Fori(0, TILES // 2 - 1) as i:
                step1(i, 0)
                step1(i, 1)
            step1(n, 0, prefetch=False)
            step1(n, 1, prefetch=False)
            for u in range(2):
                sp.wait_ge(out_stored[u], 16 * (TILES // 2))
            for v in range(4):
                sp.wait_ge(zs_out[v], 16 * (LISTED // 4))

        @block.gpsimd
        def _(pool):
            nc.gpsimd.memset(ones[:, :], 1.0).then_inc(ones_ready, 1)
            nc.gpsimd.memset(ones_col[:, :], 1.0).then_inc(ones_ready, 1)
            nc.gpsimd.memset(ident[:, :], 0.0).then_inc(id_zero, 1)
            pool.wait_ge(id_zero, 1)
            nc.gpsimd.affine_select(out=ident[:, :], in_=ident[:, :], compare_op=ALU.not_equal, fill=1.0,
                                    base=0, pattern=[[-1, P]], channel_multiplier=1).then_inc(id_ready, 1)
            nc.gpsimd.memset(taps[:, :, :], 0.0).then_inc(taps_zero, 1)
            nc.gpsimd.memset(upper[:, :], 1.0).then_inc(upper_ready, 1)
            nc.gpsimd.memset(before[:, :, :], 0.0).then_inc(upper_ready, 1)
            pool.wait_ge(upper_ready, 2)
            nc.gpsimd.affine_select(out=upper[:, :], in_=upper[:, :], compare_op=ALU.is_gt, fill=0.0,
                                    base=0, pattern=[[1, P]], channel_multiplier=-1).then_inc(upper_ready, 1)
            nc.gpsimd.iota(iota[:, :], pattern=[[1, 32]], base=0, channel_multiplier=0,
                           allow_small_or_imprecise_dtypes=True).then_inc(iota_ready, 1)
            nc.gpsimd.memset(xd[:, 0:PAD, 0:1], 0.0).then_inc(pads_ready, 1)
            nc.gpsimd.memset(xd[:, PAD:BLK, NB:NB + 1], 0.0).then_inc(pads_ready, 1)
            for w in range(2):
                pool.wait_ge(th_ready, w + 1)
                nc.gpsimd.tensor_tensor(tl[:, w, :, :, :], traw[:, w, :, :].rearrange("p j (g c) -> p g j c", c=CI),
                                        th[:, w, :, :, :], ALU.subtract).then_inc(tl_ready, 1)
            pool.wait_ge(bias0_in, 16)
            pool.wait_ge(prep_ps, PREP)

            def residual(i, u, first=False):
                pool.wait_ge(x_in[u], 16 * (i + 1))
                if not first:
                    pool.wait_ge(x1_stored[u], 16 * i)
                nc.gpsimd.tensor_tensor(xb[u][:, :], xin[u][:, :], bias0b[:, :], ALU.add).then_inc(xb_ready, 1)

            def carry(semaphore, count, carries):
                pool.wait_ge(semaphore, count)
                if not isinstance(carries, int) or carries:
                    pool.wait_ge(carried, carries)
                nc.gpsimd.tensor_tensor(carrier[:, :], ones_col[:, :], ones_col[:, :], ALU.add).then_inc(carried, 1)

            def scatter(t):
                carry(place_ready, 2 * t + 2, t)
                for k in range(2):
                    nc.gpsimd.indirect_dma_start(hs_dram, bass.IndirectOffsetOnAxis(ap=place[:, k:k + 1], axis=0),
                                                 listed[:, k, :, :].rearrange("p a r -> p (a r)"), None)\
                      .then_inc(listed_out, 16)

            residual(0, 0, first=True)
            residual(0, 1, first=True)
            for u in range(2):
                scatter(u)
                residual(1, u)
            with pool.Fori(2, TILES // 2) as i:
                for u in range(2):
                    scatter(2 * i + u - 2)
                    residual(i, u)
            scatter(TILES - 2)
            scatter(TILES - 1)
            pool.wait_ge(base_done[1], TILES)
            pool.wait_ge(a0.y_lo[1], TILES)
            pool.wait_ge(w1_ps, TILES)
            nc.gpsimd.iota(pad_no[:, :], pattern=[[CAP, E0]], base=0, channel_multiplier=0,
                           allow_small_or_imprecise_dtypes=True).then_inc(zeros_ready, 1)
            nc.gpsimd.iota(tile_row[:, :], pattern=[[P, 2 * TILES]], base=0, channel_multiplier=0,
                           allow_small_or_imprecise_dtypes=True).then_inc(zeros_ready, 1)
            nc.gpsimd.iota(tile_no[:, :], pattern=[[1, LISTED]], base=0, channel_multiplier=0,
                           allow_small_or_imprecise_dtypes=True).then_inc(zeros_ready, 1)
            nc.gpsimd.iota(expert[:, :], pattern=[[0, 1]], base=0, channel_multiplier=1).then_inc(zeros_ready, 1)
            nc.gpsimd.memset(zeros[:, :], 0.0).then_inc(zeros_ready, 1)

            def gather(i, u, first=False):
                t = 2 * i + u
                if not first:
                    pool.wait_ge(x1_ready, t - 1)
                nc.gpsimd.tensor_copy(gpos[u][:, :], place1[:, t, :]).then_inc(gpos_ready, 1)
                carry(gpos_ready, t + 1, TILES + t)
                for k in range(2):
                    nc.gpsimd.indirect_dma_start(ga[u][:, k, :], None, zs_dram,
                                                 bass.IndirectOffsetOnAxis(ap=gpos[u][:, k:k + 1], axis=0))\
                      .then_inc(ga_in[u], 16)

            def sum_x1(i, u, first=False):
                t = 2 * i + u
                pool.wait_ge(ga_in[u], 32 * i + 32)
                nc.gpsimd.tensor_tensor(ga[u][:, 0, :], ga[u][:, 0, :], ga[u][:, 1, :], ALU.add).then_inc(ga_sum, 1)
                pool.wait_ge(ga_sum, t + 1)
                pool.wait_ge(xr_in[u], 16 * i + 16)
                if not first:
                    pool.wait_ge(a1.z_out[1], t - 1)
                    pool.wait_ge(a1.z_out[0], t - 1)
                nc.gpsimd.tensor_tensor(xin[u][:, :], ga[u][:, 0, :], xr[u][:, :], ALU.add).then_inc(x1_ready, 1)

            for v in range(4):
                pool.wait_ge(zs_out[v], 16 * (LISTED // 4))
            pool.wait_ge(zt_ps, LISTED)
            pool.wait_ge(place1_ready, 1)
            gather(0, 0, first=True)
            gather(0, 1, first=True)
            gather(1, 0)
            sum_x1(0, 1, first=True)
            with pool.Fori(1, TILES // 2 - 1) as i:
                gather(i, 1)
                sum_x1(i, 0)
                gather(i + 1, 0)
                sum_x1(i, 1)
            n = TILES // 2 - 1
            gather(n, 1)
            sum_x1(n, 0)
            sum_x1(n, 1)

        @block.scalar
        def _(act):
            def copy(o, i_):
                return nc.scalar.activation(o, i_, ACT.Copy)

            act.dma_start(convnat[:, :], conv_w.rearrange("o c k -> o (c k)")).then_inc(conv_in, 16)
            act.dma_start(cnat[:, :], cond).then_inc(c_in, 16)
            act.dma_start(ctxnat[:, :], ctx_w).then_inc(ctxw_in, 16)
            act.dma_start(siderow[:, :], row(side, 1)).then_inc(side_in, 16)
            act.dma_start(arnat[0:R0, :], loraA0).then_inc(ar_in, 16)
            act.dma_start(arnat[R0:AR, :], router).then_inc(ar_in, 16)

            def blocks(i, u):
                act.wait_ge(x_in[u], 16 * i + 16)
                v = xin[u][:, :].rearrange("p (m j) -> p j m", j=BLK)
                copy(xd[:, PAD:BLK, 0:NB], v[:, 0:PAD, :])
                copy(xd[:, 0:PAD, 1:NB + 1], v[:, PAD:BLK, :]).then_inc(xd_ready, 1)

            def x8_high(t):
                act.wait_ge(x8_in, 128 * t + 128)
                copy(x8h[:, :, :], x8[:, :, :]).then_inc(x8_hi, 1)

            def y_high(s, t, b, y):
                act.wait_ge(s.y_ps[b], t + 1)
                copy(*y_places(s, yh[y], b)).then_inc(s.y_hi[b], 1)

            def exps(s, t):
                act.wait_ge(s.route, (ROUTE0 if s is a0 else ROUTE1) * t + 3)
                if s is a0:
                    nc.scalar.activation(ex[:, 0:E0], lg[:, 0:E0], ACT.Exp, bias=negm[:, :],
                                         accum_out=exsum[:, :]).then_inc(s.exp, 1)
                nc.scalar.activation(e12[:, :], top8[:, 0:2], ACT.Exp, bias=negm[:, :],
                                     accum_out=e12sum[:, :]).then_inc(s.exp, 1)

            high = list(prep_places(w0h, bh))

            def prep_high(first, end):
                for q in range(first, end):
                    act.wait_ge(prep_ps, q + 1)
                    copy(*high[q]).then_inc(prep_hi, 1)

            def hidden(j):
                act.wait_ge(hid_ps, j + 1)
                nc.scalar.activation(hid[j][:, :], z[0][:, NS * j:NS * (j + 1)], ACT.Gelu,
                                     bias=cbias[j][:, :]).then_inc(hid_ready, 1)

            act.wait_ge(taps_zero, 1)
            act.wait_ge(taps_ps, 1)
            copy(taps[:, LO:LO + 8, :], z[0][0:CI, :].rearrange("p (k o) -> p k o", o=C)).then_inc(taps_sb, 1)
            copy(taps[:, LO + 8, :], z[1][0:CI, 0:C]).then_inc(taps_sb, 1)
            act.wait_ge(pads_ready, 2)
            blocks(0, 0)
            prep_high(0, 8)
            act.wait_ge(condT_ps, 2)
            copy(condT[:, :], prepp[:, 0:NS]).then_inc(condT_sb, 1)
            copy(ctxrep[:, :, :, :], prepp[:, NS:NS + C].rearrange("p (g c) -> p g c", c=CI).unsqueeze(2)
                 .to_broadcast([P, GROUPS, BLK, CI])).then_inc(rep_ready, 1)
            act.wait_ge(side_in, 16)
            copy(siderep[:, :, :, :], siderow[:, :].rearrange("p (g c) -> p g c", c=CI).unsqueeze(2)
                 .to_broadcast([1, GROUPS, BLK, CI])).then_inc(rep_ready, 1)
            prep_high(8, 12)
            act.wait_ge(traw_in, 16 * 2)
            for w in range(2):
                copy(th[:, w, :, :, :], traw[:, w, :, :].rearrange("p j (g c) -> p g j c", c=CI)).then_inc(th_ready, 1)
            prep_high(12, 16)
            x8_high(0)
            act.wait_ge(mlp_in, 16 * 8)
            hidden(0)
            prep_high(16, 18)
            hidden(1)
            act.wait_ge(mixT_ps, 1)
            copy(mixT[:, :, :], z[1][:, :].rearrange("p (k o) -> p k o", o=C)).then_inc(mixT_ready, 1)
            prep_high(18, PREP_A)
            act.wait_ge(att_max, 3)
            nc.scalar.activation(att[:, :], lg[0:NS, 0:MIX], ACT.Exp, bias=astat[:, 1:2],
                                 accum_out=astat[:, 2:3]).then_inc(att_exp, 1)
            y_high(a0, 0, 0, 0)
            y_high(a0, 0, 1, 0)

            def x1_high(i, u):
                act.wait_ge(x1_ready, 2 * i + u + 1)
                copy(x1h[:, :], xin[u][:, :]).then_inc(x1_hi, 1)

            def mix_high(t):
                act.wait_ge(msum_done, t + 1)
                for s in range(2):
                    q = slice(64 * s, 64 * (s + 1))
                    copy(mixh[q, q], msum[q, :]).then_inc(mix_hi, 1)

            def mixed_out(t):
                for b in range(2):
                    act.wait_ge(a1.c_ps[b], t + 1)
                    act.wait_ge(mbrow_ready, t + 1)
                    nc.scalar.activation(mid1[:, HALF * b:HALF * (b + 1)], cp[b][:, :], ACT.Identity,
                                         bias=mbrow[:, :]).then_inc(a1.c_out[b], 1)

            def w1_high(t, u, first=False):
                if not first:
                    act.wait_ge(w1_stored, 64 * t)
                act.wait_ge(w1_ps, t + 1)
                copy(stage[0][:, 0:256], prepp[:, 0:256])
                if u == 0:
                    copy(stage[0][0:K1, 256:384], prepp[0:K1, 256:384]).then_inc(w1_hi, 1)
                else:
                    copy(stage[0][0:64, 256:256 + GC], prepp[0:64, 256:256 + GC]).then_inc(w1_hi, 1)

            def step0(i, u, first=False):
                t = 2 * i + u
                if first:
                    act.wait_ge(x8_in, 128)
                    blocks(0, 1)
                    prep_high(PREP_A, PREP - 2)
                    x8_high(1)
                    prep_high(PREP - 2, PREP)
                    exps(a0, 0)
                if exists(t + 2):
                    act.wait_ge(x8_in, 128 * t + 256)
                    act.wait_ge(a0.c_ps[1], t + 2)
                    blocks(i + 1, u)
                if not first:
                    exps(a0, t)
                w1_high(t, u, first)
                if exists(t + 1):
                    for b in range(2):
                        y_high(a0, t + 1, b, 1 - u)
                if exists(t + 2):
                    x8_high(t + 2)

            step0(0, 0, first=True)
            step0(0, 1)
            with act.Fori(1, TILES // 2 - 2) as i:
                step0(i, 0)
                step0(i, 1)
            n = TILES // 2 - 1
            for i, u in ((n - 1, 0), (n - 1, 1), (n, 0), (n, 1)):
                step0(i, u)

            def ht_high(j, v, first=False):
                act.wait_ge(ht_ps, j + 1)
                if not first:
                    act.wait_ge(zt_ps, j - 1)
                copy(hh[v % 2][:, :], tp[v % 2][:, 0:P]).then_inc(hh_ready, 1)

            def outputs(i, v, first=False, last=False):
                j = 4 * i + v
                if not last:
                    ht_high(j + 1, v + 1, first=first and v == 0)
                act.wait_ge(zt_ps, j + 1)
                if not first:
                    act.wait_ge(zs_out[v], 16 * i)
                copy(zt[v][:, 0:HALF], (z[0], cp[0])[v % 2][:, :]).then_inc(zt_act, 1)

            pad_lists(act, 1)
            act.wait_ge(tab_ready, 2)
            act.wait_ge(place1_ready, 1)
            act.wait_ge(pad_out, 16 * E0)
            ht_high(0, 0, first=True)
            for v in range(4):
                outputs(0, v, first=True)
            with act.Fori(1, LISTED // 4 - 1) as i:
                for v in range(4):
                    outputs(i, v)
            for v in range(4):
                outputs(LISTED // 4 - 1, v, last=v == 3)

            act.wait_ge(mix_zero, 2)
            mix_high(0)
            x1_high(0, 0)
            mixed_out(0)
            y_high(a1, 0, 0, 0)
            y_high(a1, 0, 1, 0)

            def step1(i, u, last=False):
                t = 2 * i + u
                if not last:
                    act.wait_ge(a1.c_ps[1], t + 1)
                    mix_high(t + 1)
                exps(a1, t)
                if not last:
                    x1_high(i + u, 1 - u)
                    mixed_out(t + 1)
                act.wait_ge(a1.hT_ps, t + 1)
                copy(h1h[:, :, :], prepp[0:K1, 0:2 * P].rearrange("p (k r) -> p k r", r=P)).then_inc(a1.hT_hi, 1)
                if not last:
                    y_high(a1, t + 1, 0, 0)
                    y_high(a1, t + 1, 1, 0)

            with act.Fori(0, TILES // 2 - 1) as i:
                step1(i, 0)
                step1(i, 1)
            step1(TILES // 2 - 1, 0)
            step1(TILES // 2 - 1, 1, last=True)

        @block.vector
        def _(dve):
            V = nc.vector

            def x8_low(t):
                dve.wait_ge(x8_hi, t + 1)
                V.tensor_tensor(x8l[:, :, :], x8[:, :, :], x8h[:, :, :], ALU.subtract).then_inc(x8_lo, 1)

            def conv_out(t):
                for b in range(2):
                    dve.wait_ge(a0.c_ps[b], t + 1)
                    v = [a[:, :].rearrange("p (g s m) -> p g s m", g=2, s=2)
                         for a in (mid[:, HALF * b:HALF * (b + 1)], cp[b])]
                    V.tensor_tensor(v[0], v[1], cbT[:, t, 2 * b:2 * b + 2, :].unsqueeze(3)
                                    .to_broadcast([P, 2, 2, NB]), ALU.add).then_inc(a0.c_out[b], 1)

            def y_low(s, t, y):
                for b in range(2):
                    dve.wait_ge(s.y_hi[b], t + 1)
                    o, v = y_places(s, yl[y], b)
                    V.tensor_tensor(o, v, y_places(s, yh[y], b)[0], ALU.subtract).then_inc(s.y_lo[b], 1)

            def routing(s, t, projected, first, experts, scale):
                r, steps = s.route, ROUTE0 if s is a0 else ROUTE1

                def after(k):
                    dve.wait_ge(r, steps * t + k)
                dve.wait_ge(projected, t + 1)
                V.tensor_copy(lg[:, 0:experts], z[2][:, first:first + experts]).then_inc(r, 1)
                V.max(top8[:, :], z[2][:, first:first + experts]).then_inc(r, 1)
                after(2)
                V.tensor_scalar(negm[:, :], top8[:, 0:1], -1.0, None, ALU.mult).then_inc(r, 1)
                V.max_index(idx[:, :], top8[:, :], lg[:, 0:experts]).then_inc(r, 1)
                after(4)
                V.tensor_copy(idxf[:, :], idx[:, 0:2]).then_inc(r, 1)
                dve.wait_ge(s.exp, (2 if s is a0 else 1) * (t + 1))
                if s is a0:
                    V.tensor_scalar(den[:, :], exsum[:, :], EPS, e12sum[:, :], ALU.mult, ALU.add).then_inc(r, 1)
                else:
                    V.tensor_copy(den[:, :], e12sum[:, :]).then_inc(r, 1)
                after(6)
                V.reciprocal(rden[:, :], den[:, :]).then_inc(r, 1)
                after(7)
                V.tensor_scalar(w12[:, :], e12[:, :], rden[:, :], scale, ALU.mult, ALU.mult).then_inc(r, 1)
                after(8)
                if s is a0:
                    return
                V.tensor_scalar(comb1[:, 0:experts], iota[:, 0:experts], idxf[:, 0:1], w12[:, 0:1],
                                ALU.is_equal, ALU.mult).then_inc(r, 1)
                V.tensor_scalar(comb2[:, 0:experts], iota[:, 0:experts], idxf[:, 1:2], w12[:, 1:2],
                                ALU.is_equal, ALU.mult).then_inc(r, 1)
                after(10)

            def list0(t, first=False):
                routing(a0, t, base_done[2], SM0 + R0, E0, SCALE0)
                r = a0.route

                def after(k):
                    dve.wait_ge(r, ROUTE0 * t + k)
                V.tensor_scalar(odd[:, :], idx[:, 0:2], 1, None, ALU.bitwise_and).then_inc(r, 1)
                for k in range(2):
                    V.tensor_scalar(onehot[:, k, :], iota[:, 0:E0], idxf[:, k:k + 1], None, ALU.is_equal).then_inc(r, 1)
                V.tensor_copy(chosen[:, t, :], idxf[:, :]).then_inc(r, 1)
                after(12)
                V.tensor_copy(oddf[:, :], odd[:, :]).then_inc(r, 1)
                V.tensor_tensor(before[:, 1, :], before[:, 0, :], onehot[:, 0, :], ALU.add).then_inc(r, 1)
                after(14)
                V.tensor_tensor(w22[:, :, 1], w12[:, :], oddf[:, :], ALU.mult).then_inc(r, 1)
                after(15)
                V.tensor_tensor(w22[:, :, 0], w12[:, :], w22[:, :, 1], ALU.subtract).then_inc(r, 1)
                after(16)
                if not first:
                    dve.wait_ge(listed_out, 32 * t)
                V.tensor_tensor(listed[:, :, :, :].rearrange("p k a r -> p (k a) r"),
                                z[2][:, SM0:SM0 + R0].unsqueeze(1).to_broadcast([P, 4, R0]),
                                w22[:, :, :].rearrange("p k a -> p (k a)").unsqueeze(2).to_broadcast([P, 4, R0]),
                                ALU.mult).then_inc(listed_ready, 1)

            def rank0(t):
                dve.wait_ge(rank_ps, t + 1)
                counted = comb[:, 0:2 * E0].rearrange("p (k e) -> p k e", e=E0)
                V.tensor_tensor(counted, z[2][:, RK:RK + 2 * E0].rearrange("p (k e) -> p k e", e=E0),
                                onehot[:, :, :], ALU.mult).then_inc(before_ready, 1)
                V.tensor_tensor(before[:, 0, :], before[:, 1, :], onehot[:, 1, :], ALU.add).then_inc(before_ready, 1)
                dve.wait_ge(before_ready, 5 * t + 2)
                V.tensor_reduce(rank[:, t, :], counted, AX.X, ALU.add).then_inc(before_ready, 1)
                V.tensor_scalar(placef[:, :], idxf[:, :], float(CAP), None, ALU.mult).then_inc(before_ready, 1)
                dve.wait_ge(before_ready, 5 * t + 4)
                V.tensor_tensor(placef[:, :], placef[:, :], rank[:, t, :], ALU.add).then_inc(before_ready, 1)
                dve.wait_ge(before_ready, 5 * t + 5)
                V.tensor_copy(place[:, :], placef[:, :]).then_inc(place_ready, 1)
                V.tensor_copy(den[:, :], placef[:, 0:1]).then_inc(place_ready, 1)

            def spread1(t):
                routing(a1, t, small_done, SM1, E1, SCALE1)
                V.tensor_tensor(comb[:, 0:E1], comb1[:, 0:E1], comb2[:, 0:E1], ALU.add).then_inc(a1.hx, 1)
                dve.wait_ge(a1.hx, 2 * t + 1)
                V.tensor_tensor(hx1[:, :].rearrange("p (e r) -> p e r", r=R1),
                                z[2][:, SM1 + E1:SM1 + GC].rearrange("p (e r) -> p e r", r=R1),
                                comb[:, 0:E1].unsqueeze(2).to_broadcast([P, E1, R1]), ALU.mult).then_inc(a1.hx, 1)

            high, low = list(prep_places(w0h, bh)), list(prep_places(w0l, bl))

            def prep_low(first, end):
                for q in range(first, end):
                    dve.wait_ge(prep_hi, q + 1)
                    V.tensor_tensor(low[q][0], low[q][1], high[q][0], ALU.subtract).then_inc(prep_lo, 1)

            prep_low(0, 16)
            dve.wait_ge(ctx_ps, 1)
            V.tensor_copy(cbT[:, :, :, :].rearrange("p t g s -> p g t s"),
                          z[2][:, 0:GROUPS * NS].rearrange("p (g t s) -> p g t s", g=GROUPS, s=2)).then_inc(cbT_ready, 1)
            x8_low(0)
            prep_low(16, 20)
            dve.wait_ge(mlp_in, 16 * 8)
            dve.wait_ge(att_ps, 1)
            V.tensor_tensor(lg[0:NS, 0:MIX], prepp[0:NS, 256:256 + MIX], b2b[:, :], ALU.add).then_inc(att_max, 1)
            dve.wait_ge(att_max, 1)
            V.tensor_reduce(astat[:, 0:1], lg[0:NS, 0:MIX], AX.X, ALU.max).then_inc(att_max, 1)
            dve.wait_ge(att_max, 2)
            V.tensor_scalar(astat[:, 1:2], astat[:, 0:1], -1.0, None, ALU.mult).then_inc(att_max, 1)
            prep_low(20, PREP_A)
            conv_out(0)
            dve.wait_ge(att_exp, 1)
            V.reciprocal(astat[:, 3:4], astat[:, 2:3]).then_inc(att_max, 1)
            dve.wait_ge(att_max, 4)
            V.tensor_scalar(att[:, :], att[:, :], astat[:, 3:4], None, ALU.mult).then_inc(att_ready, 1)
            y_low(a0, 0, 0)
            dve.wait_ge(iota_ready, 1)

            def x1_low(u, t):
                dve.wait_ge(x1_hi, t + 1)
                V.tensor_tensor(x1l[:, :], xin[u][:, :], x1h[:, :], ALU.subtract).then_inc(x1_lo, 1)

            def mix(t):
                V.tensor_copy(mbrow[:, :], mbT[:, t, :]).then_inc(mbrow_ready, 1)
                V.tensor_tensor(mprod[:, :, :], mixT[:, :, :],
                                attb[:, t, :].unsqueeze(2).to_broadcast([P, MIX, C]), ALU.mult).then_inc(mprod_done, 1)
                dve.wait_ge(mprod_done, t + 1)
                V.tensor_reduce(msum[:, :], mprod[:, :, :].rearrange("p k o -> p o k"), AX.X, ALU.add)\
                    .then_inc(msum_done, 1)
                dve.wait_ge(mix_hi, 2 * t + 2)
                for s in range(2):
                    q = slice(64 * s, 64 * (s + 1))
                    V.tensor_tensor(mixl[q, q], msum[q, :], mixh[q, q], ALU.subtract).then_inc(mix_lo, 1)

            def w1_low(t, u):
                dve.wait_ge(w1_hi, t + 1)
                V.tensor_tensor(stage[1][:, 0:256], prepp[:, 0:256], stage[0][:, 0:256], ALU.subtract)
                if u == 0:
                    q, w = slice(0, K1), slice(256, 384)
                else:
                    q, w = slice(0, 64), slice(256, 256 + GC)
                V.tensor_tensor(stage[1][q, w], prepp[q, w], stage[0][q, w], ALU.subtract).then_inc(w1_lo, 1)

            def step0(i, u, first=False):
                t = 2 * i + u

                def residual(b):
                    dve.wait_ge(base_done[b], t + 1)
                    w = base_columns(b, B0)
                    o = xb[u][:, w]
                    return V.tensor_tensor(o, z[b][:, 0:w.stop - w.start], o, ALU.add).then_inc(a0.z_out[b], 1)

                if first:
                    prep_low(PREP_A, PREP_A + 2)
                    dve.wait_ge(attT_ps, 1)
                    V.tensor_copy(attT[:, :], prepp[0:MIX, 320:320 + NS]).then_inc(attT_sb, 1)
                    prep_low(PREP_A + 2, PREP_A + 8)
                    dve.wait_ge(mb_ps, 1)
                    mv = prepp[:, 384:384 + NS].rearrange("p (t s) -> p t s", s=2)
                    for s in range(2):
                        q = slice(64 * s, 64 * (s + 1))
                        V.tensor_copy(mbT[q, :, 0], mv[q, :, s]).then_inc(mbT_ready, 1)
                    prep_low(PREP_A + 8, PREP - 2)
                    x8_low(1)
                    prep_low(PREP - 2, PREP)
                    dve.wait_ge(upper_ready, 3)
                    list0(0, first=True)
                    conv_out(1)
                else:
                    if exists(t + 1):
                        conv_out(t + 1)
                    list0(t)
                dve.wait_ge(xb_ready, t + 1)
                residual(2)
                residual(0)
                w1_low(t, u)
                if exists(t + 1):
                    y_low(a0, t + 1, 1 - u)
                if exists(t + 2):
                    x8_low(t + 2)
                residual(1)
                rank0(t)

            step0(0, 0, first=True)
            step0(0, 1)
            with dve.Fori(1, TILES // 2 - 2) as i:
                step0(i, 0)
                step0(i, 1)
            n = TILES // 2 - 1
            for i, u in ((n - 1, 0), (n - 1, 1), (n, 0), (n, 1)):
                step0(i, u)

            step = [0]

            def done(op):
                step[0] += 1
                op.then_inc(tab, 1)
                dve.wait_ge(tab, step[0])

            dve.wait_ge(zeros_ready, 5)
            dve.wait_ge(lists_ps, 1)
            done(V.tensor_tensor(padf[:, :], z[2][0:1, RK + E0:RK + 2 * E0], pad_no[:, :], ALU.add))
            V.tensor_copy(pad_row[:, :, 0], padf[:, :]).then_inc(pad_ready, 1)
            done(V.tensor_copy(counts[:, :], z[2][0:E0, RK:RK + 1]))
            done(V.tensor_scalar(ind[:, 0:2 * TILES], tile_row[:, :], counts[:, 0:1], None, ALU.is_lt))
            done(V.tensor_reduce(tiles_of[:, :], ind[:, 0:2 * TILES], AX.X, ALU.add))
            V.tensor_scalar(spread_tiles[:, :], upper[0:E0, 0:E0], tiles_of[:, 0:1], None, ALU.mult)\
                .then_inc(lists_ready, 1)
            done(V.tensor_scalar(pair[:, :], expert[:, :], 1, None, ALU.logical_shift_right))
            done(V.tensor_copy(pairf[:, :], pair[:, :]))
            done(V.tensor_copy(place0[:, :], expert[:, :]))
            done(V.tensor_scalar(place0[:, :], place0[:, :], float(CAP // P), None, ALU.mult))
            dve.wait_ge(lists_ps, 2)
            done(V.tensor_copy(first_tile[:, :], z[2][0:E0, RK + 2 * E0:RK + 2 * E0 + 1]))
            done(V.tensor_tensor(end_tile[:, :], first_tile[:, :], tiles_of[:, :], ALU.add))
            done(V.tensor_tensor(jump[:, :], place0[:, :], first_tile[:, :], ALU.subtract))
            done(V.tensor_scalar(ind[:, :], tile_no[:, :], first_tile[:, 0:1], None, ALU.is_ge))
            done(V.tensor_scalar(ind2[:, :], tile_no[:, :], end_tile[:, 0:1], None, ALU.is_ge))
            done(V.tensor_tensor(ind[:, :], ind[:, :], ind2[:, :], ALU.subtract))
            V.tensor_tensor(indj[:, :], tile_no[:, :], ind[:, :], ALU.mult).then_inc(lists_ready, 1)
            done(V.tensor_copy(first_row[:, :], z[2][:, RK + 3 * E0:RK + 4 * E0]))
            dve.wait_ge(lists_ps, 3)
            V.tensor_copy(tab_pair[:, :, 0], z[0][0:1, 0:LISTED]).then_inc(tab_ready, 1)
            V.tensor_copy(tab_row[:, :, 0], z[0][0:1, P:P + LISTED]).then_inc(tab_ready, 1)
            n2 = 2 * TILES
            v = match[:, :, :]
            done(V.tensor_tensor(v, chosen[:, :, :].rearrange("p t k -> p (t k)").unsqueeze(2).to_broadcast([P, n2, E0]),
                                 iota[:, 0:E0].unsqueeze(1).to_broadcast([P, n2, E0]), ALU.is_equal))
            done(V.tensor_tensor(v, v, first_row[:, :].unsqueeze(1).to_broadcast([P, n2, E0]), ALU.mult))
            done(V.tensor_reduce(place1f[:, :], v, AX.X, ALU.add))
            done(V.tensor_scalar(place1f[:, :], place1f[:, :], float(P), None, ALU.mult))
            done(V.tensor_tensor(place1f[:, :], place1f[:, :], rank[:, :, :].rearrange("p t k -> p (t k)"), ALU.add))
            V.tensor_copy(place1[:, :, :].rearrange("p t k -> p (t k)"), place1f[:, :]).then_inc(place1_ready, 1)
            dve.wait_ge(mixT_ready, 1)
            dve.wait_ge(attb_in, 32)
            dve.wait_ge(mbT_ready, 2)
            for m in (mixh, mixl):
                V.memset(m[:, :].bitcast(U32), 0).then_inc(mix_zero, 1)
            dve.wait_ge(mix_zero, 2)

            def ht_low(j, v):
                dve.wait_ge(hh_ready, j + 1)
                V.tensor_tensor(hl[v % 2][:, :], tp[v % 2][:, 0:P], hh[v % 2][:, :], ALU.subtract).then_inc(hl_ready, 1)

            def outputs(i, v, first=False, last=False):
                j = 4 * i + v
                if not last:
                    ht_low(j + 1, v + 1)
                dve.wait_ge(zt_ps, j + 1)
                if not first:
                    dve.wait_ge(zs_out[v], 16 * i)
                V.tensor_copy(zt[v][:, HALF:L], (z[1], cp[1])[v % 2][:, :]).then_inc(zt_dve, 1)

            dve.wait_ge(place1_ready, 1)
            ht_low(0, 0)
            for v in range(4):
                outputs(0, v, first=True)
            with dve.Fori(1, LISTED // 4 - 1) as i:
                for v in range(4):
                    outputs(i, v)
            for v in range(4):
                outputs(LISTED // 4 - 1, v, last=v == 3)
            mix(0)
            dve.wait_ge(ga_in[0], 32)
            V.tensor_tensor(ga[0][:, 0, :], ga[0][:, 0, :], ga[0][:, 1, :], ALU.add).then_inc(ga_sum, 1)
            dve.wait_ge(ga_sum, 1)
            dve.wait_ge(xr_in[0], 16)
            dve.wait_ge(xd_ready, TILES)
            dve.wait_ge(xb_ready, TILES)
            V.tensor_tensor(xin[0][:, :], ga[0][:, 0, :], xr[0][:, :], ALU.add).then_inc(x1_ready, 1)
            x1_low(0, 0)
            y_low(a1, 0, 0)

            def step1(i, u, first=False, last=False):
                t = 2 * i + u
                if not last:
                    dve.wait_ge(a1.c_out[1], t + 1)
                    mix(t + 1)
                spread1(t)
                if not last:
                    x1_low(1 - u, t + 1)
                dve.wait_ge(a1.hT_hi, t + 1)
                V.tensor_tensor(h1l[:, :, :], prepp[0:K1, 0:2 * P].rearrange("p (k r) -> p k r", r=P),
                                h1h[:, :, :], ALU.subtract).then_inc(a1.hT_lo, 1)
                if not last:
                    y_low(a1, t + 1, 0)
                dve.wait_ge(x1_stored[u], 16 * (TILES // 2))
                if not first:
                    dve.wait_ge(out_stored[u], 16 * i)
                for b in range(2):
                    dve.wait_ge(a1.z_ps[b], t + 1)
                    w = base_columns(b, B1)
                    V.tensor_tensor(xb[u][:, w], z[b][:, 0:w.stop - w.start], xin[u][:, w], ALU.add)\
                        .then_inc(a1.z_out[b], 1)

            step1(0, 0, first=True)
            step1(0, 1, first=True)
            with dve.Fori(1, TILES // 2 - 1) as i:
                step1(i, 0)
                step1(i, 1)
            step1(TILES // 2 - 1, 0)
            step1(TILES // 2 - 1, 1, last=True)

        @block.tensor
        def _(pe):
            T = nc.tensor

            def three(o, ah, al, wh, wl, start, stop, **kw):
                T.matmul(o, ah, wh, start=start, stop=False, **kw)
                T.matmul(o, al, wh, start=False, stop=False, **kw)
                return T.matmul(o, ah, wl, start=False, stop=stop, **kw)

            def over_y(b, y, wh, wl, stop=False):
                for k in range(KC):
                    mm = three(z[b][:, 0:wh[b].shape[2]], yh[y][:, k, :], yl[y][:, k, :], wh[b][:, k, :], wl[b][:, k, :],
                               k == 0, stop and k == KC - 1, skip_group_check=True)
                return mm

            def over_h(s, b, width, hh, hl, wh, wl):
                w = base_columns(b, width)
                for k in range(hh.shape[1]):
                    mm = three(z[b][:, 0:w.stop - w.start], hh[:, k, :], hl[:, k, :], wh[:, k, w], wl[:, k, w],
                               False, k == hh.shape[1] - 1, skip_group_check=True)
                mm.then_inc(s.z_ps[b], 1)

            def conv(t):
                pe.wait_ge(x8_hi, t + 1)
                pe.wait_ge(x8_lo, t + 1)
                for b in range(2):
                    for g in (2 * b, 2 * b + 1):
                        o = cp[b][:, 2 * NB * (g % 2):2 * NB * (g % 2 + 1)].rearrange("p (s m) -> p s m", s=2)
                        for w in range(2):
                            ah, al = (a[:, w, g, :, :].rearrange("p j c -> p (j c)") for a in (th, tl))
                            vh, vl = (a[:, g:g + GROUPS + 1:GROUPS, w:w + NB] for a in (x8h, x8l))
                            mm = three(o, ah, al, vh, vl, w == 0, w == 1)
                    mm.then_inc(a0.c_ps[b], 1)

            def turn_conv(t):
                for b in range(2):
                    pe.wait_ge(a0.c_out[b], t + 1)
                for n in range(2):
                    for g in range(GROUPS):
                        mm = T.transpose(tp[n][:, P * g:P * (g + 1)], mid[:, NB * (2 * g + n):NB * (2 * g + n + 1)],
                                         ident[:, :])
                    mm.then_inc(a0.y_ps[n], 1)

            pe.wait_ge(id_ready, 1)
            pe.wait_ge(conv_in, 16)
            cv = convnat[:, :].rearrange("o (c k) -> o k c", k=TAPS)
            for k in range(TAPS):
                o = z[k // 8][0:CI, C * (k % 8):C * (k % 8) + C]
                mm = T.transpose(o, cv[:, k, :], ident[0:C, 0:C])
            mm.then_inc(taps_ps, 1)
            wv = w0nat[:, :, :].rearrange("p n (b j) -> p n j b", j=BLK)
            av = arnat[:, :].rearrange("a (b j) -> a j b", j=BLK)

            def turn_w0(first, end):
                for q in range(first, end):
                    b, k = divmod(q, KC)
                    if q >= 4:
                        pe.wait_ge(prep_lo, q - 3)
                    w = base_columns(b, B0)
                    for n in range(w.start // P, w.stop // P):
                        if k == 0:
                            pe.wait_ge(w0_in[n], 16)
                        c0 = P * n - w.start
                        mm = T.transpose(pbank(q)[:, c0:c0 + P], wv[:, n, BLK - 1 - k, :], ident[:, :])
                    if b == 2:
                        if k == 0:
                            pe.wait_ge(ar_in, 32)
                        mm = T.transpose(pbank(q)[:, SM0:SM0 + AR], av[:, BLK - 1 - k, :], ident[0:AR, 0:AR])
                    mm.then_inc(prep_ps, 1)

            turn_w0(0, 8)
            pe.wait_ge(c_in, 16)
            T.transpose(prepp[:, 0:NS], cnat[:, :], ident[0:NS, 0:NS]).then_inc(condT_ps, 1)
            pe.wait_ge(ctxw_in, 16)
            T.transpose(prepp[:, NS:NS + C], ctxnat[:, :], ident[0:C, 0:C]).then_inc(condT_ps, 1)
            turn_w0(8, 12)
            pe.wait_ge(condT_sb, 1)
            pe.wait_ge(rep_ready, 2)
            pe.wait_ge(ones_ready, 2)
            pe.wait_ge(upper_ready, 3)
            for g in range(GROUPS):
                o = z[2][:, NS * g:NS * (g + 1)]
                T.matmul(o, ctxrep[:, g, :, :].rearrange("p j c -> p (j c)"), condT[:, :], start=True, stop=False)
                mm = T.matmul(o, siderep[:, g, :, :].rearrange("p j c -> p (j c)"), ones[:, :], start=False, stop=True)
            mm.then_inc(ctx_ps, 1)
            turn_w0(12, 16)
            pe.wait_ge(taps_sb, 2)
            pe.wait_ge(mlp_in, 16 * 8)
            T.matmul(z[0][:, 0:NS], cw[0][:, :], condT[:, :], start=True, stop=True).then_inc(hid_ps, 1)
            turn_w0(16, 18)
            pe.wait_ge(hid_ready, 1)
            T.matmul(z[0][:, NS:2 * NS], cw[1][:, :], hid[0][:, :], start=True, stop=True).then_inc(hid_ps, 1)
            pe.wait_ge(mixw_in, 32)
            for j in range(4):
                mm = T.transpose(z[1][:, P * j:P * (j + 1)], mixnat[:, j, :, :].rearrange("p s i -> p (s i)"),
                                 ident[:, :])
            mm.then_inc(mixT_ps, 1)
            turn_w0(18, 20)
            pe.wait_ge(hid_ready, 2)
            T.matmul(prepp[0:NS, 256:256 + MIX], hid[1][:, :], w2[:, :], start=True, stop=True).then_inc(att_ps, 1)
            turn_w0(20, PREP_A)
            pe.wait_ge(tl_ready, 2)
            pe.wait_ge(prep_lo, PREP_A)
            conv(0)
            turn_conv(0)

            def turn_b(first, end):
                for q in range(PREP_A + 2 * first, PREP_A + 2 * end):
                    k, hj = divmod(q - PREP_A, 2)
                    if q >= PREP_A + 2:
                        pe.wait_ge(prep_lo, q - 3)
                    if hj == 0:
                        pe.wait_ge(b_in[k % 4], 16 * (k // 4 + 1))
                    for j in range(4 * hj, 4 * hj + 4):
                        mm = T.transpose(pbank(q)[:, P * (j % 4):P * (j % 4) + P], bnat[k % 4][:, j, :, :].rearrange("p e r -> p (e r)"),
                                         ident[:, :])
                    mm.then_inc(prep_ps, 1)

            turn_b(0, 1)

            def w1_pieces(u):
                for k in range(4):
                    T.transpose(prepp[:, 64 * k:64 * (k + 1)], w1nat[:, P * k:P * (k + 1)], ident[0:64, 0:64])
                if u == 0:
                    for k in range(2):
                        e = E1 // 2
                        mm = T.transpose(prepp[0:K1, 256 + 64 * k:320 + 64 * k],
                                         lbnat[:, e * k:e * (k + 1), :].rearrange("p e r -> p (e r)"),
                                         ident[0:64, 0:64])
                else:
                    T.transpose(prepp[0:64, 256:256 + E1], gnat[:, 0:64], ident[0:E1, 0:E1])
                    for k in range(2):
                        c0 = 256 + E1 + K1 * k
                        mm = T.transpose(prepp[0:64, c0:c0 + K1], lanat[:, k, :], ident[0:K1, 0:K1])
                mm.then_inc(w1_ps, 1)

            def mixing(t):
                pe.wait_ge(x1_hi, t + 1)
                pe.wait_ge(x1_lo, t + 1)
                pe.wait_ge(mix_lo, 2 * t + 2)
                for b in range(2):
                    w = slice(HALF * b, HALF * (b + 1))
                    three(cp[b][:, :], mixh[:, :], mixl[:, :], x1h[:, w], x1l[:, w], True, True)\
                        .then_inc(a1.c_ps[b], 1)

            def turn_mixed(t):
                for b in range(2):
                    pe.wait_ge(a1.c_out[b], t + 1)
                    for k in range(4):
                        mm = T.transpose(tp[b][:, P * k:P * (k + 1)], mid1[:, P * (4 * b + k):P * (4 * b + k + 1)],
                                         ident[:, :])
                    mm.then_inc(a1.y_ps[b], 1)

            def step0(t, u, first=False):
                for b in range(2):
                    pe.wait_ge(a0.y_hi[b], t + 1)
                    pe.wait_ge(a0.y_lo[b], t + 1)
                if first:
                    pe.wait_ge(cbT_ready, 1)
                    pe.wait_ge(mixT_ready, 1)
                else:
                    pe.wait_ge(a0.z_out[2], t)
                    pe.wait_ge(place_ready, 2 * t)
                over_y(2, u, w0h, w0l, stop=True).then_inc(base_done[2], 1)
                if first:
                    pe.wait_ge(att_ready, 1)
                    T.transpose(prepp[0:MIX, 320:320 + NS], att[:, :], ident[0:NS, 0:NS]).then_inc(attT_ps, 1)
                    turn_b(1, 4)
                    pe.wait_ge(attT_sb, 1)
                    T.matmul(prepp[:, 384:384 + NS], mixbias[:, :, :].rearrange("p s c -> p (s c)"), attT[:, :],
                             start=True, stop=True).then_inc(mb_ps, 1)
                    pe.wait_ge(mbT_ready, 2)
                pe.wait_ge(w1_in, 48 * t + 48)
                if not first:
                    pe.wait_ge(w1_lo, t)
                    pe.wait_ge(a0.z_out[0], t)
                over_y(0, u, w0h, w0l, stop=True).then_inc(base_done[0], 1)
                if first:
                    turn_b(4, 8)
                    pe.wait_ge(prep_lo, PREP - 2)
                    conv(1)
                w1_pieces(u)
                if exists(t + 1):
                    turn_conv(t + 1)
                if not first:
                    pe.wait_ge(a0.z_out[1], t)
                over_y(1, u, w0h, w0l, stop=True).then_inc(base_done[1], 1)
                pe.wait_ge(listed_ready, t + 1)
                pe.wait_ge(a0.z_out[2], t + 1)
                o = z[2][:, RK:RK + 2 * E0]
                T.matmul(o, upper[:, :], onehot[:, :, :].rearrange("p k e -> p (k e)"), start=True, stop=False)
                T.matmul(o, every_row, before[:, :, :].rearrange("p k e -> p (k e)"), start=False, stop=True)\
                    .then_inc(rank_ps, 1)
                if exists(t + 2):
                    conv(t + 2)

            every_row = ones_col[:, 0:1].to_broadcast([P, P])
            step0(0, 0, first=True)
            step0(1, 1)
            with pe.Fori(1, TILES // 2 - 2) as i:
                step0(2 * i, 0)
                step0(2 * i + 1, 1)
            for t in range(TILES - 4, TILES):
                step0(t, t % 2)

            pe.wait_ge(place_ready, 2 * TILES)
            T.matmul(z[2][0:E0, RK:RK + 1], before[:, 0, :], ones_col[:, :], start=True, stop=True)
            T.matmul(z[2][0:1, RK + E0:RK + 2 * E0], ones_col[:, :], before[:, 0, :], start=True, stop=True)\
                .then_inc(lists_ps, 1)
            pe.wait_ge(lists_ready, 1)
            T.matmul(z[2][0:E0, RK + 2 * E0:RK + 2 * E0 + 1], upper[0:E0, 0:E0], tiles_of[:, :], start=True, stop=True)
            T.matmul(z[2][:, RK + 3 * E0:RK + 4 * E0], ones_col[0:E0, 0:1].to_broadcast([E0, P]), spread_tiles[:, :],
                     start=True, stop=True).then_inc(lists_ps, 1)
            pe.wait_ge(lists_ready, 2)
            pe.wait_ge(a0.z_out[0], TILES)
            T.matmul(z[0][0:1, 0:LISTED], pairf[:, :], ind[:, :], start=True, stop=True)
            T.matmul(z[0][0:1, P:P + LISTED], jump[:, :], ind[:, :], start=True, stop=False)
            T.matmul(z[0][0:1, P:P + LISTED], ones_col[0:E0, :], indj[:, :], start=False, stop=True).then_inc(lists_ps, 1)

            def turn_ht(i, v, first=False):
                j = 4 * i + v
                pe.wait_ge(ht_in[v], 16 * i + 16)
                if not first:
                    pe.wait_ge(hl_ready, j - 1)
                T.transpose(tp[v % 2][:, 0:P], ht[v][:, :], ident[:, :]).then_inc(ht_ps, 1)

            def listed_products(i, v, first=False, last=False):
                j = 4 * i + v
                if not last:
                    if v == 3:
                        turn_ht(i + 1, 0)
                    else:
                        turn_ht(i, v + 1, first=first and v == 0)
                pe.wait_ge(hl_ready, j + 1)
                if not (first and v < 2):
                    pe.wait_ge(zt_act, j - 1)
                    pe.wait_ge(zt_dve, j - 1)
                k = pe.value_load(tab_pair[0:1, j, :], min_val=0, max_val=KC - 1)
                for half in range(2):
                    w = slice(HALF * half, HALF * (half + 1))
                    mm = three((z, cp)[v % 2][half][:, :], hh[v % 2][:, :], hl[v % 2][:, :], bh[:, k, w], bl[:, k, w],
                               True, True)
                mm.then_inc(zt_ps, 1)

            pe.wait_ge(tab_ready, 2)
            pe.wait_ge(place1_ready, 1)
            turn_ht(0, 0, first=True)
            for v in range(4):
                listed_products(0, v, first=True)
            with pe.Fori(1, LISTED // 4 - 1) as i:
                for v in range(4):
                    listed_products(i, v)
            for v in range(4):
                listed_products(LISTED // 4 - 1, v, last=v == 3)
            pe.wait_ge(zt_act, LISTED)
            pe.wait_ge(zt_dve, LISTED)
            mixing(0)
            turn_mixed(0)

            def step1(t, first=False, last=False):
                for b in range(2):
                    pe.wait_ge(a1.y_hi[b], t + 1)
                    pe.wait_ge(a1.y_lo[b], t + 1)
                if first:
                    pe.wait_ge(a0.z_out[2], TILES)
                    pe.wait_ge(w1_back[2], 32)
                over_y(2, 0, w1h, w1l, stop=True).then_inc(small_done, 1)
                if first:
                    pe.wait_ge(a0.z_out[0], TILES)
                    pe.wait_ge(w1_back[0], 32)
                else:
                    pe.wait_ge(a1.z_out[0], t)
                over_y(0, 0, w1h, w1l)
                if not last:
                    mixing(t + 1)
                pe.wait_ge(a1.hx, 2 * t + 2)
                for k in range(2):
                    mm = T.transpose(prepp[0:K1, P * k:P * (k + 1)], hx1[:, K1 * k:K1 * (k + 1)], ident[:, :])
                mm.then_inc(a1.hT_ps, 1)
                if first:
                    pe.wait_ge(a0.z_out[1], TILES)
                    pe.wait_ge(w1_back[1], 32)
                else:
                    pe.wait_ge(a1.z_out[1], t)
                over_y(1, 0, w1h, w1l)
                if not last:
                    turn_mixed(t + 1)
                if first:
                    pe.wait_ge(lb_in, 32)
                pe.wait_ge(a1.hT_lo, t + 1)
                for b in range(2):
                    over_h(a1, b, B1, h1h, h1l, lbh, lbl)

            step1(0, first=True)
            with pe.Fori(1, TILES - 1) as t:
                step1(t)
            step1(TILES - 1, last=True)


_INS = ['x', 'cond_128', 'fside_S_0', 'L0_cond_weight', 'L0_cond_c_weight', 'L0_ffn_base_w', 'L0_ffn_base_b',
        'L0_ffn_A', 'L0_ffn_B', 'L0_ffn_router_w', 'L1_cond_W0', 'L1_cond_b0', 'L1_cond_W1', 'L1_cond_b1',
        'L1_cond_W2', 'L1_cond_b2', 'L1_cond_weight', 'L1_cond_bias_k', 'L1_ffn_base_W', 'L1_ffn_gate_W',
        'L1_ffn_lora_A', 'L1_ffn_lora_B']


def kernel(**inputs):
    import numpy as _np
    import concourse.bacc as _bacc
    from concourse import mybir as _mybir
    from concourse.bass_utils import run_bass_kernel_spmd as _run

    nc = _bacc.Bacc("TRN2", target_bir_lowering=False, num_devices=1)
    arrays, args = {}, []
    for name in _INS:
        a = _np.ascontiguousarray(inputs[name])
        arrays[f"in_{name}_dram"] = a
        args.append(nc.dram_tensor(f"in_{name}_dram", a.shape, _mybir.dt.from_np(a.dtype), kind="ExternalInput").ap())
    args.append(nc.dram_tensor("out_0_dram", (NS, C, L), F32, kind="ExternalOutput").ap())
    build(nc, *args)
    r = _run(nc, [arrays], core_ids=[0])
    return r.results[0]["out_0_dram"]
```
